# Optimizing a Trainium2 kernel written in Bass

```python
import numpy as np
import jax
import jax.numpy as jnp

def _softmax(x, axis=-1):
    return jax.nn.softmax(x, axis=axis)

def _gelu(x):
    return jax.nn.gelu(x, approximate=True)

def _silu(x):
    return jax.nn.silu(x)

def _sigmoid(x):
    return jax.nn.sigmoid(x)

def _layernorm(x, axis=-1, eps=1e-05):
    m = jnp.mean(x, axis=axis, keepdims=True)
    v = jnp.var(x, axis=axis, keepdims=True)
    return (x - m) / jnp.sqrt(v + eps)

def _scatter_add(tgt, idx, src, axis=0):
    return tgt.at[idx].add(src)

def _segment_sum(src, seg, n):
    return jax.ops.segment_sum(src, seg, n)
kernel_name = 'mk_vit_tower_cls_d2_tok_img768_r4_7e6ee8'

def setup_inputs(seed: int=0):
    np.random.seed(seed)
    _w = jnp.asarray

    def _rec_inputs():
        import jax
        import jax.numpy as jnp
        _rk = jax.random.key(seed)
        x = -0.000356955 + 1 * jax.random.normal(jax.random.fold_in(_rk, 1), (64, 3, 224, 224), jnp.float32)
        cls_tok = 0.02 * jax.random.normal(jax.random.fold_in(_rk, 5), (1, 1, 192), jnp.float32)
        return (x, cls_tok)
    x, cls_tok = _rec_inputs()

    def _L0_tok_setup():
        import jax, jax.numpy as jnp
        import numpy as np
        N_PATCHES = 14
        HIDDEN_D = 192
        LN_EPS = 1e-05

        def positional_embeddings(seq_len, d):
            i = jnp.arange(seq_len, dtype=jnp.float32)[:, None]
            j = jnp.arange(d, dtype=jnp.float32)[None, :]
            exponent = jnp.floor(j / 2.0) * 2.0 / d
            angle = i / jnp.power(10000.0, exponent)
            return jnp.where(jnp.arange(d)[None, :] % 2 == 0, jnp.sin(angle), jnp.cos(angle))

        def patchify(images, n_patches):
            B, C, H, W = images.shape
            ph, pw = (H // n_patches, W // n_patches)
            x = images.reshape(B, C, n_patches, ph, n_patches, pw)
            x = x.transpose(0, 2, 4, 1, 3, 5)
            return x.reshape(B, n_patches * n_patches, C * ph * pw)
        key = jax.random.key(seed)
        k_img, k_w, k_b, k_cls = jax.random.split(key, 4)
        B, C, H, W = (128, 3, 224, 224)
        lin_in = H // N_PATCHES * (W // N_PATCHES) * C
        bound = 1.0 / np.sqrt(lin_in)
        return {'images': jax.random.normal(k_img, (B, C, H, W), dtype=jnp.float32), 'W': jax.random.uniform(k_w, (HIDDEN_D, lin_in), jnp.float32, -bound, bound), 'b': jax.random.uniform(k_b, (HIDDEN_D,), jnp.float32, -bound, bound), 'class_token': jax.random.uniform(k_cls, (1, HIDDEN_D), jnp.float32), 'gamma': jnp.ones((HIDDEN_D,), jnp.float32), 'beta': jnp.zeros((HIDDEN_D,), jnp.float32)}
    _L0_tok_all = _L0_tok_setup()
    _L0_tok_in = {k: v for k, v in _L0_tok_all.items() if k in ('W', 'b', 'class_token', 'gamma', 'beta')}
    del _L0_tok_all

    def _L0_attn_setup():
        import jax, jax.numpy as jnp
        import numpy as np
        BATCH, SEQ, D_MODEL, D_STATE, K = (2, 512, 192, 16, 4)

        def _block(x, in_proj_w, conv_w, conv_b, dt_w, dt_b, B_w, C_w, A_log, D_param, out_w, ln_g, ln_b):
            B, L, D = x.shape
            residual = x
            xz = x @ in_proj_w.T
            x_branch, z = jnp.split(xz, 2, axis=-1)
            xc = jnp.transpose(x_branch, (0, 2, 1))
            xc = jax.lax.conv_general_dilated(xc, conv_w, (1,), [(3, 3)], feature_group_count=D, dimension_numbers=('NCH', 'OIH', 'NCH'))
            xc = xc[:, :, :L] + conv_b[None, :, None]
            u = jnp.transpose(jax.nn.silu(xc), (0, 2, 1))
            dt = jax.nn.softplus(u @ dt_w.T + dt_b)
            Bv = u @ B_w.T
            Cv = u @ C_w.T
            A = -jnp.exp(A_log)
            dA = jnp.exp(dt[..., None] * A)
            dBu = dt[..., None] * Bv[:, :, None, :] * u[..., None]

            def step(h, ins):
                dA_t, dBu_t, C_t = ins
                h = dA_t * h + dBu_t
                return (h, jnp.einsum('bdn,bn->bd', h, C_t))
            h0 = jnp.zeros((B, D, A.shape[1]), u.dtype)
            _, ys = jax.lax.scan(step, h0, (jnp.transpose(dA, (1, 0, 2, 3)), jnp.transpose(dBu, (1, 0, 2, 3)), jnp.transpose(Cv, (1, 0, 2))))
            y = jnp.transpose(ys, (1, 0, 2))
            y = y + D_param * u
            y = y * jax.nn.silu(z)
            y = y @ out_w.T
            r = y + residual
            mu = jnp.mean(r, axis=-1, keepdims=True)
            var = jnp.var(r, axis=-1, keepdims=True)
            return (r - mu) / jnp.sqrt(var + 1e-05) * ln_g + ln_b
        key = jax.random.key(seed)
        ks = jax.random.split(key, 8)
        s = 0.02
        x = jax.random.normal(ks[0], (BATCH, SEQ, D_MODEL), jnp.float32)
        in_proj_w = jax.random.normal(ks[1], (2 * D_MODEL, D_MODEL), jnp.float32) * s
        conv_w = jax.random.normal(ks[2], (D_MODEL, 1, K), jnp.float32) * 0.25
        conv_b = jnp.zeros((D_MODEL,), jnp.float32)
        dt_w = jax.random.normal(ks[3], (D_MODEL, D_MODEL), jnp.float32) * s
        dt_b = jnp.full((D_MODEL,), -4.0, jnp.float32)
        B_w = jax.random.normal(ks[4], (D_STATE, D_MODEL), jnp.float32) * s
        C_w = jax.random.normal(ks[5], (D_STATE, D_MODEL), jnp.float32) * s
        A_log = jnp.broadcast_to(jnp.log(jnp.arange(1, D_STATE + 1, dtype=jnp.float32)), (D_MODEL, D_STATE)) + 0.0
        D_param = jnp.ones((D_MODEL,), jnp.float32)
        out_w = jax.random.normal(ks[6], (D_MODEL, D_MODEL), jnp.float32) * s
        ln_g = jnp.ones((D_MODEL,), jnp.float32)
        ln_b = jnp.zeros((D_MODEL,), jnp.float32)
        return {'x': x, 'in_proj_w': in_proj_w, 'conv_w': conv_w, 'conv_b': conv_b, 'dt_w': dt_w, 'dt_b': dt_b, 'B_w': B_w, 'C_w': C_w, 'A_log': A_log, 'D_param': D_param, 'out_w': out_w, 'ln_g': ln_g, 'ln_b': ln_b}
    _L0_attn_all = _L0_attn_setup()
    _L0_attn_in = {k: v for k, v in _L0_attn_all.items() if k in ('in_proj_w', 'conv_w', 'conv_b', 'dt_w', 'dt_b', 'B_w', 'C_w', 'A_log', 'D_param', 'out_w', 'ln_g', 'ln_b')}
    del _L0_attn_all

    def _L0_ffn_setup():
        import jax, jax.numpy as jnp
        import numpy as np
        B, T, E = (2, 256, 192)
        H = 768
        N_EXP = 4
        key = jax.random.key(seed)
        ks = jax.random.split(key, 8)
        s_e = 1.0 / np.sqrt(E)
        s_h = 1.0 / np.sqrt(H)
        return {'x': jax.random.normal(ks[0], (B, T, E), dtype=jnp.float32), 'Wg': jax.random.uniform(ks[1], (E, N_EXP), minval=-s_e, maxval=s_e, dtype=jnp.float32), 'bg': jax.random.uniform(ks[2], (N_EXP,), minval=-s_e, maxval=s_e, dtype=jnp.float32), 'W1': jax.random.uniform(ks[3], (N_EXP, E, H), minval=-s_e, maxval=s_e, dtype=jnp.float32), 'b1': jax.random.uniform(ks[4], (N_EXP, H), minval=-s_e, maxval=s_e, dtype=jnp.float32), 'W2': jax.random.uniform(ks[5], (N_EXP, H, E), minval=-s_h, maxval=s_h, dtype=jnp.float32), 'b2': jax.random.uniform(ks[6], (N_EXP, E), minval=-s_h, maxval=s_h, dtype=jnp.float32)}
    _L0_ffn_all = _L0_ffn_setup()
    _L0_ffn_in = {k: v for k, v in _L0_ffn_all.items() if k in ('Wg', 'bg', 'W1', 'b1', 'W2', 'b2')}
    del _L0_ffn_all

    def _L1_attn_setup():
        import jax, jax.numpy as jnp
        import numpy as np

        def _selective_scan(dt, Bm, Cm, xp, A):
            Bsz, L, d_inner = xp.shape
            N = A.shape[1]

            def step(h, inp):
                dt_t, B_t, C_t, x_t = inp
                dA = jnp.exp(dt_t[..., None] * A)
                dBx = (dt_t * x_t)[..., None] * B_t[:, None, :]
                h = dA * h + dBx
                y = jnp.einsum('bdn,bn->bd', h, C_t)
                return (h, y)
            h0 = jnp.zeros((Bsz, d_inner, N), dtype=xp.dtype)
            inputs = (jnp.moveaxis(dt, 1, 0), jnp.moveaxis(Bm, 1, 0), jnp.moveaxis(Cm, 1, 0), jnp.moveaxis(xp, 1, 0))
            _, ys = jax.lax.scan(step, h0, inputs)
            return jnp.moveaxis(ys, 0, 1)
        key = jax.random.key(seed)
        ks = jax.random.split(key, 9)
        B, L, D = (2, 512, 192)
        d_inner, N, R = (384, 16, 48)
        s = 0.02
        x = jax.random.normal(ks[0], (B, L, D), dtype=jnp.float32)
        W_in = jax.random.normal(ks[1], (D, 2 * d_inner), dtype=jnp.float32) * s
        W_x = jax.random.normal(ks[2], (d_inner, R + 2 * N), dtype=jnp.float32) * s
        W_dt = jax.random.normal(ks[3], (R, d_inner), dtype=jnp.float32) * s
        b_dt = jax.random.normal(ks[4], (d_inner,), dtype=jnp.float32) * s
        A_log = jnp.log(jnp.broadcast_to(jnp.arange(1, N + 1, dtype=jnp.float32), (d_inner, N)))
        D_skip = jnp.ones((d_inner,), dtype=jnp.float32)
        W_out = jax.random.normal(ks[5], (d_inner, D), dtype=jnp.float32) * s
        gamma = jnp.ones((D,), dtype=jnp.float32)
        beta = jnp.zeros((D,), dtype=jnp.float32)
        return {'x': x, 'W_in': W_in, 'W_x': W_x, 'W_dt': W_dt, 'b_dt': b_dt, 'A_log': A_log, 'D_skip': D_skip, 'W_out': W_out, 'gamma': gamma, 'beta': beta}
    _L1_attn_all = _L1_attn_setup()
    _L1_attn_in = {k: v for k, v in _L1_attn_all.items() if k in ('W_in', 'W_x', 'W_dt', 'b_dt', 'A_log', 'D_skip', 'W_out', 'gamma', 'beta')}
    del _L1_attn_all

    def _L1_ffn_setup():
        import jax, jax.numpy as jnp
        import numpy as np
        DIM = 192
        NUM_EXPERTS = 8
        TOP_K = 2
        MLP_RATIO = 4
        CAPACITY_RATIO = 1.25
        key = jax.random.key(seed)
        ks = jax.random.split(key, 6)
        B, N, C = (16, 256, DIM)
        H = MLP_RATIO * C
        s_in = 1.0 / np.sqrt(C)
        s_h = 1.0 / np.sqrt(H)
        return {'x': jax.random.normal(ks[0], (B, N, C), dtype=jnp.float32), 'Wg': jax.random.normal(ks[1], (C, NUM_EXPERTS), dtype=jnp.float32) * s_in, 'W1': jax.random.normal(ks[2], (NUM_EXPERTS, C, H), dtype=jnp.float32) * s_in, 'b1': jnp.zeros((NUM_EXPERTS, H), dtype=jnp.float32), 'W2': jax.random.normal(ks[3], (NUM_EXPERTS, H, C), dtype=jnp.float32) * s_h, 'b2': jnp.zeros((NUM_EXPERTS, C), dtype=jnp.float32)}
    _L1_ffn_all = _L1_ffn_setup()
    _L1_ffn_in = {k: v for k, v in _L1_ffn_all.items() if k in ('Wg', 'W1', 'b1', 'W2', 'b2')}
    del _L1_ffn_all
    return {'x': x, 'cls_tok': cls_tok, 'L0_tok_W': _L0_tok_in['W'], 'L0_tok_b': _L0_tok_in['b'], 'L0_tok_class_token': _L0_tok_in['class_token'], 'L0_tok_gamma': _L0_tok_in['gamma'], 'L0_tok_beta': _L0_tok_in['beta'], 'L0_attn_in_proj_w': _L0_attn_in['in_proj_w'], 'L0_attn_conv_w': _L0_attn_in['conv_w'], 'L0_attn_conv_b': _L0_attn_in['conv_b'], 'L0_attn_dt_w': _L0_attn_in['dt_w'], 'L0_attn_dt_b': _L0_attn_in['dt_b'], 'L0_attn_B_w': _L0_attn_in['B_w'], 'L0_attn_C_w': _L0_attn_in['C_w'], 'L0_attn_A_log': _L0_attn_in['A_log'], 'L0_attn_D_param': _L0_attn_in['D_param'], 'L0_attn_out_w': _L0_attn_in['out_w'], 'L0_attn_ln_g': _L0_attn_in['ln_g'], 'L0_attn_ln_b': _L0_attn_in['ln_b'], 'L0_ffn_Wg': _L0_ffn_in['Wg'], 'L0_ffn_bg': _L0_ffn_in['bg'], 'L0_ffn_W1': _L0_ffn_in['W1'], 'L0_ffn_b1': _L0_ffn_in['b1'], 'L0_ffn_W2': _L0_ffn_in['W2'], 'L0_ffn_b2': _L0_ffn_in['b2'], 'L1_attn_W_in': _L1_attn_in['W_in'], 'L1_attn_W_x': _L1_attn_in['W_x'], 'L1_attn_W_dt': _L1_attn_in['W_dt'], 'L1_attn_b_dt': _L1_attn_in['b_dt'], 'L1_attn_A_log': _L1_attn_in['A_log'], 'L1_attn_D_skip': _L1_attn_in['D_skip'], 'L1_attn_W_out': _L1_attn_in['W_out'], 'L1_attn_gamma': _L1_attn_in['gamma'], 'L1_attn_beta': _L1_attn_in['beta'], 'L1_ffn_Wg': _L1_ffn_in['Wg'], 'L1_ffn_W1': _L1_ffn_in['W1'], 'L1_ffn_b1': _L1_ffn_in['b1'], 'L1_ffn_W2': _L1_ffn_in['W2'], 'L1_ffn_b2': _L1_ffn_in['b2']}

def reference(x, cls_tok, L0_tok_W, L0_tok_b, L0_tok_class_token, L0_tok_gamma, L0_tok_beta, L0_attn_in_proj_w, L0_attn_conv_w, L0_attn_conv_b, L0_attn_dt_w, L0_attn_dt_b, L0_attn_B_w, L0_attn_C_w, L0_attn_A_log, L0_attn_D_param, L0_attn_out_w, L0_attn_ln_g, L0_attn_ln_b, L0_ffn_Wg, L0_ffn_bg, L0_ffn_W1, L0_ffn_b1, L0_ffn_W2, L0_ffn_b2, L1_attn_W_in, L1_attn_W_x, L1_attn_W_dt, L1_attn_b_dt, L1_attn_A_log, L1_attn_D_skip, L1_attn_W_out, L1_attn_gamma, L1_attn_beta, L1_ffn_Wg, L1_ffn_W1, L1_ffn_b1, L1_ffn_W2, L1_ffn_b2):
    import jax
    import jax.numpy as jnp

    def _L0_tok_ref(images, W, b, class_token, gamma, beta):
        import jax, jax.numpy as jnp
        import numpy as np
        N_PATCHES = 14
        HIDDEN_D = 192
        LN_EPS = 1e-05

        def positional_embeddings(seq_len, d):
            i = jnp.arange(seq_len, dtype=jnp.float32)[:, None]
            j = jnp.arange(d, dtype=jnp.float32)[None, :]
            exponent = jnp.floor(j / 2.0) * 2.0 / d
            angle = i / jnp.power(10000.0, exponent)
            return jnp.where(jnp.arange(d)[None, :] % 2 == 0, jnp.sin(angle), jnp.cos(angle))

        def patchify(images, n_patches):
            B, C, H, W = images.shape
            ph, pw = (H // n_patches, W // n_patches)
            x = images.reshape(B, C, n_patches, ph, n_patches, pw)
            x = x.transpose(0, 2, 4, 1, 3, 5)
            return x.reshape(B, n_patches * n_patches, C * ph * pw)
        B = images.shape[0]
        patches = patchify(images, N_PATCHES)
        tokens = jnp.einsum('bpi,di->bpd', patches, W) + b
        cls = jnp.broadcast_to(class_token[None, :, :], (B, 1, HIDDEN_D))
        tokens = jnp.concatenate([cls, tokens], axis=1)
        pos = positional_embeddings(N_PATCHES ** 2 + 1, HIDDEN_D)
        out = tokens + pos[None, :, :]
        mean = out.mean(axis=-1, keepdims=True)
        var = out.var(axis=-1, keepdims=True)
        out = (out - mean) / jnp.sqrt(var + LN_EPS)
        return out * gamma + beta

    def _L0_attn_ref(x, in_proj_w, conv_w, conv_b, dt_w, dt_b, B_w, C_w, A_log, D_param, out_w, ln_g, ln_b):
        import jax, jax.numpy as jnp
        import numpy as np
        BATCH, SEQ, D_MODEL, D_STATE, K = (2, 512, 192, 16, 4)

        def _block(x, in_proj_w, conv_w, conv_b, dt_w, dt_b, B_w, C_w, A_log, D_param, out_w, ln_g, ln_b):
            B, L, D = x.shape
            residual = x
            xz = x @ in_proj_w.T
            x_branch, z = jnp.split(xz, 2, axis=-1)
            xc = jnp.transpose(x_branch, (0, 2, 1))
            xc = jax.lax.conv_general_dilated(xc, conv_w, (1,), [(3, 3)], feature_group_count=D, dimension_numbers=('NCH', 'OIH', 'NCH'))
            xc = xc[:, :, :L] + conv_b[None, :, None]
            u = jnp.transpose(jax.nn.silu(xc), (0, 2, 1))
            dt = jax.nn.softplus(u @ dt_w.T + dt_b)
            Bv = u @ B_w.T
            Cv = u @ C_w.T
            A = -jnp.exp(A_log)
            dA = jnp.exp(dt[..., None] * A)
            dBu = dt[..., None] * Bv[:, :, None, :] * u[..., None]

            def step(h, ins):
                dA_t, dBu_t, C_t = ins
                h = dA_t * h + dBu_t
                return (h, jnp.einsum('bdn,bn->bd', h, C_t))
            h0 = jnp.zeros((B, D, A.shape[1]), u.dtype)
            _, ys = jax.lax.scan(step, h0, (jnp.transpose(dA, (1, 0, 2, 3)), jnp.transpose(dBu, (1, 0, 2, 3)), jnp.transpose(Cv, (1, 0, 2))))
            y = jnp.transpose(ys, (1, 0, 2))
            y = y + D_param * u
            y = y * jax.nn.silu(z)
            y = y @ out_w.T
            r = y + residual
            mu = jnp.mean(r, axis=-1, keepdims=True)
            var = jnp.var(r, axis=-1, keepdims=True)
            return (r - mu) / jnp.sqrt(var + 1e-05) * ln_g + ln_b
        return _block(x, in_proj_w, conv_w, conv_b, dt_w, dt_b, B_w, C_w, A_log, D_param, out_w, ln_g, ln_b)

    def _L0_ffn_ref(x, Wg, bg, W1, b1, W2, b2):
        import jax, jax.numpy as jnp
        import numpy as np
        B, T, E = (2, 256, 192)
        H = 768
        N_EXP = 4
        gate_logits = jnp.einsum('bte,en->btn', x, Wg) + bg
        top = jnp.argmax(gate_logits, axis=-1)
        h = jax.nn.gelu(jnp.einsum('bte,neh->nbth', x, W1) + b1[:, None, None, :], approximate=False)
        y = jnp.einsum('nbth,nhe->nbte', h, W2) + b2[:, None, None, :]
        onehot = jax.nn.one_hot(top, N_EXP, dtype=x.dtype)
        out = jnp.einsum('nbte,btn->bte', y, onehot)
        return out

    def _L1_attn_ref(x, W_in, W_x, W_dt, b_dt, A_log, D_skip, W_out, gamma, beta):
        import jax, jax.numpy as jnp
        import numpy as np

        def _selective_scan(dt, Bm, Cm, xp, A):
            Bsz, L, d_inner = xp.shape
            N = A.shape[1]

            def step(h, inp):
                dt_t, B_t, C_t, x_t = inp
                dA = jnp.exp(dt_t[..., None] * A)
                dBx = (dt_t * x_t)[..., None] * B_t[:, None, :]
                h = dA * h + dBx
                y = jnp.einsum('bdn,bn->bd', h, C_t)
                return (h, y)
            h0 = jnp.zeros((Bsz, d_inner, N), dtype=xp.dtype)
            inputs = (jnp.moveaxis(dt, 1, 0), jnp.moveaxis(Bm, 1, 0), jnp.moveaxis(Cm, 1, 0), jnp.moveaxis(xp, 1, 0))
            _, ys = jax.lax.scan(step, h0, inputs)
            return jnp.moveaxis(ys, 0, 1)
        R = W_dt.shape[0]
        N = A_log.shape[1]
        d_inner = A_log.shape[0]
        xz = jnp.einsum('bld,de->ble', x, W_in)
        xp, z = (xz[..., :d_inner], xz[..., d_inner:])
        xp = jax.nn.silu(xp)
        x_dbl = jnp.einsum('bld,dr->blr', xp, W_x)
        dt = jax.nn.softplus(jnp.einsum('blr,rd->bld', x_dbl[..., :R], W_dt) + b_dt)
        Bm = x_dbl[..., R:R + N]
        Cm = x_dbl[..., R + N:]
        A = -jnp.exp(A_log)
        ys = _selective_scan(dt, Bm, Cm, xp, A)
        y = (ys + D_skip * xp) * jax.nn.silu(z)
        mamba_out = jnp.einsum('bld,de->ble', y, W_out)
        h = x + mamba_out
        mu = jnp.mean(h, axis=-1, keepdims=True)
        var = jnp.mean(jnp.square(h - mu), axis=-1, keepdims=True)
        return (h - mu) * jax.lax.rsqrt(var + 1e-05) * gamma + beta

    def _L1_ffn_ref(x, Wg, W1, b1, W2, b2):
        import jax, jax.numpy as jnp
        import numpy as np
        DIM = 192
        NUM_EXPERTS = 8
        TOP_K = 2
        MLP_RATIO = 4
        CAPACITY_RATIO = 1.25
        B, N, C = x.shape
        E = W1.shape[0]
        K = TOP_K
        T = B * N
        cap = int(CAPACITY_RATIO * T * K / E)
        xf = x.reshape(T, C)
        logits = xf @ Wg
        topv, topi = jax.lax.top_k(logits, K)
        w = jax.nn.softmax(topv, axis=-1)
        priority = w[:, 0]
        order = jnp.argsort(-priority)
        e_ids = topi[order].reshape(T * K)
        w_ord = w[order].reshape(T * K)
        tok_rep = jnp.repeat(order, K)
        oh = jax.nn.one_hot(e_ids, E, dtype=jnp.int32)
        pos = (jnp.cumsum(oh, axis=0) * oh).sum(-1) - 1
        keep = pos < cap
        slot = jnp.where(keep, e_ids * cap + pos, E * cap)
        buf = jnp.zeros((E * cap + 1, C), xf.dtype).at[slot].set(xf[tok_rep])
        buf_e = buf[:E * cap].reshape(E, cap, C)
        h = jax.nn.gelu(jnp.einsum('ecd,edh->ech', buf_e, W1) + b1[:, None, :], approximate=False)
        out = jnp.einsum('ech,ehd->ecd', h, W2) + b2[:, None, :]
        out_flat = jnp.concatenate([out.reshape(E * cap, C), jnp.zeros((1, C), xf.dtype)], axis=0)
        y_assign = out_flat[slot] * (w_ord * keep.astype(xf.dtype))[:, None]
        y = jnp.zeros((T, C), xf.dtype).at[tok_rep].add(y_assign)
        return y.reshape(B, N, C)
    h = _L0_tok_ref(x, L0_tok_W, L0_tok_b, L0_tok_class_token, L0_tok_gamma, L0_tok_beta)
    h = jnp.concatenate([jnp.broadcast_to(cls_tok, (h.shape[0], 1, h.shape[2])), h], axis=1)
    h = h + _L0_attn_ref(_layernorm(h, axis=-1), L0_attn_in_proj_w, L0_attn_conv_w, L0_attn_conv_b, L0_attn_dt_w, L0_attn_dt_b, L0_attn_B_w, L0_attn_C_w, L0_attn_A_log, L0_attn_D_param, L0_attn_out_w, L0_attn_ln_g, L0_attn_ln_b)
    h = h + _L0_ffn_ref(_layernorm(h, axis=-1), L0_ffn_Wg, L0_ffn_bg, L0_ffn_W1, L0_ffn_b1, L0_ffn_W2, L0_ffn_b2)
    h = h + _L1_attn_ref(_layernorm(h, axis=-1), L1_attn_W_in, L1_attn_W_x, L1_attn_W_dt, L1_attn_b_dt, L1_attn_A_log, L1_attn_D_skip, L1_attn_W_out, L1_attn_gamma, L1_attn_beta)
    h = h + _L1_ffn_ref(_layernorm(h, axis=-1), L1_ffn_Wg, L1_ffn_W1, L1_ffn_b1, L1_ffn_W2, L1_ffn_b2)
    return h

_drawn_inputs = setup_inputs


def setup_inputs(seed=0):
    import zlib

    import numpy as np

    out = dict(_drawn_inputs(seed))
    spreads = {'L0_tok_gamma': (1.0, 0.2),
     'L0_tok_beta': (0.0, 0.1),
     'L0_attn_conv_b': (0.0, 0.8),
     'L0_attn_dt_b': (-4.0, 0.6),
     'L0_attn_D_param': (1.0, 0.6),
     'L0_attn_ln_g': (1.0, 0.2),
     'L0_attn_ln_b': (0.0, 0.1),
     'L1_attn_D_skip': (1.0, 0.6),
     'L1_attn_gamma': (1.0, 0.2),
     'L1_attn_beta': (0.0, 0.1),
     'L1_ffn_b1': (0.0, 0.574),
     'L1_ffn_b2': (0.0, 0.381)}
    factors = {'L0_attn_in_proj_w': 8.0,
     'L0_attn_conv_w': 8.0,
     'L0_attn_dt_w': 8.0,
     'L0_attn_B_w': 8.0,
     'L0_attn_C_w': 8.0,
     'L0_attn_A_log': 8.0,
     'L0_attn_out_w': 8.0,
     'L0_ffn_b1': 4.004,
     'L0_ffn_b2': 3.426,
     'L1_attn_W_in': 7.048,
     'L1_attn_W_x': 8.0,
     'L1_attn_W_dt': 8.0,
     'L1_attn_b_dt': 8.0,
     'L1_attn_A_log': 8.0,
     'L1_attn_W_out': 7.117}
    for name, (base, spread) in spreads.items():
        noise = np.random.default_rng([zlib.crc32(name.encode()), seed]).standard_normal(out[name].shape)
        drawn = base * np.exp(spread * noise) if base else spread * noise
        out[name] = jnp.asarray(drawn.astype(out[name].dtype))
    for name, factor in factors.items():
        out[name] = (out[name] * factor).astype(out[name].dtype)
    return out
```

```python
from contextlib import ExitStack

import numpy as np

import concourse.bass as bass
from concourse import mybir

F32 = mybir.dt.float32
BF16 = mybir.dt.bfloat16
I32 = mybir.dt.int32
U32 = mybir.dt.uint32
ALU = mybir.AluOpType
ACT = mybir.ActivationFunctionType
AX = mybir.AxisListType

IMAGES = 64
GRID = 14
PATCH_K = 768
SEQ = GRID * GRID + 2
PAIRS = IMAGES // 2
COLS = 2 * SEQ
ROWS = COLS // 4
TILES = PAIRS * 4
TOKENS = IMAGES * SEQ
D = 192
F = D // 2
N_STATE = 16
HID = 768
EPS = 1e-5
BANK = 512
CAP = int(1.25 * TOKENS * 2 / 8)


class Semaphores:

    def __init__(self):
        self.taken = []

    def take(self, nc, name):
        self.taken.append(nc.alloc_semaphore(name=name))
        return self.taken[-1]

    def hand_back(self, nc):
        nc.clear_and_free_semaphores(self.taken)
        nc.all_engine_barrier()


class Signal:

    def __init__(self, nc, held, name, per=1, unit=1, primed=True):
        self.sem = held.take(nc, name)
        self.per, self.unit, self.ahead = per, unit, int(primed)

    def now(self, i, k=None):
        return (i + self.ahead) * (self.per * self.unit) + (self.per if k is None else k) * self.unit

    def before(self, i, k=None):
        return (i - 1 + self.ahead) * (self.per * self.unit) + (self.per if k is None else k) * self.unit


def prime(eng, *signals):
    for s in signals:
        eng.sem_inc(s.sem, s.per * s.unit)


class Norm:

    def __init__(self, nc, held, name):
        self.mean = Signal(nc, held, name + "_mean")
        self.centred = Signal(nc, held, name + "_centred")
        self.square = Signal(nc, held, name + "_square")
        self.var = Signal(nc, held, name + "_var")
        self.log = Signal(nc, held, name + "_log")
        self.rstd = Signal(nc, held, name + "_rstd")


def load_all(sp, loads, sem):
    for dst, src in loads:
        sp.dma_start(dst, src).then_inc(sem, 16)
    return 16 * len(loads)


def mamba(nc, held, layer, dram, logits, slots, pairs):
    first = layer == 0
    P, C = (96, 2) if first else (128, 3)
    E = 4 if first else 8
    RING = 3
    T = str(layer)
    with ExitStack() as ctx:
        def sb(name, shape, dt=F32):
            return ctx.enter_context(nc.sbuf_tensor(f"m{T}_{name}", shape, dt))

        def ps(name, shape):
            return ctx.enter_context(nc.psum_tensor(f"m{T}_ps_{name}", shape, F32))

        def signal(name, per=1, unit=1):
            return Signal(nc, held, f"m{T}_{name}", per, unit)

        loads = []

        def const(name, key, shape, dt=F32):
            t = sb(name, shape, dt)
            flat = t[:] if len(shape) == 2 else t[:].rearrange(
                "p a b -> p (a b)" if len(shape) == 3 else "p a b c -> p (a b c)")
            loads.append((flat, dram[key]))
            return t

        ident = const("ident", "ident", [128, 128])
        select = const("select", "select", [96, 32, 128], BF16)
        avg = const("avg", "avg", [F, F])
        gate_w = const("gate_w", f"gate_w{T}", [F, 2, E])
        a_log = const("a_log", f"a_log{T}", [P, C, N_STATE])
        skip_w = const("skip_w", f"skip{T}", [P, C])
        dt_bias = const("dt_bias", f"dt_b{T}", [P, C])
        ln_g = const("ln_g", f"ln_g{T}", [F, 2])
        ln_b = const("ln_b", f"ln_b{T}", [F, 2])
        out_w = const("out_w", f"out_w{T}", [P, C, D])
        in_w = const("in_w", f"in_w{T}", [F, 2, 2 * P * C])
        if first:
            tok_w = const("tok_w", "tok_w", [128, 6, D])
            tok_b = const("tok_b", "tok_b", [F, 2])
            tok_g = const("tok_g", "tok_g", [F, 2])
            tok_beta = const("tok_beta", "tok_beta", [F, 2])
            class_token = const("class_token", "class_token", [F, 2])
            cls_tok = const("cls_tok", "cls_tok", [F, 2])
            pos = const("pos", "pos", [F, 2, SEQ - 1])
            conv_w = const("conv_w", "conv_w", [F, 2, 4])
            conv_b = const("conv_b", "conv_b", [F, 2])
            dt_w = const("dt_w", "dt_w0", [F, 2, D])
            bc_w = const("bc_w", "bc_w0", [F, 2, 32])
            gate_b = const("gate_b", "gate_b0", [ROWS, E])
        else:
            x_w = const("x_w", "x_w1", [P, C, 80])
            dt_w = const("dt_w", "dt_w1", [48, P * C])
        n_loads = 16 * len(loads)
        eps = sb("eps", [128, 1])
        a_neg = sb("a_neg", [P, C, N_STATE])

        if first:
            patches = sb("patches", [128, 2, 6, COLS - 4])
            emb = sb("emb", [F, 2, 2, SEQ])
            cls_emb = sb("cls_emb", [F, 2, 2, 2])
            x_pad = sb("x_pad", [F, 2, 2, SEQ + 3])
            conv = sb("conv", [F, 2, 2, SEQ])
        else:
            gathered = sb("gathered", [ROWS, 4, D])
            slot_ix = sb("slot_ix", [ROWS, 4], U32)
            low_rank = sb("low_rank", [48, COLS])
        h = sb("h", [F, 2, 2, COLS])
        xn = sb("xn", [F, 2, 2, COLS])
        cen = sb("cen", [F, 2, COLS])
        sq = sb("sq", [F, 2, COLS])
        logv = sb("logv", [F, COLS])
        rstd = sb("rstd", [F, COLS])
        u = sb("u", [P, 2, C, COLS])
        sz = sb("sz", [P, 2, C, COLS])
        sp_abs = sb("sp_abs", [P, C, COLS])
        sp_exp = sb("sp_exp", [P, C, COLS])
        sp_one = sb("sp_one", [P, C, COLS])
        sp_raw = sb("sp_raw", [P, C, COLS])
        dt = sb("dt", [P, 2, C, COLS])
        du = sb("du", [P, 2, C, COLS])
        bc_stack = sb("bc_stack", [96, 2, COLS], BF16)
        bc_rest = sb("bc_rest", [32, COLS])
        bc_mid = sb("bc_mid", [32, COLS], BF16)
        c_sb = sb("c_sb", [P, RING, COLS])
        decay = sb("decay", [P, RING, C, COLS])
        drive = sb("drive", [P, 2, C, COLS])
        state = sb("state", [P, RING, C, COLS])
        state_c = sb("state_c", [P, RING, C, COLS])
        y_skip = sb("y_skip", [P, C, COLS])
        y = sb("y", [P, C, COLS])
        r = sb("r", [F, 2, COLS])
        cen2 = sb("cen2", [F, 2, COLS])
        sq2 = sb("sq2", [F, 2, COLS])
        logv2 = sb("logv2", [F, COLS])
        rstd2 = sb("rstd2", [F, COLS])
        normed = sb("normed", [F, 2, COLS])
        h_out = sb("h_out", [F, 2, COLS])
        xf = sb("xf", [F, 2, COLS])
        rows = sb("rows", [ROWS, 4, D])
        rows_h = None if first else sb("rows_h", [ROWS, 4, D])

        ps_y = ps("y", [128, C, BANK])
        ps_b = ps("b", [128, BANK])
        ps_c = ps("c", [128, BANK])
        ps_f = ps("f", [128, 2, BANK])
        ps_k = ps("k", [128, BANK])

        loaded = held.take(nc, f"m{T}_loaded")
        ready = held.take(nc, f"m{T}_ready")
        waited = held.take(nc, f"m{T}_waited")
        in_landed = [signal(f"in_landed_{p}", 1, 16) for p in (0, 1)]
        norms = {k: Norm(nc, held, f"m{T}_{k}") for k in (["tok"] if first else []) + ["pre", "post", "ffn"]}
        setup = held.take(nc, f"m{T}_setup")
        if first:
            tok_done = signal("tok_done")
            emb_cls = signal("emb_cls")
            emb_done = signal("emb_done")
            tok_scaled = signal("tok_scaled")
            h_done = signal("h_done", 2)
            pad_done = signal("pad_done")
            conv_done = signal("conv_done", 8)
        else:
            ix_done = signal("ix_done")
            gather_landed = Signal(nc, held, f"m{T}_gather_landed", 4, 16, primed=False)
            turned = signal("turned")
            h_done = signal("h_done")
            rank_proj = signal("rank_proj")
            rank_copied = signal("rank_copied")
        xn_done = signal("xn_done")
        x_proj = signal("x_proj", C)
        z_proj = signal("z_proj", C)
        u_done = signal("u_done", C)
        z_done = signal("z_done", C)
        dt_proj = signal("dt_proj", C)
        bc_proj = signal("bc_proj")
        raw_done = signal("raw_done", C)
        abs_done = signal("abs_done")
        exp_done = signal("exp_done")
        one_done = signal("one_done")
        log_done = signal("log_done")
        corr_done = signal("corr_done")
        sum_done = signal("sum_done")
        dt_done = signal("dt_done")
        du_done = signal("du_done")
        bc_hi = signal("bc_hi")
        bc_r1 = signal("bc_r1")
        bc_m = signal("bc_m", 2)
        bc_lo = signal("bc_lo")
        b_spread = signal("b_spread", N_STATE)
        c_spread = signal("c_spread", N_STATE)
        c_copied = signal("c_copied", N_STATE)
        decayed = signal("decayed", N_STATE * C)
        driven = signal("driven", N_STATE)
        scanned = signal("scanned", N_STATE)
        weighed = signal("weighed", N_STATE)
        summed = signal("summed", N_STATE)
        skip_done = signal("skip_done", C)
        y_done = signal("y_done")
        out_proj = signal("out_proj", 2)
        r_done = signal("r_done", 2)
        r_scaled = signal("r_scaled")
        affine = signal("affine", 2)
        h_out_done = signal("h_out_done")
        xf_done = signal("xf_done")
        n_turn = 2 if first else 4
        rows_turned = signal("rows_turned", n_turn)
        rows_done = signal("rows_done", n_turn)
        gate_proj = signal("gate_proj")
        gate_done = signal("gate_done")
        stored = signal("stored", 2, 16)

        block = ctx.enter_context(nc.Block())
        half = range(2)

        @block.sync
        def _(sp):
            load_all(sp, loads, loaded)
            prime(sp, *in_landed, stored)

            def fetch(i, par):
                if first:
                    if not isinstance(i, int):
                        sp.wait_ge(tok_done.sem, tok_done.before(i - 1))
                    sp.dma_start(patches[:, par, :, :].rearrange("p a b -> p (a b)"),
                                 dram["x"][i, :, :]).then_inc(in_landed[par].sem, 16)
                else:
                    if not isinstance(i, int):
                        sp.wait_ge(h_out_done.sem, h_out_done.before(i - 1))
                    sp.dma_start(h[:, par, :, :].rearrange("p a b -> p (a b)"),
                                 dram["h0"][i, :, :]).then_inc(in_landed[par].sem, 16)

            def store(i):
                if first:
                    sp.wait_ge(h_out_done.sem, h_out_done.now(i))
                    sp.dma_start(dram["h0"][i, :, :], h_out[:].rearrange("p a b -> p (a b)")).then_inc(stored.sem, 16)
                else:
                    sp.wait_ge(rows_done.sem, rows_done.now(i))
                    sp.dma_start(dram["h1"][i, :, :], rows_h[:].rearrange("p a b -> p (a b)")).then_inc(stored.sem, 16)
                sp.wait_ge(rows_done.sem, rows_done.now(i))
                sp.dma_start(dram[f"xf{T}"][i, :, :], rows[:].rearrange("p a b -> p (a b)")).then_inc(stored.sem, 16)

            fetch(0, 0)
            fetch(1, 1)
            with sp.Fori(0, pairs // 2 - 1) as ii:
                for par in half:
                    store(2 * ii + par)
                    fetch(2 * ii + par + 2, par)
            store(pairs - 2)
            store(pairs - 1)
            sp.wait_ge(stored.sem, stored.now(pairs - 1))

        @block.tensor
        def _(pe):
            pe.wait_ge(loaded, n_loads)
            pe.wait_ge(ready, 3)
            prime(pe, x_proj, z_proj, dt_proj, bc_proj, b_spread, c_spread, summed, out_proj, rows_turned, gate_proj,
                  *(n.mean for n in norms.values()), *(n.var for n in norms.values()))
            if first:
                prime(pe, tok_done)
            else:
                prime(pe, turned, rank_proj)

            def average(src, bank, sig):
                for c in half:
                    mm = nc.tensor.matmul(bank[0:F, 0:COLS], avg[:, :], src[:, c, :], start=(c == 0), stop=(c == 1))
                mm.then_inc(sig.sem, 1)

            def project(bank, m0, m1, weights, src, k):
                for c in range(k):
                    mm = nc.tensor.matmul(bank[0:m1 - m0, 0:COLS], weights[:, c, m0:m1], src[:, c, :],
                                          start=(c == 0), stop=(c == k - 1))
                return mm

            def front(ii, i, par):
                if first:
                    pe.wait_ge(in_landed[par].sem, in_landed[par].now(ii))
                    pe.wait_ge(bc_r1.sem, bc_r1.before(i))
                    pe.wait_ge(bc_hi.sem, bc_hi.before(i))
                    pe.wait_ge(raw_done.sem, raw_done.before(i))
                    for c in half:
                        for k in range(6):
                            mm = nc.tensor.matmul(ps_f[0:F, c, 0:COLS - 4], tok_w[:, k, c * F:(c + 1) * F],
                                                  patches[:, par, k, :], start=(k == 0), stop=(k == 5))
                    mm.then_inc(tok_done.sem, 1)
                    n = norms["tok"]
                    e = emb[:].rearrange("p c m t -> p c (m t)")
                    pe.wait_ge(emb_done.sem, emb_done.now(i))
                    average(e, ps_f[:, 0, :], n.mean)
                    pe.wait_ge(n.square.sem, n.square.now(i))
                    average(sq, ps_f[:, 1, :], n.var)
                else:
                    pe.wait_ge(gather_landed.sem, gather_landed.now(i))
                    pe.wait_ge(raw_done.sem, raw_done.before(i))
                    for c in half:
                        for j in range(4):
                            mm = nc.tensor.transpose(ps_f[0:F, c, j * ROWS:(j + 1) * ROWS],
                                                     gathered[:, j, c * F:(c + 1) * F], ident[0:ROWS, 0:ROWS])
                    mm.then_inc(turned.sem, 1)
                n = norms["pre"]
                pe.wait_ge(h_done.sem, h_done.now(i))
                average(h[:, par, :, :], ps_f[:, 0, :], n.mean)
                pe.wait_ge(n.square.sem, n.square.now(i))
                average(sq, ps_f[:, 1, :], n.var)
                pe.wait_ge(xn_done.sem, xn_done.now(i))
                for c in range(C):
                    if c >= 2:
                        pe.wait_ge(u_done.sem, u_done.now(i, c - 1))
                    project(ps_f[:, c % 2, :], c * P, (c + 1) * P, in_w, xn[:, par, :, :], 2).then_inc(x_proj.sem, 1)
                for c in range(C):
                    b = (C + c) % 2
                    if first:
                        pe.wait_ge(pad_done.sem, pad_done.now(i))
                    elif c < 2:
                        pe.wait_ge(u_done.sem, u_done.now(i, C - 1 + c))
                    else:
                        pe.wait_ge(z_done.sem, z_done.now(i, c - 1))
                    project(ps_f[:, b, :], (C + c) * P, (C + c + 1) * P, in_w, xn[:, par, :, :], 2).then_inc(z_proj.sem, 1)
                pe.wait_ge(u_done.sem, u_done.now(i))
                pe.wait_ge(z_done.sem, z_done.now(i))
                if first:
                    for c in half:
                        project(ps_f[:, c, :], c * P, (c + 1) * P, dt_w, u[:, par, :, :], C).then_inc(dt_proj.sem, 1)
                    pe.wait_ge(raw_done.sem, raw_done.now(i, 1))
                    project(ps_f[:, 0, :], 0, 32, bc_w, u[:, par, :, :], C).then_inc(bc_proj.sem, 1)
                else:
                    project(ps_f[:, 0, :], 0, 48, x_w, u[:, par, :, :], C).then_inc(rank_proj.sem, 1)
                    project(ps_f[:, 1, :], 48, 80, x_w, u[:, par, :, :], C).then_inc(bc_proj.sem, 1)
                    pe.wait_ge(rank_copied.sem, rank_copied.now(i))
                    for c in range(C):
                        if c == 1:
                            pe.wait_ge(bc_hi.sem, bc_hi.now(i))
                            pe.wait_ge(bc_r1.sem, bc_r1.now(i))
                        if c == 2:
                            pe.wait_ge(raw_done.sem, raw_done.now(i, 1))
                        nc.tensor.matmul(ps_f[0:P, c % 2, 0:COLS], dt_w[:, c * P:(c + 1) * P], low_rank[:, :],
                                         start=True, stop=True).then_inc(dt_proj.sem, 1)

            def sum_states(i, par, n):
                pe.wait_ge(weighed.sem, weighed.now(i, n + 1))
                if n == 0:
                    pe.wait_ge(skip_done.sem, skip_done.before(i))
                for c in range(C):
                    mm = nc.tensor.matmul(ps_y[0:P, c, 0:COLS], ident[0:P, 0:P], state_c[:, n % RING, c, :],
                                          start=(n == 0), stop=(n == N_STATE - 1))
                mm.then_inc(summed.sem, 1)

            def scan(i, par):
                pe.wait_ge(bc_lo.sem, bc_lo.now(i))
                pe.wait_ge(bc_m.sem, bc_m.now(i))
                for n in range(N_STATE):
                    pe.wait_ge(driven.sem, driven.now(i, n) if n else driven.before(i))
                    nc.tensor.matmul(ps_b[0:P, 0:COLS], select[:, n, 0:P], bc_stack[:, par, :],
                                     start=True, stop=True).then_inc(b_spread.sem, 1)
                    pe.wait_ge(c_copied.sem, c_copied.now(i, n) if n else c_copied.before(i))
                    nc.tensor.matmul(ps_c[0:P, 0:COLS], select[:, N_STATE + n, 0:P], bc_stack[:, par, :],
                                     start=True, stop=True).then_inc(c_spread.sem, 1)
                    if n >= 2:
                        sum_states(i, par, n - 2)
                sum_states(i, par, N_STATE - 2)
                sum_states(i, par, N_STATE - 1)

            def back(i, par):
                pe.wait_ge(y_done.sem, y_done.now(i))
                for c in half:
                    if c:
                        pe.wait_ge(r_done.sem, r_done.now(i, 1))
                    else:
                        pe.wait_ge(gate_done.sem, gate_done.before(i))
                    project(ps_k, c * F, (c + 1) * F, out_w, y, C).then_inc(out_proj.sem, 1)
                n = norms["post"]
                pe.wait_ge(r_done.sem, r_done.now(i))
                average(r, ps_k, n.mean)
                pe.wait_ge(n.square.sem, n.square.now(i))
                average(sq2, ps_k, n.var)
                n = norms["ffn"]
                pe.wait_ge(h_out_done.sem, h_out_done.now(i))
                average(h_out, ps_k, n.mean)
                pe.wait_ge(n.square.sem, n.square.now(i))
                average(sq2, ps_k, n.var)
                pe.wait_ge(xf_done.sem, xf_done.now(i))
                for t in range(n_turn):
                    src = xf if t < 2 else h_out
                    if t:
                        pe.wait_ge(rows_done.sem, rows_done.now(i, t))
                    for j in half:
                        for c in half:
                            a = (2 * (t % 2) + j) * ROWS
                            mm = nc.tensor.transpose(ps_k[0:ROWS, j * D + c * F:j * D + (c + 1) * F],
                                                     src[:, c, a:a + ROWS], ident[0:F, 0:F])
                    mm.then_inc(rows_turned.sem, 1)
                pe.wait_ge(rows_done.sem, rows_done.now(i))
                for j in range(4):
                    for c in half:
                        mm = nc.tensor.matmul(ps_k[0:ROWS, j * E:(j + 1) * E], xf[:, c, j * ROWS:(j + 1) * ROWS],
                                              gate_w[:, c, :], start=(c == 0), stop=(c == 1))
                mm.then_inc(gate_proj.sem, 1)

            with pe.Fori(0, pairs // 2) as ii:
                for par in half:
                    i = 2 * ii + par
                    front(ii, i, par)
                    scan(i, par)
                    back(i, par)

        @block.scalar
        def _(act):
            act.wait_ge(loaded, n_loads)
            act.wait_ge(ready, 1)
            prime(act, u_done, z_done, raw_done, abs_done, exp_done, log_done, bc_hi, bc_m, c_copied, decayed, affine, rows_done,
                  *(n.square for n in norms.values()), *(n.log for n in norms.values()),
                  *(n.rstd for n in norms.values()))
            if first:
                prime(act, h_done, pad_done)
            else:
                prime(act, rank_copied)
            nc.scalar.activation(a_neg[:].rearrange("p a b -> p (a b)"), a_log[:].rearrange("p a b -> p (a b)"),
                                 ACT.Exp).then_inc(ready, 1)
            act.wait_ge(ready, 3)

            def norm(n, i, cen, sq, logv, rstd, bank):
                act.wait_ge(n.centred.sem, n.centred.now(i))
                nc.scalar.activation(sq[:], cen[:], ACT.Square).then_inc(n.square.sem, 1)
                act.wait_ge(n.var.sem, n.var.now(i))
                nc.scalar.activation(logv[:, :], bank[0:F, 0:COLS], ACT.Ln, bias=eps[0:F, :]).then_inc(n.log.sem, 1)
                act.wait_ge(n.log.sem, n.log.now(i))
                nc.scalar.activation(rstd[:, :], logv[:, :], ACT.Exp, scale=-0.5).then_inc(n.rstd.sem, 1)

            def front(ii, i, par):
                if first:
                    n = norms["tok"]
                    norm(n, i, cen, sq, logv, rstd, ps_f[:, 1, :])
                    act.wait_ge(tok_scaled.sem, tok_scaled.now(i))
                    act.wait_ge(h_out_done.sem, h_out_done.before(i))
                    for c in half:
                        nc.scalar.activation(
                            h[:, par, c, :].rearrange("p (m t) -> p m t", m=2)[:, :, 1:SEQ],
                            emb[:, c, :, 1:SEQ], ACT.Identity, bias=tok_beta[:, c:c + 1],
                            scale=tok_g[:, c:c + 1]).then_inc(h_done.sem, 1)
                norm(norms["pre"], i, cen, sq, logv, rstd, ps_f[:, 1, :])
                if first:
                    act.wait_ge(x_proj.sem, x_proj.now(i))
                    act.wait_ge(conv_done.sem, conv_done.before(i))
                    nc.scalar.activation(x_pad[:, :, :, 3:], ps_f[0:F, :, 0:COLS].rearrange(
                        "p c (m t) -> p c m t", m=2), ACT.Copy).then_inc(pad_done.sem, 1)
                else:
                    for c in range(C):
                        act.wait_ge(x_proj.sem, x_proj.now(i, c + 1))
                        nc.scalar.activation(u[:, par, c, :], ps_f[0:P, c % 2, 0:COLS], ACT.Silu).then_inc(u_done.sem, 1)
                for c in range(C):
                    act.wait_ge(z_proj.sem, z_proj.now(i, c + 1))
                    nc.scalar.activation(sz[:, par, c, :], ps_f[0:P, (C + c) % 2, 0:COLS], ACT.Silu).then_inc(z_done.sem, 1)
                if first:
                    for c in range(C):
                        act.wait_ge(conv_done.sem, conv_done.now(i, 4 * c + 4))
                        nc.scalar.activation(u[:, par, c, :], conv[:, c, :, :].rearrange("p m t -> p (m t)"),
                                             ACT.Silu, bias=conv_b[:, c:c + 1]).then_inc(u_done.sem, 1)
                else:
                    act.wait_ge(rank_proj.sem, rank_proj.now(i))
                    nc.scalar.activation(low_rank[:, :], ps_f[0:48, 0, 0:COLS], ACT.Copy).then_inc(rank_copied.sem, 1)
                    split_hi(i, par, 1)
                for c in range(C):
                    act.wait_ge(dt_proj.sem, dt_proj.now(i, c + 1))
                    if c == 0:
                        act.wait_ge(dt_done.sem, dt_done.before(i))
                    nc.scalar.activation(sp_raw[:, c, :], ps_f[0:P, c % 2, 0:COLS], ACT.Identity,
                                         bias=dt_bias[:, c:c + 1]).then_inc(raw_done.sem, 1)
                if first:
                    split_hi(i, par, 0)
                act.wait_ge(raw_done.sem, raw_done.now(i))
                nc.scalar.activation(sp_abs[:], sp_raw[:], ACT.Abs).then_inc(abs_done.sem, 1)
                act.wait_ge(abs_done.sem, abs_done.now(i))
                act.wait_ge(sum_done.sem, sum_done.before(i))
                nc.scalar.activation(sp_exp[:], sp_abs[:], ACT.Exp, scale=-1.0).then_inc(exp_done.sem, 1)
                act.wait_ge(one_done.sem, one_done.now(i))
                act.wait_ge(exp_done.sem, exp_done.now(i))
                nc.scalar.activation(sp_abs[:], sp_one[:], ACT.Ln).then_inc(log_done.sem, 1)
                act.wait_ge(bc_r1.sem, bc_r1.now(i))
                nc.scalar.activation(bc_mid[:, :], bc_rest[:, :], ACT.Copy).then_inc(bc_m.sem, 1)
                nc.scalar.activation(bc_stack[32:64, par, :], bc_rest[:, :], ACT.Copy).then_inc(bc_m.sem, 1)

            def split_hi(i, par, bank):
                act.wait_ge(bc_proj.sem, bc_proj.now(i))
                nc.scalar.activation(bc_stack[0:32, par, :], ps_f[0:32, bank, 0:COLS], ACT.Copy).then_inc(bc_hi.sem, 1)

            def scan(i, par):
                act.wait_ge(dt_done.sem, dt_done.now(i))
                for n in range(N_STATE):
                    k = n - RING + 1
                    act.wait_ge(scanned.sem, scanned.now(i, k) if k > 0 else scanned.before(i, N_STATE + k))
                    for c in range(C):
                        nc.scalar.activation(
                            decay[:, n % RING, c, :].rearrange("p (m t) -> p m t", m=2)[:, :, 1:SEQ],
                            dt[:, par, c, :].rearrange("p (m t) -> p m t", m=2)[:, :, 1:SEQ],
                            ACT.Exp, scale=a_neg[:, c, n:n + 1]).then_inc(decayed.sem, 1)
                    act.wait_ge(c_spread.sem, c_spread.now(i, n + 1))
                    act.wait_ge(weighed.sem, weighed.now(i, k) if k > 0 else weighed.before(i, N_STATE + k))
                    nc.scalar.activation(c_sb[:, n % RING, :], ps_c[0:P, 0:COLS], ACT.Copy).then_inc(c_copied.sem, 1)

            def back(i, par):
                norm(norms["post"], i, cen2, sq2, logv2, rstd2, ps_k)
                act.wait_ge(r_scaled.sem, r_scaled.now(i))
                for c in half:
                    nc.scalar.activation(normed[:, c, :], r[:, c, :], ACT.Identity, bias=ln_b[:, c:c + 1],
                                         scale=ln_g[:, c:c + 1]).then_inc(affine.sem, 1)
                norm(norms["ffn"], i, cen2, sq2, logv2, rstd2, ps_k)
                for t in range(n_turn):
                    act.wait_ge(rows_turned.sem, rows_turned.now(i, t + 1))
                    if t == 0:
                        act.wait_ge(stored.sem, stored.before(i))
                    dst = rows if t < 2 else rows_h
                    nc.scalar.activation(dst[:, 2 * (t % 2):2 * (t % 2) + 2, :].rearrange("p a b -> p (a b)"),
                                         ps_k[0:ROWS, 0:2 * D], ACT.Copy).then_inc(rows_done.sem, 1)

            with act.Fori(0, pairs // 2) as ii:
                for par in half:
                    i = 2 * ii + par
                    front(ii, i, par)
                    scan(i, par)
                    back(i, par)

        @block.gpsimd
        def _(pool):
            prime(pool, weighed)

            def gather(i):
                pool.wait_ge(ix_done.sem, ix_done.now(i))
                pool.wait_ge(turned.sem, turned.before(i))
                pool.sem_inc(waited, 1)
                for j in range(4):
                    pool.indirect_dma_start(
                        out=gathered[:, j, :], out_offset=None, in_=dram["moe_out0"],
                        in_offset=bass.IndirectOffsetOnAxis(ap=slot_ix[:, j:j + 1], axis=0)).then_inc(gather_landed.sem, 16)

            def scan(i, par):
                for n in range(N_STATE):
                    pool.wait_ge(scanned.sem, scanned.now(i, n + 1))
                    pool.wait_ge(c_copied.sem, c_copied.now(i, n + 1))
                    k = n - RING + 1
                    pool.wait_ge(summed.sem, summed.now(i, k) if k > 0 else summed.before(i, N_STATE + k))
                    nc.gpsimd.tensor_tensor(state_c[:, n % RING, :, :], state[:, n % RING, :, :],
                                            c_sb[:, n % RING, :].unsqueeze(1).to_broadcast([P, C, COLS]),
                                            ALU.mult).then_inc(weighed.sem, 1)

            with pool.Fori(0, pairs // 2) as ii:
                for par in half:
                    i = 2 * ii + par
                    if not first:
                        gather(i)
                    scan(i, par)

        @block.vector
        def _(dve):
            nc.vector.memset(eps[:, :], EPS).then_inc(ready, 1)
            chain = [0]

            def link(ins):
                chain[0] += 1
                ins.then_inc(setup, 1)
                dve.wait_ge(setup, chain[0])

            link(nc.vector.memset(decay[:].rearrange("p a b c -> p (a b c)"), 0.0))
            dve.wait_ge(loaded, n_loads)
            if first:
                link(nc.vector.memset(x_pad[:].rearrange("p a b c -> p (a b c)"), 0.0))
                for c in half:
                    link(nc.vector.tensor_scalar(pos[:, c, 1:], pos[:, c, 1:], tok_b[:, c:c + 1], None, ALU.add))
                    for m in half:
                        link(nc.vector.tensor_tensor(emb[:, c, m, 1:2], pos[:, c, 0:1], class_token[:, c:c + 1], ALU.add))
                        link(nc.vector.tensor_copy(emb[:, c, m, 0:1], cls_tok[:, c:c + 1]))
                        for par in half:
                            link(nc.vector.tensor_copy(h[:, par, c, m * SEQ:m * SEQ + 1], cls_tok[:, c:c + 1]))
                link(nc.vector.tensor_copy(cls_emb[:].rearrange("p c m t -> p (c m) t"),
                                           emb[:, :, :, 0:2].rearrange("p c m t -> p (c m) t")))
            prime(dve, gate_done, xn_done, one_done, corr_done, sum_done, dt_done, du_done, bc_r1, bc_lo, driven, scanned,
                  skip_done, y_done, r_done, r_scaled, h_out_done, xf_done, *(n.centred for n in norms.values()))
            if first:
                prime(dve, emb_done, emb_cls, tok_scaled, conv_done)
            else:
                prime(dve, h_done, ix_done)
            dve.wait_ge(ready, 2)
            nc.vector.tensor_scalar(a_neg[:].rearrange("p a b -> p (a b)"), a_neg[:].rearrange("p a b -> p (a b)"),
                                    -1.0, None, ALU.mult).then_inc(ready, 1)

            def wide(t):
                return t.unsqueeze(1).to_broadcast([t.shape[0], 2, COLS])

            def centre(n, i, src, cen, bank):
                dve.wait_ge(n.mean.sem, n.mean.now(i))
                nc.vector.tensor_tensor(cen[:], src, wide(bank[0:F, 0:COLS]), ALU.subtract).then_inc(n.centred.sem, 1)

            def scale(n, i, dst, cen, rstd, sig):
                dve.wait_ge(n.rstd.sem, n.rstd.now(i))
                nc.vector.tensor_tensor(dst, cen[:], wide(rstd[:, :]), ALU.mult).then_inc(sig.sem, 1)

            def front(ii, i, par):
                if first:
                    dve.wait_ge(tok_done.sem, tok_done.now(i))
                    dve.wait_ge(h_done.sem, h_done.before(i))
                    nc.vector.tensor_copy(emb[:, :, :, 0:2].rearrange("p c m t -> p (c m) t"),
                                          cls_emb[:].rearrange("p c m t -> p (c m) t")).then_inc(emb_cls.sem, 1)
                    nc.vector.tensor_tensor(
                        emb[:, :, :, 2:], ps_f[0:F, :, 0:COLS - 4].rearrange("p c (m t) -> p c m t", m=2),
                        pos[:, :, 1:].unsqueeze(2).to_broadcast([F, 2, 2, SEQ - 2]), ALU.add).then_inc(emb_done.sem, 1)
                    n = norms["tok"]
                    e = emb[:].rearrange("p c m t -> p c (m t)")
                    dve.wait_ge(emb_cls.sem, emb_cls.now(i))
                    dve.wait_ge(emb_done.sem, emb_done.now(i))
                    centre(n, i, e, cen, ps_f[:, 0, :])
                    scale(n, i, e, cen, rstd, tok_scaled)
                else:
                    nc.vector.tensor_copy(slot_ix[:, :], slots[:, bass.ds(i * 4, 4)]).then_inc(ix_done.sem, 1)
                    dve.wait_ge(turned.sem, turned.now(i))
                    dve.wait_ge(in_landed[par].sem, in_landed[par].now(ii))
                    nc.vector.tensor_tensor(h[:, par, :, :], h[:, par, :, :], ps_f[0:F, :, 0:COLS],
                                            ALU.add).then_inc(h_done.sem, 1)
                dve.wait_ge(h_done.sem, h_done.now(i))
                centre(norms["pre"], i, h[:, par, :, :], cen, ps_f[:, 0, :])
                scale(norms["pre"], i, xn[:, par, :, :], cen, rstd, xn_done)
                if first:
                    dve.wait_ge(pad_done.sem, pad_done.now(i))
                    dve.wait_ge(u_done.sem, u_done.before(i))
                    for c in half:
                        nc.vector.tensor_scalar(conv[:, c, :, :], x_pad[:, c, :, 0:SEQ], conv_w[:, c, 0:1], None,
                                                ALU.mult).then_inc(conv_done.sem, 1)
                        for k in range(1, 4):
                            dve.wait_ge(conv_done.sem, conv_done.now(i, 4 * c + k))
                            nc.vector.scalar_tensor_tensor(
                                out=conv[:, c, :, :], in0=x_pad[:, c, :, k:k + SEQ], scalar=conv_w[:, c, k:k + 1],
                                in1=conv[:, c, :, :], op0=ALU.mult, op1=ALU.add).then_inc(conv_done.sem, 1)
                else:
                    split_rest(i, par, 1)
                if first:
                    split_rest(i, par, 0)
                dve.wait_ge(exp_done.sem, exp_done.now(i))
                nc.vector.tensor_scalar(sp_one[:], sp_exp[:], 1.0, None, ALU.add).then_inc(one_done.sem, 1)
                dve.wait_ge(one_done.sem, one_done.now(i))
                dve.wait_ge(log_done.sem, log_done.now(i))
                nc.vector.scalar_tensor_tensor(out=sp_exp[:], in0=sp_one[:], scalar=1.0, in1=sp_exp[:],
                                               op0=ALU.subtract, op1=ALU.subtract).then_inc(corr_done.sem, 1)
                dve.wait_ge(corr_done.sem, corr_done.now(i))
                nc.vector.tensor_tensor(sp_abs[:], sp_abs[:], sp_exp[:], ALU.subtract).then_inc(sum_done.sem, 1)
                dve.wait_ge(sum_done.sem, sum_done.now(i))
                nc.vector.scalar_tensor_tensor(out=dt[:, par, :, :], in0=sp_raw[:], scalar=0.0, in1=sp_abs[:],
                                               op0=ALU.max, op1=ALU.add).then_inc(dt_done.sem, 1)
                dve.wait_ge(dt_done.sem, dt_done.now(i))
                dve.wait_ge(u_done.sem, u_done.now(i))
                nc.vector.tensor_tensor(du[:, par, :, :], dt[:, par, :, :], u[:, par, :, :], ALU.mult).then_inc(du_done.sem, 1)
                dve.wait_ge(bc_m.sem, bc_m.now(i))
                nc.vector.tensor_tensor(bc_stack[64:96, par, :], bc_rest[:, :], bc_mid[:, :],
                                        ALU.subtract).then_inc(bc_lo.sem, 1)

            def split_rest(i, par, bank):
                dve.wait_ge(bc_hi.sem, bc_hi.now(i))
                dve.wait_ge(bc_lo.sem, bc_lo.before(i))
                nc.vector.tensor_tensor(bc_rest[:, :], ps_f[0:32, bank, 0:COLS], bc_stack[0:32, par, :],
                                        ALU.subtract).then_inc(bc_r1.sem, 1)

            def scan(i, par):
                dve.wait_ge(du_done.sem, du_done.now(i))
                for n in range(N_STATE):
                    dve.wait_ge(b_spread.sem, b_spread.now(i, n + 1))
                    if n >= 2:
                        dve.wait_ge(scanned.sem, scanned.now(i, n - 1))
                    else:
                        dve.wait_ge(scanned.sem, scanned.before(i, N_STATE + n - 1))
                    nc.vector.tensor_tensor(drive[:, n % 2, :, :], du[:, par, :, :],
                                            ps_b[0:P, 0:COLS].unsqueeze(1).to_broadcast([P, C, COLS]),
                                            ALU.mult).then_inc(driven.sem, 1)
                    dve.wait_ge(driven.sem, driven.now(i, n + 1))
                    dve.wait_ge(decayed.sem, decayed.now(i, C * (n + 1)))
                    k = n - RING + 1
                    dve.wait_ge(weighed.sem, weighed.now(i, k) if k > 0 else weighed.before(i, N_STATE + k))
                    nc.vector.tensor_tensor_scan(
                        state[:, n % RING, :, :].rearrange("p a b -> p (a b)"),
                        decay[:, n % RING, :, :].rearrange("p a b -> p (a b)"),
                        drive[:, n % 2, :, :].rearrange("p a b -> p (a b)"), 0.0, ALU.mult, ALU.add).then_inc(scanned.sem, 1)

            def back(i, par):
                dve.wait_ge(summed.sem, summed.now(i))
                dve.wait_ge(y_done.sem, y_done.before(i))
                for c in range(C):
                    nc.vector.scalar_tensor_tensor(out=y_skip[:, c, :], in0=u[:, par, c, :], scalar=skip_w[:, c:c + 1],
                                                   in1=ps_y[0:P, c, 0:COLS], op0=ALU.mult,
                                                   op1=ALU.add).then_inc(skip_done.sem, 1)
                dve.wait_ge(skip_done.sem, skip_done.now(i))
                dve.wait_ge(out_proj.sem, out_proj.before(i))
                dve.wait_ge(z_done.sem, z_done.now(i))
                nc.vector.tensor_tensor(y[:], y_skip[:], sz[:, par, :, :], ALU.mult).then_inc(y_done.sem, 1)
                for c in half:
                    dve.wait_ge(out_proj.sem, out_proj.now(i, c + 1))
                    dve.wait_ge(affine.sem, affine.before(i))
                    nc.vector.tensor_tensor(r[:, c, :], ps_k[0:F, 0:COLS], xn[:, par, c, :], ALU.add).then_inc(r_done.sem, 1)
                n = norms["post"]
                dve.wait_ge(r_done.sem, r_done.now(i))
                centre(n, i, r[:], cen2, ps_k)
                scale(n, i, r[:], cen2, rstd2, r_scaled)
                dve.wait_ge(affine.sem, affine.now(i))
                dve.wait_ge(stored.sem, stored.before(i))
                dve.wait_ge(rows_turned.sem, rows_turned.before(i))
                nc.vector.tensor_tensor(h_out[:], h[:, par, :, :], normed[:], ALU.add).then_inc(h_out_done.sem, 1)
                n = norms["ffn"]
                dve.wait_ge(h_out_done.sem, h_out_done.now(i))
                centre(n, i, h_out[:], cen2, ps_k)
                dve.wait_ge(gate_proj.sem, gate_proj.before(i))
                scale(n, i, xf[:], cen2, rstd2, xf_done)
                dve.wait_ge(gate_proj.sem, gate_proj.now(i))
                dst = logits[:, bass.ds(i * 4, 4), 0:E]
                src = ps_k[0:ROWS, 0:4 * E].rearrange("p (j e) -> p j e", e=E)
                if first:
                    nc.vector.tensor_tensor(dst, src, gate_b[:, :].unsqueeze(1).to_broadcast([ROWS, 4, E]),
                                            ALU.add).then_inc(gate_done.sem, 1)
                else:
                    nc.vector.tensor_copy(dst, src).then_inc(gate_done.sem, 1)

            with dve.Fori(0, pairs // 2) as ii:
                for par in half:
                    i = 2 * ii + par
                    front(ii, i, par)
                    scan(i, par)
                    back(i, par)


TOP = (1, 2)
EXPERTS = (4, 8)
BLOCKS = tuple(TOKENS * TOP[t] // COLS + EXPERTS[t] - 1 for t in (0, 1))
BISECT = 24


def route(nc, held, layer, dram, logits, slots_in, slots_out, weights, expert_of):
    E, K = EXPERTS[layer], TOP[layer]
    NB = BLOCKS[layer]
    DROP = NB * COLS
    T = str(layer)
    with ExitStack() as ctx:
        def sb(name, shape, dt=F32):
            return ctx.enter_context(nc.sbuf_tensor(f"r{T}_{name}", shape, dt))

        def sem(name):
            return held.take(nc, f"r{T}_{name}")

        earlier = sb("earlier", [ROWS, ROWS])
        ones = sb("ones", [ROWS, ROWS])
        steps = sb("steps", [ROWS, 32])
        numbers = sb("numbers", [ROWS, BLOCKS[1]])
        token_of = sb("token_of", [ROWS, TILES])
        zeros = sb("zeros", [ROWS, 4 * D])
        best = sb("best", [ROWS, K, TILES])
        free = sb("free", [ROWS, TILES])
        work = sb("work", [ROWS, E, TILES])
        equal = sb("equal", [ROWS, E, TILES])
        chosen = sb("chosen", [ROWS, K, E, TILES])
        keep = sb("keep", [ROWS, E, TILES])
        score = sb("score", [ROWS, E, TILES])
        flags = sb("flags", [ROWS, E, TILES])
        flags2 = sb("flags2", [ROWS, E, TILES])
        restart = sb("restart", [ROWS, E, TILES])
        run = sb("run", [ROWS, E, TILES])
        place = sb("place", [ROWS, E, TILES])
        bar = sb("bar", [ROWS, E])
        cand = sb("cand", [ROWS, E])
        step = sb("step", [ROWS, 1])
        part = sb("part", [ROWS, E])
        quota = sb("quota", [ROWS, E])
        over = sb("over", [ROWS, E, 32])
        n_blocks = sb("n_blocks", [ROWS, E])
        ends = sb("ends", [ROWS, E])
        base = sb("base", [ROWS, E])
        owner = sb("owner", [ROWS, NB, E])
        kept = sb("kept", [ROWS, TILES])
        spot = sb("spot", [ROWS, TILES])
        lost = sb("lost", [ROWS, TILES])
        ratio = sb("ratio", [ROWS, TILES])
        rows = sb("rows", [ROWS, 2, 4, D])
        index = sb("index", [ROWS, 2, K, 4], U32)

        ps_sum = ctx.enter_context(nc.psum_tensor(f"r{T}_ps_sum", [128, BANK], F32))
        ps_tile = ctx.enter_context(nc.psum_tensor(f"r{T}_ps_tile", [128, 2, BANK], F32))
        ps_in = ctx.enter_context(nc.psum_tensor(f"r{T}_ps_in", [128, 2, BANK], F32))

        loaded = sem("loaded")
        waited = sem("waited")
        dve_step = sem("dve_step")
        gap_ready = sem("gap_ready")
        exp_ready = sem("exp_ready")
        zeros_ready = sem("zeros_ready")
        zeroed = sem("zeroed")
        slots_ready = sem("slots_ready")
        rounds_counted = Signal(nc, held, f"r{T}_rounds_counted")
        rounds_summed = Signal(nc, held, f"r{T}_rounds_summed")
        flags_ready = sem("flags_ready")
        prefix_ready = sem("prefix_ready")
        rows_landed = [Signal(nc, held, f"r{T}_rows_landed_{p}", 1, 16) for p in (0, 1)]
        index_ready = Signal(nc, held, f"r{T}_index_ready")
        scattered = [Signal(nc, held, f"r{T}_scattered_{p}", 4 * K, 16, primed=False) for p in (0, 1)]
        halves = range((E * TILES + BANK - 1) // BANK)
        wide = E * TILES // len(halves)

        block = ctx.enter_context(nc.Block())

        @block.sync
        def _(sp):
            loads = [(earlier[:, :], dram["earlier"]), (ones[:, :], dram["ones"]), (steps[:, :], dram["steps"]),
                     (numbers[:, :], dram["numbers"]), (token_of[:, :], dram["token_of"])]
            load_all(sp, loads, loaded)
            prime(sp, *rows_landed)
            sp.wait_ge(zeros_ready, 1)
            sp.dma_start(dram["moe_out" + T][DROP:DROP + 1, :], zeros[0:1, 0:D]).then_inc(zeroed, 16)
            with sp.Fori(0, NB) as b:
                sp.dma_start(dram["moe_in" + T][bass.ds(b * COLS, COLS), :].rearrange("(p j) d -> p (j d)", j=4),
                             zeros[:, :]).then_inc(zeroed, 16)

            def fetch(i, par):
                sp.dma_start(rows[:, par, :, :].rearrange("p a b -> p (a b)"),
                             dram["xf" + T][i, :, :]).then_inc(rows_landed[par].sem, 16)

            fetch(0, 0)
            fetch(1, 1)
            with sp.Fori(1, PAIRS // 2) as ii:
                for par in (0, 1):
                    sp.wait_ge(scattered[par].sem, scattered[par].before(ii))
                    sp.dma_start(rows[:, par, :, :].rearrange("p a b -> p (a b)"),
                                 dram["xf" + T][2 * ii + par, :, :]).then_inc(rows_landed[par].sem, 16)

        @block.scalar
        def _(act):
            if K == 2:
                act.wait_ge(gap_ready, 1)
                nc.scalar.activation(ratio[:, :], lost[:, :], ACT.Exp).then_inc(exp_ready, 1)

        @block.tensor
        def _(pe):
            pe.wait_ge(loaded, 16 * 5)
            prime(pe, rounds_summed)
            if K == 2:
                with pe.Fori(0, BISECT + 1) as r:
                    pe.wait_ge(rounds_counted.sem, rounds_counted.now(r))
                    nc.tensor.matmul(ps_sum[0:ROWS, 0:E], ones[:, :], part[:, :], start=True,
                                     stop=True).then_inc(rounds_summed.sem, 1)

            for turn in range(K):
                pe.wait_ge(flags_ready, turn + 1)
                source = flags if turn < K - 1 else keep
                source = source[:].rearrange("p e t -> p (e t)")
                for x in halves:
                    nc.tensor.matmul(ps_in[0:ROWS, x, 0:wide], earlier[:, :], source[:, x * wide:(x + 1) * wide],
                                     start=True, stop=True)
                    mm = nc.tensor.matmul(ps_tile[0:ROWS, x, 0:wide], ones[:, :], source[:, x * wide:(x + 1) * wide],
                                          start=True, stop=True)
                mm.then_inc(prefix_ready, 1)

        @block.vector
        def _(dve):
            count = [0]

            def link(ins):
                count[0] += 1
                ins.then_inc(dve_step, 1)
                dve.wait_ge(dve_step, count[0])

            def over_experts(t):
                return t.unsqueeze(1).to_broadcast([ROWS, E, TILES])

            def over_tiles(t):
                return t.unsqueeze(2).to_broadcast([ROWS, E, TILES])

            nc.vector.memset(zeros[:, :], 0.0).then_inc(zeros_ready, 1)
            link(nc.vector.memset(restart[:].rearrange("p e t -> p (e t)"), 1.0))
            link(nc.vector.memset(restart[:, :, 0:1], 0.0))
            by_expert = logits[:, :, 0:E].rearrange("p t e -> p e t")
            for k in range(K):
                if k == 0:
                    link(nc.vector.tensor_copy(work[:], by_expert))
                else:
                    link(nc.vector.scalar_tensor_tensor(
                        out=work[:].rearrange("p e t -> p (e t)"),
                        in0=chosen[:, 0, :, :].rearrange("p e t -> p (e t)"), scalar=-3.0e38,
                        in1=work[:].rearrange("p e t -> p (e t)"), op0=ALU.mult, op1=ALU.add))
                link(nc.vector.tensor_reduce(best[:, k, :], work[:].rearrange("p e t -> p t e"), AX.X, ALU.max))
                link(nc.vector.tensor_tensor(equal[:], work[:], over_experts(best[:, k, :]), ALU.is_equal))
                link(nc.vector.memset(free[:, :], 1.0))
                for e in range(E):
                    link(nc.vector.tensor_tensor(chosen[:, k, e, :], equal[:, e, :], free[:, :], ALU.mult))
                    link(nc.vector.tensor_tensor(free[:, :], free[:, :], chosen[:, k, e, :], ALU.subtract))

            def prefix(turn):
                dve.wait_ge(prefix_ready, turn + 1)
                for x in halves:
                    part_ = slice(x * wide, (x + 1) * wide)
                    flat = [t[:].rearrange("p e t -> p (e t)")[:, part_] for t in (restart, run, place)]
                    link(nc.vector.tensor_tensor_scan(flat[1], flat[0], ps_tile[0:ROWS, x, 0:wide], 0.0,
                                                      ALU.mult, ALU.add))
                    link(nc.vector.tensor_tensor(flat[2], flat[1], ps_tile[0:ROWS, x, 0:wide], ALU.subtract))
                    link(nc.vector.tensor_tensor(flat[2], flat[2], ps_in[0:ROWS, x, 0:wide], ALU.add))

            if K == 2:
                nc.vector.tensor_tensor(lost[:, :], best[:, 1, :], best[:, 0, :], ALU.subtract).then_inc(gap_ready, 1)
                dve.wait_ge(exp_ready, 1)
                link(nc.vector.tensor_scalar(kept[:, :], ratio[:, :], 1.0, None, ALU.add))
                link(nc.vector.reciprocal(weights[:, 0, :], kept[:, :]))
                link(nc.vector.tensor_tensor(weights[:, 1, :], weights[:, 0, :], ratio[:, :], ALU.mult))
                link(nc.vector.tensor_scalar(spot[:, :], weights[:, 0, :], 0.5, None, ALU.max))
                link(nc.vector.tensor_tensor(score[:], chosen[:, 0, :, :], chosen[:, 1, :, :], ALU.add))
                link(nc.vector.tensor_tensor(score[:], score[:], over_experts(spot[:, :]), ALU.mult))
                link(nc.vector.memset(bar[:, :], 0.5))
                link(nc.vector.memset(step[:, :], 0.5))
                prime(dve, rounds_counted, *())
                start = count[0]
                with dve.Fori(0, BISECT) as r:
                    turn = r * 5 + start
                    nc.vector.tensor_scalar(cand[:, :], bar[:, :], step[:, 0:1], None, ALU.add).then_inc(dve_step, 1)
                    dve.wait_ge(dve_step, turn + 1)
                    nc.vector.tensor_tensor(flags[:], score[:], over_tiles(cand[:, :]), ALU.is_ge).then_inc(dve_step, 1)
                    dve.wait_ge(dve_step, turn + 2)
                    nc.vector.tensor_reduce(part[:, :], flags[:], AX.X, ALU.add).then_inc(rounds_counted.sem, 1)
                    dve.wait_ge(rounds_summed.sem, rounds_summed.now(r))
                    nc.vector.tensor_scalar(quota[:, :], ps_sum[0:ROWS, 0:E], float(CAP), step[:, 0:1],
                                            ALU.is_ge, ALU.mult).then_inc(dve_step, 1)
                    dve.wait_ge(dve_step, turn + 3)
                    nc.vector.tensor_tensor(bar[:, :], bar[:, :], quota[:, :], ALU.add).then_inc(dve_step, 1)
                    dve.wait_ge(dve_step, turn + 4)
                    nc.vector.tensor_scalar(step[:, :], step[:, :], 0.5, None, ALU.mult).then_inc(dve_step, 1)
                    dve.wait_ge(dve_step, turn + 5)
                count[0] = start + 5 * BISECT
                link(nc.vector.tensor_tensor(flags2[:], score[:], over_tiles(bar[:, :]), ALU.is_gt))
                nc.vector.tensor_reduce(part[:, :], flags2[:], AX.X, ALU.add).then_inc(rounds_counted.sem, 1)
                nc.vector.tensor_tensor(flags[:], score[:], over_tiles(bar[:, :]), ALU.is_equal).then_inc(flags_ready, 1)
                dve.wait_ge(rounds_summed.sem, rounds_summed.now(BISECT))
                link(nc.vector.tensor_scalar(quota[:, :], ps_sum[0:ROWS, 0:E], -1.0, float(CAP), ALU.mult, ALU.add))
                prefix(0)
                link(nc.vector.tensor_tensor(place[:], place[:], over_tiles(quota[:, :]), ALU.is_lt))
                link(nc.vector.tensor_tensor(place[:], place[:], flags[:], ALU.mult))
                nc.vector.tensor_tensor(keep[:], place[:], flags2[:], ALU.add).then_inc(flags_ready, 1)
            else:
                nc.vector.tensor_copy(keep[:], chosen[:, 0, :, :]).then_inc(flags_ready, 1)
            prefix(K - 1)
            totals = run[:, :, TILES - 1:TILES].to_broadcast([ROWS, E, 32])
            dve.wait_ge(loaded, 16 * 5)
            link(nc.vector.tensor_tensor(over[:], totals, steps[:, :].unsqueeze(1).to_broadcast([ROWS, E, 32]),
                                         ALU.is_gt))
            link(nc.vector.tensor_reduce(n_blocks[:, :], over[:], AX.X, ALU.add))
            link(nc.vector.tensor_copy(ends[:, 0:1], n_blocks[:, 0:1]))
            for e in range(1, E):
                link(nc.vector.tensor_tensor(ends[:, e:e + 1], ends[:, e - 1:e], n_blocks[:, e:e + 1], ALU.add))
            link(nc.vector.tensor_tensor(base[:, :], ends[:, :], n_blocks[:, :], ALU.subtract))
            link(nc.vector.tensor_scalar(base[:, :], base[:, :], float(COLS), None, ALU.mult))
            link(nc.vector.tensor_tensor(owner[:], numbers[:, 0:NB].unsqueeze(2).to_broadcast([ROWS, NB, E]),
                                         ends[:, :].unsqueeze(1).to_broadcast([ROWS, NB, E]), ALU.is_ge))
            link(nc.vector.tensor_reduce(kept[:, 0:NB], owner[:], AX.X, ALU.add))
            link(nc.vector.tensor_scalar(expert_of[:, 0:NB], kept[0:1, 0:NB], float(E - 1), None, ALU.min))
            link(nc.vector.tensor_tensor(place[:], place[:], over_tiles(base[:, :]), ALU.add))
            for k in range(K):
                link(nc.vector.tensor_tensor(flags[:], chosen[:, k, :, :], keep[:], ALU.mult))
                link(nc.vector.tensor_reduce(kept[:, :], flags[:].rearrange("p e t -> p t e"), AX.X, ALU.add))
                link(nc.vector.tensor_tensor(flags[:], flags[:], place[:], ALU.mult))
                link(nc.vector.tensor_reduce(spot[:, :], flags[:].rearrange("p e t -> p t e"), AX.X, ALU.add))
                if K == 2:
                    link(nc.vector.tensor_tensor(weights[:, k, :], weights[:, k, :], kept[:, :], ALU.mult))
                link(nc.vector.tensor_scalar(kept[:, :], kept[:, :], -1.0, 1.0, ALU.mult, ALU.add))
                link(nc.vector.scalar_tensor_tensor(out=slots_in[:, k, :], in0=kept[:, :], scalar=float(DROP),
                                                    in1=spot[:, :], op0=ALU.mult, op1=ALU.add))
                link(nc.vector.tensor_scalar(lost[:, :], token_of[:, :], float(DROP + k * TOKENS), None, ALU.add))
                link(nc.vector.tensor_tensor(lost[:, :], lost[:, :], kept[:, :], ALU.mult))
                link(nc.vector.tensor_tensor(slots_out[:, k, :], lost[:, :], spot[:, :], ALU.add))
            prime(dve, index_ready)
            for par in (0, 1):
                nc.vector.tensor_copy(index[:, par, :, :], slots_out[:, :, 4 * par:4 * par + 4]).then_inc(index_ready.sem, 1)
            with dve.Fori(1, PAIRS // 2) as ii:
                for par in (0, 1):
                    i = 2 * ii + par
                    dve.wait_ge(scattered[par].sem, scattered[par].before(ii))
                    nc.vector.tensor_copy(index[:, par, :, :], slots_out[:, :, bass.ds(i * 4, 4)]).then_inc(index_ready.sem, 1)

        @block.gpsimd
        def _(pool):
            pool.wait_ge(zeroed, 16 * (NB + 1))
            with pool.Fori(0, PAIRS // 2) as ii:
                for par in (0, 1):
                    i = 2 * ii + par
                    pool.wait_ge(rows_landed[par].sem, rows_landed[par].now(ii))
                    pool.wait_ge(index_ready.sem, index_ready.now(i))
                    pool.sem_inc(waited, 1)
                    for j in range(4):
                        for k in range(K):
                            pool.indirect_dma_start(
                                out=dram["moe_in" + T], in_=rows[:, par, j, :], in_offset=None,
                                out_offset=bass.IndirectOffsetOnAxis(ap=index[:, par, k, j:j + 1], axis=0),
                            ).then_inc(scattered[par].sem, 16)
            for par in (0, 1):
                pool.wait_ge(scattered[par].sem, scattered[par].now(PAIRS // 2 - 1))


def moe(nc, held, layer, dram, expert_of):
    NB = BLOCKS[layer]
    T = str(layer)
    E = EXPERTS[layer]
    KC = HID // 128
    with ExitStack() as ctx:
        def sb(name, shape, dt=F32):
            return ctx.enter_context(nc.sbuf_tensor(f"e{T}_{name}", shape, dt))

        def signal(name, per=1, unit=1):
            return Signal(nc, held, f"e{T}_{name}", per, unit)

        ident = sb("ident", [128, 128])
        w1 = sb("w1", [F, 2, 2, HID])
        w2 = sb("w2", [128, 2, KC, D])
        b1 = sb("b1", [128, 2, KC])
        b2 = sb("b2", [ROWS, 2, D])
        x_rows = sb("x_rows", [ROWS, 2, 4, D])
        x = sb("x", [F, 2, 2, COLS])
        hidden = sb("hidden", [128, KC, COLS])
        y = sb("y", [ROWS, 2, 4, D])
        ps_x = ctx.enter_context(nc.psum_tensor(f"e{T}_ps_x", [128, 2, BANK], F32))
        ps_h = ctx.enter_context(nc.psum_tensor(f"e{T}_ps_h", [128, 2, BANK], F32))
        ps_o = ctx.enter_context(nc.psum_tensor(f"e{T}_ps_o", [128, 4, BANK], F32))

        ident_landed = held.take(nc, f"e{T}_ident_landed")
        x_landed = [signal(f"x_landed_{p}", 1, 16) for p in (0, 1)]
        w_landed = [signal(f"w_landed_{p}", 4, 16) for p in (0, 1)]
        stored = [signal(f"stored_{p}", 1, 16) for p in (0, 1)]
        turned = signal("turned")
        x_done = signal("x_done")
        hid_proj = signal("hid_proj", KC)
        hid_done = signal("hid_done", KC)
        out_proj = signal("out_proj", 4)
        y_done = signal("y_done", 4)

        block = ctx.enter_context(nc.Block())

        def each_block(eng, body):
            with eng.Fori(0, NB // 2) as bb:
                for par in (0, 1):
                    body(bb, 2 * bb + par, par)
            if NB % 2:
                body(NB // 2, NB - 1, 0)

        @block.sync
        def _(sp):
            sp.dma_start(ident[:, :], dram["ident"]).then_inc(ident_landed, 16)
            prime(sp, *x_landed, *w_landed)

            def fetch(bb, b, par):
                sp.wait_ge(turned.sem, turned.before(b - 1) if not isinstance(b, int) or b >= 2 else turned.before(0))
                sp.dma_start(x_rows[:, par, :, :], dram["moe_in" + T][bass.ds(b * COLS, COLS), :].rearrange(
                    "(j p) d -> p j d", p=ROWS)).then_inc(x_landed[par].sem, 16)
                sp.wait_ge(y_done.sem, y_done.before(b - 1) if not isinstance(b, int) or b >= 2 else y_done.before(0))
                e = sp.value_load(expert_of[0:1, bass.ds(b, 1)], min_val=0, max_val=E - 1)
                for dst, src in ((w1[:, par, :, :].rearrange("p a b -> p (a b)"), dram["w1_" + T][bass.ds(e, 1), :, :]),
                                 (w2[:, par, :, :].rearrange("p a b -> p (a b)"), dram["w2_" + T][bass.ds(e, 1), :, :]),
                                 (b1[:, par, :], dram["b1_" + T][bass.ds(e, 1), :, :])):
                    sp.dma_start(dst, src.rearrange("a p n -> (a p) n")).then_inc(w_landed[par].sem, 16)
                sp.dma_start(b2[:, par, :], dram["b2_" + T][bass.ds(e, 1), :, :].rearrange(
                    "a p n -> (a p) n").to_broadcast([ROWS, D])).then_inc(w_landed[par].sem, 16)

            each_block(sp, fetch)

        @block.tensor
        def _(pe):
            prime(pe, turned, hid_proj, out_proj)
            pe.wait_ge(ident_landed, 16)

            def turn(bb, b, par):
                pe.wait_ge(x_landed[par].sem, x_landed[par].now(bb))
                pe.wait_ge(x_done.sem, x_done.before(b))
                for c in (0, 1):
                    for j in range(4):
                        mm = nc.tensor.transpose(ps_x[0:F, c, j * ROWS:(j + 1) * ROWS],
                                                 x_rows[:, par, j, c * F:(c + 1) * F], ident[0:ROWS, 0:ROWS])
                mm.then_inc(turned.sem, 1)

            def hidden_layer(bb, b, par):
                pe.wait_ge(w_landed[par].sem, w_landed[par].now(bb))
                pe.wait_ge(x_done.sem, x_done.now(b))
                for k in range(KC):
                    pe.wait_ge(hid_done.sem, hid_done.now(b, k - 1) if k >= 2 else hid_done.before(b, KC + k - 1))
                    for c in (0, 1):
                        mm = nc.tensor.matmul(ps_h[:, k % 2, 0:COLS], w1[:, par, c, k * 128:(k + 1) * 128],
                                              x[:, par, c, :], start=(c == 0), stop=(c == 1))
                    mm.then_inc(hid_proj.sem, 1)

            def output_layer(bb, b, par):
                pe.wait_ge(hid_done.sem, hid_done.now(b))
                for j in range(4):
                    pe.wait_ge(y_done.sem, y_done.before(b, j + 1))
                    for k in range(KC):
                        mm = nc.tensor.matmul(ps_o[0:ROWS, j, 0:D], hidden[:, k, j * ROWS:(j + 1) * ROWS],
                                              w2[:, par, k, :], start=(k == 0), stop=(k == KC - 1))
                    mm.then_inc(out_proj.sem, 1)

            turn(0, 0, 0)
            with pe.Fori(0, NB // 2) as bb:
                for par in (0, 1):
                    b = 2 * bb + par
                    hidden_layer(bb, b, par)
                    turn(bb + par, b + 1, 1 - par)
                    output_layer(bb, b, par)
            hidden_layer(NB // 2, NB - 1, 0)
            output_layer(NB // 2, NB - 1, 0)

        @block.scalar
        def _(act):
            prime(act, hid_done, *stored)

            def body(bb, b, par):
                act.wait_ge(w_landed[par].sem, w_landed[par].now(bb))
                act.wait_ge(out_proj.sem, out_proj.before(b))
                for k in range(KC):
                    act.wait_ge(hid_proj.sem, hid_proj.now(b, k + 1))
                    nc.scalar.activation(hidden[:, k, :], ps_h[:, k % 2, 0:COLS], ACT.Gelu,
                                         bias=b1[:, par, k:k + 1]).then_inc(hid_done.sem, 1)
                act.wait_ge(y_done.sem, y_done.now(b))
                act.dma_start(dram["moe_out" + T][bass.ds(b * COLS, COLS), :].rearrange("(j p) d -> p j d", p=ROWS),
                              y[:, par, :, :]).then_inc(stored[par].sem, 16)

            each_block(act, body)
            act.wait_ge(stored[0].sem, stored[0].now(NB // 2))
            act.wait_ge(stored[1].sem, stored[1].now(NB // 2 - 1))

        @block.vector
        def _(dve):
            prime(dve, x_done, y_done)

            def body(bb, b, par):
                dve.wait_ge(turned.sem, turned.now(b))
                nc.vector.tensor_copy(x[:, par, :, :], ps_x[0:F, :, 0:COLS]).then_inc(x_done.sem, 1)
                dve.wait_ge(w_landed[par].sem, w_landed[par].now(bb))
                dve.wait_ge(stored[par].sem, stored[par].before(bb))
                for j in range(4):
                    dve.wait_ge(out_proj.sem, out_proj.now(b, j + 1))
                    nc.vector.tensor_tensor(y[:, par, j, :], ps_o[0:ROWS, j, 0:D], b2[:, par, :],
                                            ALU.add).then_inc(y_done.sem, 1)

            each_block(dve, body)


def combine(nc, held, dram, slots_in, weights):
    with ExitStack() as ctx:
        def sb(name, shape, dt=F32):
            return ctx.enter_context(nc.sbuf_tensor(f"c_{name}", shape, dt))

        def by_parity(name, per=1, unit=1):
            return [Signal(nc, held, f"c_{name}_{p}", per, unit) for p in (0, 1)]

        h = sb("h", [ROWS, 2, 4, D])
        picked = sb("picked", [ROWS, 2, 2, 4, D])
        index = sb("index", [ROWS, 2, 2, 4], U32)
        share = sb("share", [ROWS, 2, 2, 4])
        h_landed = by_parity("h_landed", 1, 16)
        gathered = [Signal(nc, held, f"c_gathered_{p}", 8, 16, primed=False) for p in (0, 1)]
        index_done = by_parity("index_done", 2)
        added = by_parity("added", 8)
        stored = by_parity("stored", 1, 16)
        waited = held.take(nc, "c_waited")
        block = ctx.enter_context(nc.Block())

        def each_pair(eng, body):
            with eng.Fori(0, PAIRS // 2) as ii:
                for par in (0, 1):
                    body(ii, 2 * ii + par, par)

        @block.sync
        def _(sp):
            prime(sp, *h_landed)

            def body(ii, i, par):
                sp.wait_ge(stored[par].sem, stored[par].before(ii))
                sp.dma_start(h[:, par, :, :].rearrange("p a b -> p (a b)"), dram["h1"][i, :, :]).then_inc(h_landed[par].sem, 16)

            each_pair(sp, body)

        @block.gpsimd
        def _(pool):
            def body(ii, i, par):
                pool.wait_ge(index_done[par].sem, index_done[par].now(ii))
                pool.wait_ge(added[par].sem, added[par].before(ii))
                pool.sem_inc(waited, 1)
                for k in (0, 1):
                    for j in range(4):
                        pool.indirect_dma_start(
                            out=picked[:, par, k, j, :], out_offset=None, in_=dram["moe_out1"],
                            in_offset=bass.IndirectOffsetOnAxis(ap=index[:, par, k, j:j + 1], axis=0),
                        ).then_inc(gathered[par].sem, 16)

            each_pair(pool, body)

        @block.vector
        def _(dve):
            prime(dve, *index_done, *added)

            def indices(ii, i, par):
                nc.vector.tensor_copy(index[:, par, :, :], slots_in[:, :, bass.ds(i * 4, 4)]).then_inc(index_done[par].sem, 1)
                nc.vector.tensor_copy(share[:, par, :, :], weights[:, :, bass.ds(i * 4, 4)]).then_inc(index_done[par].sem, 1)

            def body(ii, i, par):
                indices(ii, i, par)
                dve.wait_ge(h_landed[par].sem, h_landed[par].now(ii))
                dve.wait_ge(gathered[par].sem, gathered[par].now(ii))
                dve.wait_ge(index_done[par].sem, index_done[par].now(ii))
                for k in (0, 1):
                    for j in range(4):
                        if k == 1:
                            dve.wait_ge(added[par].sem, added[par].now(ii, j + 1))
                        nc.vector.scalar_tensor_tensor(out=h[:, par, j, :], in0=picked[:, par, k, j, :],
                                                       scalar=share[:, par, k, j:j + 1], in1=h[:, par, j, :],
                                                       op0=ALU.mult, op1=ALU.add).then_inc(added[par].sem, 1)

            each_pair(dve, body)

        @block.scalar
        def _(act):
            prime(act, *stored)
            out = dram["out"].rearrange("m t d -> (m t) d").rearrange("(i j p) d -> i p j d", j=4, p=ROWS)

            def body(ii, i, par):
                act.wait_ge(added[par].sem, added[par].now(ii))
                act.dma_start(out[bass.ds(i, 1), :, :, :].rearrange("a p j d -> p (a j) d"), h[:, par, :, :]).then_inc(stored[par].sem, 16)

            each_pair(act, body)
            for par in (0, 1):
                act.wait_ge(stored[par].sem, stored[par].now(PAIRS // 2 - 1))


def bass_vit_tower(nc, dram):
    with ExitStack() as ctx:
        def sb(name, shape, dt=F32):
            return ctx.enter_context(nc.sbuf_tensor(name, shape, dt))

        logits = sb("logits", [ROWS, TILES, 8])
        slots_in = sb("slots_in", [ROWS, 2, TILES], U32)
        slots_out = sb("slots_out", [ROWS, 2, TILES], U32)
        weights = sb("weights", [ROWS, 2, TILES])
        expert_of = sb("expert_of", [1, BLOCKS[1]], I32)
        for layer in (0, 1):
            for stage in ("mamba", "route", "moe"):
                held = Semaphores()
                if stage == "mamba":
                    mamba(nc, held, layer, dram, logits, slots_in[:, 0, :], PAIRS)
                elif stage == "route":
                    route(nc, held, layer, dram, logits, slots_in[:, 0:TOP[layer], :],
                          slots_out[:, 0:TOP[layer], :], weights, expert_of)
                else:
                    moe(nc, held, layer, dram, expert_of)
                held.hand_back(nc)
        combine(nc, Semaphores(), dram, slots_in, weights)


def layouts(inp):
    import numpy as _np
    a = {k: _np.asarray(v) for k, v in inp.items()}
    out = {}

    def put(name, x):
        out[name] = _np.ascontiguousarray(x)

    def chunks(v, p):
        v = v.reshape((-1, p) + v.shape[1:])
        return v.transpose((1, 0) + tuple(range(2, v.ndim)))

    x = a["x"].reshape(PAIRS, 2, 3, GRID, 16, GRID, 16).transpose(0, 2, 4, 6, 1, 3, 5)
    put("x", x.reshape(PAIRS, 6, 128, COLS - 4).transpose(0, 2, 1, 3).reshape(PAIRS, 128, -1))
    put("tok_w", chunks(a["L0_tok_W"].T, 128))
    for n, k in (("tok_b", "L0_tok_b"), ("tok_g", "L0_tok_gamma"), ("tok_beta", "L0_tok_beta"),
                 ("conv_b", "L0_attn_conv_b"), ("dt_b0", "L0_attn_dt_b"), ("skip0", "L0_attn_D_param"),
                 ("ln_g0", "L0_attn_ln_g"), ("ln_b0", "L0_attn_ln_b"), ("ln_g1", "L1_attn_gamma"),
                 ("ln_b1", "L1_attn_beta"), ("a_log0", "L0_attn_A_log")):
        put(n, chunks(a[k], F))
    put("class_token", chunks(a["L0_tok_class_token"].reshape(D), F))
    put("cls_tok", chunks(a["cls_tok"].reshape(D), F))
    put("conv_w", chunks(a["L0_attn_conv_w"].reshape(D, 4), F))
    put("in_w0", chunks(a["L0_attn_in_proj_w"].T, F))
    put("dt_w0", chunks(a["L0_attn_dt_w"].T, F))
    put("bc_w0", chunks(_np.concatenate([a["L0_attn_B_w"], a["L0_attn_C_w"]]).T, F))
    put("out_w0", chunks(a["L0_attn_out_w"].T, F))
    put("gate_w0", chunks(a["L0_ffn_Wg"], F))
    put("gate_b0", _np.broadcast_to(a["L0_ffn_bg"], (ROWS, 4)))
    put("in_w1", chunks(a["L1_attn_W_in"], F))
    put("x_w1", chunks(a["L1_attn_W_x"], 128))
    put("dt_w1", a["L1_attn_W_dt"])
    put("out_w1", chunks(a["L1_attn_W_out"], 128))
    put("gate_w1", chunks(a["L1_ffn_Wg"], F))
    for n, k in (("dt_b1", "L1_attn_b_dt"), ("skip1", "L1_attn_D_skip"), ("a_log1", "L1_attn_A_log")):
        put(n, chunks(a[k], 128))
    for t, e in (("0", 4), ("1", 8)):
        put("w1_" + t, a[f"L{t}_ffn_W1"].reshape(e, 2, F, HID).transpose(0, 2, 1, 3).reshape(e, F, -1))
        put("w2_" + t, a[f"L{t}_ffn_W2"].reshape(e, 6, 128, D).transpose(0, 2, 1, 3).reshape(e, 128, -1))
        put("b1_" + t, a[f"L{t}_ffn_b1"].reshape(e, 6, 128).transpose(0, 2, 1))
        put("b2_" + t, a[f"L{t}_ffn_b2"].reshape(e, 1, D))
    return out


def shape_constants():
    import numpy as _np
    from concourse import mybir as _mybir
    f32 = _np.float32
    out = {"ident": _np.eye(128, dtype=f32), "avg": _np.full((F, F), 1.0 / D, f32)}
    sel = _np.zeros((96, 32, 128), f32)
    sel[_np.arange(96), _np.arange(96) % 32, :] = 1.0
    out["select"] = sel.astype(_mybir.dt.np(BF16))
    i = _np.arange(SEQ - 1, dtype=f32)[:, None]
    j = _np.arange(D, dtype=f32)[None, :]
    angle = i / _np.power(f32(10000.0), (_np.floor(j / f32(2.0)) * f32(2.0) / f32(D)).astype(f32))
    pos = _np.where(_np.arange(D)[None, :] % 2 == 0, _np.sin(angle), _np.cos(angle)).astype(f32)
    out["pos"] = pos.T.reshape(2, F, SEQ - 1).transpose(1, 0, 2)
    out["earlier"] = _np.triu(_np.ones((ROWS, ROWS), f32), 1)
    out["ones"] = _np.ones((ROWS, ROWS), f32)
    out["steps"] = _np.broadcast_to(_np.arange(32, dtype=f32) * COLS, (ROWS, 32))
    out["numbers"] = _np.broadcast_to(_np.arange(BLOCKS[1], dtype=f32), (ROWS, BLOCKS[1]))
    out["token_of"] = _np.arange(TILES, dtype=f32)[None, :] * ROWS + _np.arange(ROWS, dtype=f32)[:, None]
    return {k: _np.ascontiguousarray(v) for k, v in out.items()}


DEBUG = 1


def kernel(**inputs):
    import numpy as _np
    import concourse.bacc as _bacc
    from concourse import mybir as _mybir
    from concourse.bass_utils import run_bass_kernel_spmd as _run

    nc = _bacc.Bacc("TRN2", target_bir_lowering=False, num_devices=1)
    arrays, dram = {}, {}
    for name, v in (layouts(inputs) | shape_constants()).items():
        arrays["in_" + name] = v
        t = nc.dram_tensor("in_" + name, v.shape, _mybir.dt.from_np(v.dtype), kind="ExternalInput").ap()
        if name not in ("x", "w1_0", "w1_1", "w2_0", "w2_1", "b1_0", "b1_1", "b2_0", "b2_1") and len(v.shape) > 2:
            t = t.rearrange("p a b -> p (a b)")
        dram[name] = t
    kind = "ExternalOutput" if DEBUG else "Internal"
    scratch = {"h0": (PAIRS, F, 2 * COLS), "h1": (PAIRS, ROWS, 4 * D)}
    for t in (0, 1):
        scratch[f"xf{t}"] = (PAIRS, ROWS, 4 * D)
        scratch[f"moe_in{t}"] = (BLOCKS[t] * COLS + TOP[t] * TOKENS, D)
        scratch[f"moe_out{t}"] = (BLOCKS[t] * COLS + 1, D)
    for name, shape in scratch.items():
        k = kind if name in ("h0", "h1", "xf0", "xf1") else "Internal"
        dram[name] = nc.dram_tensor(name, shape, F32, kind=k).ap()
    dram["out"] = nc.dram_tensor("out_0", (IMAGES, SEQ, D), F32, kind="ExternalOutput").ap()
    bass_vit_tower(nc, dram)
    r = _run(nc, [arrays], core_ids=[0])
    return r.results[0]["out_0"]
```

```python
from contextlib import ExitStack

import numpy as np

import concourse.bass as bass
from concourse import mybir

F32 = mybir.dt.float32
BF16 = mybir.dt.bfloat16
I32 = mybir.dt.int32
U32 = mybir.dt.uint32
ALU = mybir.AluOpType
ACT = mybir.ActivationFunctionType
AX = mybir.AxisListType

IMAGES = 64
GRID = 14
PATCH_K = 768
SEQ = GRID * GRID + 2
PAIRS = IMAGES // 2
COLS = 2 * SEQ
ROWS = COLS // 4
TILES = PAIRS * 4
TOKENS = IMAGES * SEQ
D = 192
F = D // 2
N_STATE = 16
HID = 768
EPS = 1e-5
BANK = 512
CAP = int(1.25 * TOKENS * 2 / 8)


class Semaphores:

    def __init__(self):
        self.taken = []

    def take(self, nc, name):
        self.taken.append(nc.alloc_semaphore(name=name))
        return self.taken[-1]

    def hand_back(self, nc):
        nc.clear_and_free_semaphores(self.taken)
        nc.all_engine_barrier()


class Signal:

    def __init__(self, nc, held, name, per=1, unit=1, primed=True):
        self.sem = held.take(nc, name)
        self.per, self.unit, self.ahead = per, unit, int(primed)

    def now(self, i, k=None):
        return (i + self.ahead) * (self.per * self.unit) + (self.per if k is None else k) * self.unit

    def before(self, i, k=None):
        return (i - 1 + self.ahead) * (self.per * self.unit) + (self.per if k is None else k) * self.unit


def prime(eng, *signals):
    for s in signals:
        eng.sem_inc(s.sem, s.per * s.unit)


class Norm:

    def __init__(self, nc, held, name):
        self.mean = Signal(nc, held, name + "_mean")
        self.centred = Signal(nc, held, name + "_centred")
        self.square = Signal(nc, held, name + "_square")
        self.var = Signal(nc, held, name + "_var")
        self.log = Signal(nc, held, name + "_log")
        self.rstd = Signal(nc, held, name + "_rstd")


def load_all(sp, loads, sem):
    for dst, src in loads:
        sp.dma_start(dst, src).then_inc(sem, 16)
    return 16 * len(loads)


def mamba(nc, held, layer, dram, logits, slots, pairs):
    first = layer == 0
    P, C = (96, 2) if first else (128, 3)
    E = 4 if first else 8
    RING = 3
    T = str(layer)
    with ExitStack() as ctx:
        def sb(name, shape, dt=F32):
            return ctx.enter_context(nc.sbuf_tensor(f"m{T}_{name}", shape, dt))

        def ps(name, shape):
            return ctx.enter_context(nc.psum_tensor(f"m{T}_ps_{name}", shape, F32))

        def signal(name, per=1, unit=1):
            return Signal(nc, held, f"m{T}_{name}", per, unit)

        loads = []

        def const(name, key, shape, dt=F32):
            t = sb(name, shape, dt)
            flat = t[:] if len(shape) == 2 else t[:].rearrange(
                "p a b -> p (a b)" if len(shape) == 3 else "p a b c -> p (a b c)")
            loads.append((flat, dram[key]))
            return t

        ident = const("ident", "ident", [128, 128])
        select = const("select", "select", [96, 32, 128], BF16)
        avg = const("avg", "avg", [F, F])
        gate_w = const("gate_w", f"gate_w{T}", [F, 2, E])
        a_log = const("a_log", f"a_log{T}", [P, C, N_STATE])
        skip_w = const("skip_w", f"skip{T}", [P, C])
        dt_bias = const("dt_bias", f"dt_b{T}", [P, C])
        ln_g = const("ln_g", f"ln_g{T}", [F, 2])
        ln_b = const("ln_b", f"ln_b{T}", [F, 2])
        out_w = const("out_w", f"out_w{T}", [P, C, D])
        in_w = const("in_w", f"in_w{T}", [F, 2, 2 * P * C])
        if first:
            tok_w = const("tok_w", "tok_w", [128, 6, D])
            tok_b = const("tok_b", "tok_b", [F, 2])
            tok_g = const("tok_g", "tok_g", [F, 2])
            tok_beta = const("tok_beta", "tok_beta", [F, 2])
            class_token = const("class_token", "class_token", [F, 2])
            cls_tok = const("cls_tok", "cls_tok", [F, 2])
            pos = const("pos", "pos", [F, 2, SEQ - 1])
            conv_w = const("conv_w", "conv_w", [F, 2, 4])
            conv_b = const("conv_b", "conv_b", [F, 2])
            dt_w = const("dt_w", "dt_w0", [F, 2, D])
            bc_w = const("bc_w", "bc_w0", [F, 2, 32])
            gate_b = const("gate_b", "gate_b0", [ROWS, E])
        else:
            x_w = const("x_w", "x_w1", [P, C, 80])
            dt_w = const("dt_w", "dt_w1", [48, P * C])
        n_loads = 16 * len(loads)
        eps = sb("eps", [128, 1])
        a_neg = sb("a_neg", [P, C, N_STATE])

        if first:
            patches = sb("patches", [128, 2, 6, COLS - 4])
            emb = sb("emb", [F, 2, 2, SEQ])
            cls_emb = sb("cls_emb", [F, 2, 2, 2])
            x_pad = sb("x_pad", [F, 2, 2, SEQ + 3])
            conv = sb("conv", [F, 2, 2, SEQ])
        else:
            gathered = sb("gathered", [ROWS, 4, D])
            slot_ix = sb("slot_ix", [ROWS, 4], U32)
            low_rank = sb("low_rank", [48, COLS])
        h = sb("h", [F, 2, 2, COLS])
        xn = sb("xn", [F, 2, 2, COLS])
        cen = sb("cen", [F, 2, COLS])
        sq = sb("sq", [F, 2, COLS])
        logv = sb("logv", [F, COLS])
        rstd = sb("rstd", [F, COLS])
        u = sb("u", [P, 2, C, COLS])
        sz = sb("sz", [P, 2, C, COLS])
        sp_abs = sb("sp_abs", [P, C, COLS])
        sp_exp = sb("sp_exp", [P, C, COLS])
        sp_one = sb("sp_one", [P, C, COLS])
        sp_raw = sb("sp_raw", [P, C, COLS])
        dt = sb("dt", [P, 2, C, COLS])
        du = sb("du", [P, 2, C, COLS])
        bc_stack = sb("bc_stack", [96, 2, COLS], BF16)
        bc_rest = sb("bc_rest", [32, COLS])
        bc_mid = sb("bc_mid", [32, COLS], BF16)
        c_sb = sb("c_sb", [P, RING, COLS])
        decay = sb("decay", [P, RING, C, COLS])
        drive = sb("drive", [P, 2, C, COLS])
        state = sb("state", [P, RING, C, COLS])
        state_c = sb("state_c", [P, RING, C, COLS])
        y = sb("y", [P, C, COLS])
        r = sb("r", [F, 2, COLS])
        cen2 = sb("cen2", [F, 2, COLS])
        sq2 = sb("sq2", [F, 2, COLS])
        logv2 = sb("logv2", [F, COLS])
        rstd2 = sb("rstd2", [F, COLS])
        normed = sb("normed", [F, 2, COLS])
        h_out = sb("h_out", [F, 2, COLS])
        h_keep = sb("h_keep", [F, 2, COLS])
        xf = sb("xf", [F, 2, COLS])
        rows = sb("rows", [ROWS, 4, D])
        rows_h = None if first else sb("rows_h", [ROWS, 4, D])

        ps_y = ps("y", [128, C, BANK])
        ps_b = ps("b", [128, BANK])
        ps_c = ps("c", [128, BANK])
        ps_f = ps("f", [128, 2, BANK])
        ps_k = ps("k", [128, BANK])

        loaded = held.take(nc, f"m{T}_loaded")
        ready = held.take(nc, f"m{T}_ready")
        waited = held.take(nc, f"m{T}_waited")
        in_landed = [signal(f"in_landed_{p}", 1, 16) for p in (0, 1)]
        norms = {k: Norm(nc, held, f"m{T}_{k}") for k in (["tok"] if first else []) + ["pre", "post", "ffn"]}
        setup = held.take(nc, f"m{T}_setup")
        if first:
            tok_done = signal("tok_done")
            emb_cls = signal("emb_cls")
            emb_done = signal("emb_done")
            tok_scaled = signal("tok_scaled")
            h_done = signal("h_done", 2)
            x_proj = signal("x_proj")
            pad_done = signal("pad_done")
            z_proj = signal("z_proj")
            z_copied = signal("z_copied")
            conv_done = signal("conv_done", 8)
        else:
            ix_done = signal("ix_done")
            gather_landed = Signal(nc, held, f"m{T}_gather_landed", 4, 16, primed=False)
            turned = signal("turned")
            h_done = signal("h_done")
            rank_proj = signal("rank_proj")
            rank_copied = signal("rank_copied")
            xz_proj = signal("xz_proj", 2 * C)
            xz_copied = signal("xz_copied", 2 * C)
        xn_done = signal("xn_done")
        h_kept = signal("h_kept")
        u_done = signal("u_done", 2 if first else 1)
        z_done = signal("z_done")
        dt_proj = signal("dt_proj", C)
        bc_proj = signal("bc_proj")
        raw_done = signal("raw_done", C)
        abs_done = signal("abs_done")
        exp_done = signal("exp_done")
        one_done = signal("one_done")
        log_done = signal("log_done")
        corr_done = signal("corr_done")
        sum_done = signal("sum_done")
        dt_done = signal("dt_done")
        du_done = signal("du_done")
        bc_hi = signal("bc_hi")
        bc_r1 = signal("bc_r1")
        bc_m = signal("bc_m", 2)
        bc_lo = signal("bc_lo")
        b_spread = signal("b_spread", N_STATE)
        c_spread = signal("c_spread", N_STATE)
        c_copied = signal("c_copied", N_STATE)
        decayed = signal("decayed", N_STATE * C)
        driven = signal("driven", N_STATE)
        scanned = signal("scanned", N_STATE)
        weighed = signal("weighed", N_STATE)
        summed = signal("summed", N_STATE)
        skip_done = signal("skip_done", C)
        y_done = signal("y_done")
        out_proj = signal("out_proj", 2)
        r_done = signal("r_done", 2)
        r_scaled = signal("r_scaled")
        affine = signal("affine", 2)
        h_out_done = signal("h_out_done")
        xf_done = signal("xf_done")
        n_turn = 2 if first else 4
        turn_slot = 12 if first else 11
        rows_turned = signal("rows_turned", n_turn)
        rows_done = signal("rows_done", n_turn)
        gate_proj = signal("gate_proj")
        gate_done = signal("gate_done")
        stored = signal("stored", 2, 16)

        block = ctx.enter_context(nc.Block())
        half = range(2)

        def ring(n):
            return n % RING if n < N_STATE - 1 else 1

        def ring_free(sig, i, n):
            if n < RING:
                return sig.before(i, max(m for m in range(N_STATE) if ring(m) == n) + 1)
            return sig.now(i, max(m for m in range(n) if ring(m) == ring(n)) + 1)

        def all_turns(turn, front_alone, back_alone):

            def run(eng):
                front_alone()
                turn(0, 0, 0, True, False)
                with eng.Fori(0, (pairs - 2) // 2) as jj:
                    for q in (0, 1):
                        turn(2 * jj + 1 + q, (1 + q) % 2, jj + 1, True, True)
                turn(pairs - 1, (pairs - 1) % 2, 0, False, True)
                back_alone()

            return run

        @block.sync
        def _(sp):
            load_all(sp, loads, loaded)
            prime(sp, *in_landed)

            def fetch(i, par):
                if first:
                    sp.dma_start(patches[:, par, :, :].rearrange("p a b -> p (a b)"),
                                 dram["x"][i, :, :]).then_inc(in_landed[par].sem, 16)
                else:
                    sp.dma_start(h[:, par, :, :].rearrange("p a b -> p (a b)"),
                                 dram["h0"][i, :, :]).then_inc(in_landed[par].sem, 16)

            fetch(0, 0)
            fetch(1, 1)
            with sp.Fori(0, pairs // 2 - 1) as ii:
                for par in half:
                    if first:
                        sp.wait_ge(tok_done.sem, tok_done.now(2 * ii + par))
                    else:
                        sp.wait_ge(h_kept.sem, h_kept.now(2 * ii + par))
                    fetch(2 * ii + par + 2, par)

        @block.tensor
        def _(pe):
            pe.wait_ge(loaded, n_loads)
            pe.wait_ge(ready, 3)
            prime(pe, dt_proj, bc_proj, b_spread, c_spread, summed, out_proj, rows_turned, gate_proj,
                  *(n.mean for n in norms.values()), *(n.var for n in norms.values()))
            if first:
                prime(pe, tok_done, x_proj, z_proj)
            else:
                prime(pe, turned, rank_proj, xz_proj)

            def average(src, bank, sig):
                for c in half:
                    mm = nc.tensor.matmul(bank[0:F, 0:COLS], avg[:, :], src[:, c, :], start=(c == 0), stop=(c == 1))
                mm.then_inc(sig.sem, 1)

            def project(bank, m0, m1, weights, src, k):
                for c in range(k):
                    mm = nc.tensor.matmul(bank[0:m1 - m0, 0:COLS], weights[:, c, m0:m1], src[:, c, :],
                                          start=(c == 0), stop=(c == k - 1))
                return mm

            def embed(i, par, ih, c):
                if c == 0:
                    pe.wait_ge(in_landed[par].sem, in_landed[par].now(ih))
                    pe.wait_ge(bc_hi.sem, bc_hi.before(i))
                    pe.wait_ge(bc_r1.sem, bc_r1.before(i))
                    pe.wait_ge(raw_done.sem, raw_done.before(i))
                for k in range(6):
                    mm = nc.tensor.matmul(ps_f[0:F, c, 0:COLS - 4], tok_w[:, k, c * F:(c + 1) * F],
                                          patches[:, par, k, :], start=(k == 0), stop=(k == 5))
                if c == 1:
                    mm.then_inc(tok_done.sem, 1)

            def turn_moe_rows(i):
                pe.wait_ge(gather_landed.sem, gather_landed.now(i))
                pe.wait_ge(raw_done.sem, raw_done.before(i))
                for c in half:
                    for j in range(4):
                        mm = nc.tensor.transpose(ps_f[0:F, c, j * ROWS:(j + 1) * ROWS],
                                                 gathered[:, j, c * F:(c + 1) * F], ident[0:ROWS, 0:ROWS])
                mm.then_inc(turned.sem, 1)

            def pre_mean(i, par):
                pe.wait_ge(h_done.sem, h_done.now(i))
                average(h[:, par, :, :], ps_f[:, 0, :], norms["pre"].mean)

            def front_var(i, name):
                n = norms[name]
                pe.wait_ge(n.square.sem, n.square.now(i))
                average(sq, ps_f[:, 1, :], n.var)

            def project_both(i, par, sig):
                for c in half:
                    m = (c if sig is x_proj else C + c) * P
                    mm = project(ps_f[:, c, :], m, m + P, in_w, xn[:, par, :, :], 2)
                mm.then_inc(sig.sem, 1)

            def project_xz(i, par, q):
                if q >= 2:
                    pe.wait_ge(xz_copied.sem, xz_copied.now(i, q - 1))
                project(ps_f[:, q % 2, :], q * P, (q + 1) * P, in_w, xn[:, par, :, :], 2).then_inc(xz_proj.sem, 1)

            def front(i, par, ih, n):
                if first:
                    if n == 0:
                        embed(i, par, ih, 0)
                    if n == 1:
                        embed(i, par, ih, 1)
                    if n == 3:
                        pe.wait_ge(emb_done.sem, emb_done.now(i))
                        average(emb[:].rearrange("p c m t -> p c (m t)"), ps_f[:, 0, :], norms["tok"].mean)
                    if n == 4:
                        front_var(i, "tok")
                    if n == 6:
                        pre_mean(i, par)
                    if n == 7:
                        front_var(i, "pre")
                    if n == 9:
                        pe.wait_ge(xn_done.sem, xn_done.now(i))
                        project_both(i, par, x_proj)
                    if n == 10:
                        pe.wait_ge(pad_done.sem, pad_done.now(i))
                        project_both(i, par, z_proj)
                    if n == 12:
                        pe.wait_ge(z_copied.sem, z_copied.now(i))
                        pe.wait_ge(u_done.sem, u_done.now(i))
                        for c in half:
                            project(ps_f[:, c, :], c * P, (c + 1) * P, dt_w, u[:, par, :, :], C).then_inc(dt_proj.sem, 1)
                    if n == 13:
                        pe.wait_ge(raw_done.sem, raw_done.now(i, 1))
                        project(ps_f[:, 0, :], 0, 32, bc_w, u[:, par, :, :], C).then_inc(bc_proj.sem, 1)
                else:
                    if n == 2:
                        turn_moe_rows(i)
                    if n == 4:
                        pre_mean(i, par)
                    if n == 5:
                        front_var(i, "pre")
                    if n == 7:
                        pe.wait_ge(xn_done.sem, xn_done.now(i))
                    if n in (7, 8, 9):
                        project_xz(i, par, 2 * (n - 7))
                        project_xz(i, par, 2 * (n - 7) + 1)
                    if n == 11:
                        pe.wait_ge(xz_copied.sem, xz_copied.now(i))
                        pe.wait_ge(u_done.sem, u_done.now(i))
                        project(ps_f[:, 0, :], 0, 48, x_w, u[:, par, :, :], C).then_inc(rank_proj.sem, 1)
                        project(ps_f[:, 1, :], 48, 80, x_w, u[:, par, :, :], C).then_inc(bc_proj.sem, 1)
                    if n in (12, 13):
                        for c in ((0, 1) if n == 12 else (2,)):
                            if c == 0:
                                pe.wait_ge(rank_copied.sem, rank_copied.now(i))
                            if c == 1:
                                pe.wait_ge(bc_hi.sem, bc_hi.now(i))
                                pe.wait_ge(bc_r1.sem, bc_r1.now(i))
                            if c == 2:
                                pe.wait_ge(raw_done.sem, raw_done.now(i, 1))
                            nc.tensor.matmul(ps_f[0:P, c % 2, 0:COLS], dt_w[:, c * P:(c + 1) * P], low_rank[:, :],
                                             start=True, stop=True).then_inc(dt_proj.sem, 1)

            def sum_states(i, n):
                pe.wait_ge(weighed.sem, weighed.now(i, n + 1))
                if n == 0:
                    pe.wait_ge(skip_done.sem, skip_done.before(i))
                for c in range(C):
                    mm = nc.tensor.matmul(ps_y[0:P, c, 0:COLS], ident[0:P, 0:P], state_c[:, ring(n), c, :],
                                          start=(n == 0), stop=(n == N_STATE - 1))
                mm.then_inc(summed.sem, 1)

            def scan(i, par, n, has_back):
                if n == 0:
                    pe.wait_ge(bc_lo.sem, bc_lo.now(i))
                    pe.wait_ge(bc_m.sem, bc_m.now(i))
                pe.wait_ge(driven.sem, driven.now(i, n) if n else driven.before(i))
                nc.tensor.matmul(ps_b[0:P, 0:COLS], select[:, n, 0:P], bc_stack[:, par, :],
                                 start=True, stop=True).then_inc(b_spread.sem, 1)
                pe.wait_ge(c_copied.sem, c_copied.now(i, n) if n else c_copied.before(i))
                nc.tensor.matmul(ps_c[0:P, 0:COLS], select[:, N_STATE + n, 0:P], bc_stack[:, par, :],
                                 start=True, stop=True).then_inc(c_spread.sem, 1)
                if n >= 2:
                    sum_states(i, n - 2)
                elif has_back:
                    sum_states(i - 1, N_STATE - 2 + n)

            def back(i, n):
                if n in (3, 4):
                    c = n - 3
                    if c == 0:
                        pe.wait_ge(y_done.sem, y_done.now(i))
                        pe.wait_ge(gate_done.sem, gate_done.before(i))
                    else:
                        pe.wait_ge(r_done.sem, r_done.now(i, 1))
                    project(ps_k, c * F, (c + 1) * F, out_w, y, C).then_inc(out_proj.sem, 1)
                if n == 5:
                    pe.wait_ge(r_done.sem, r_done.now(i))
                    average(r, ps_k, norms["post"].mean)
                if n == 9:
                    pe.wait_ge(h_out_done.sem, h_out_done.now(i))
                    average(h_out, ps_k, norms["ffn"].mean)
                if n in (6, 10):
                    nm = norms["post" if n == 6 else "ffn"]
                    pe.wait_ge(nm.square.sem, nm.square.now(i))
                    average(sq2, ps_k, nm.var)
                t = n - turn_slot
                if 0 <= t < n_turn:
                    src = xf if t >= n_turn - 2 else h_out
                    if t == 0:
                        pe.wait_ge(norms["ffn"].log.sem, norms["ffn"].log.now(i))
                    else:
                        pe.wait_ge(rows_done.sem, rows_done.now(i, t))
                    if t == n_turn - 2:
                        pe.wait_ge(xf_done.sem, xf_done.now(i))
                    for j in half:
                        for c in half:
                            a = (2 * (t % 2) + j) * ROWS
                            mm = nc.tensor.transpose(ps_k[0:ROWS, j * D + c * F:j * D + (c + 1) * F],
                                                     src[:, c, a:a + ROWS], ident[0:F, 0:F])
                    mm.then_inc(rows_turned.sem, 1)
                if t == n_turn:
                    pe.wait_ge(rows_done.sem, rows_done.now(i))
                    for j in range(4):
                        for c in half:
                            mm = nc.tensor.matmul(ps_k[0:ROWS, j * E:(j + 1) * E], xf[:, c, j * ROWS:(j + 1) * ROWS],
                                                  gate_w[:, c, :], start=(c == 0), stop=(c == 1))
                    mm.then_inc(gate_proj.sem, 1)

            def front_alone():
                for n in range(N_STATE):
                    front(0, 0, 0, n)

            def turn(i, par, fh, has_front, has_back):
                for n in range(N_STATE):
                    scan(i, par, n, has_back)
                    if has_back:
                        back(i - 1, n)
                    if has_front:
                        front(i + 1, 1 - par, fh, n)

            def back_alone():
                for n in range(N_STATE):
                    if n < 2:
                        sum_states(pairs - 1, N_STATE - 2 + n)
                    back(pairs - 1, n)

            all_turns(turn, front_alone, back_alone)(pe)

        @block.scalar
        def _(act):
            act.wait_ge(loaded, n_loads)
            act.wait_ge(ready, 1)
            prime(act, u_done, z_done, raw_done, abs_done, exp_done, log_done, bc_hi, bc_m, c_copied, decayed, affine,
                  rows_done, stored, *(n.square for n in norms.values()), *(n.log for n in norms.values()),
                  *(n.rstd for n in norms.values()))
            if first:
                prime(act, h_done, pad_done, z_copied)
            else:
                prime(act, rank_copied, xz_copied)
            act.preload_act_table_set("natural_log_exp_and_others")
            nc.scalar.activation(a_neg[:].rearrange("p a b -> p (a b)"), a_log[:].rearrange("p a b -> p (a b)"),
                                 ACT.Exp).then_inc(ready, 1)
            act.wait_ge(ready, 3)

            def square(i, n, cen, sq):
                act.wait_ge(n.centred.sem, n.centred.now(i))
                nc.scalar.activation(sq[:], cen[:], ACT.Square).then_inc(n.square.sem, 1)

            def inverse_std(i, n, logv, rstd, bank):
                act.wait_ge(n.var.sem, n.var.now(i))
                nc.scalar.activation(logv[:, :], bank[0:F, 0:COLS], ACT.Ln, bias=eps[0:F, :]).then_inc(n.log.sem, 1)
                act.wait_ge(n.log.sem, n.log.now(i))
                nc.scalar.activation(rstd[:, :], logv[:, :], ACT.Exp, scale=-0.5).then_inc(n.rstd.sem, 1)

            def raw_dt(i, c):
                act.wait_ge(dt_proj.sem, dt_proj.now(i, c + 1))
                if c == 0:
                    act.wait_ge(dt_done.sem, dt_done.before(i))
                nc.scalar.activation(sp_raw[:, c, :], ps_f[0:P, c % 2, 0:COLS], ACT.Identity,
                                     bias=dt_bias[:, c:c + 1]).then_inc(raw_done.sem, 1)

            def split_hi(i, par, bank):
                act.wait_ge(bc_proj.sem, bc_proj.now(i))
                nc.scalar.activation(bc_stack[0:32, par, :], ps_f[0:32, bank, 0:COLS], ACT.Copy).then_inc(bc_hi.sem, 1)

            def soft_exp(i):
                act.wait_ge(raw_done.sem, raw_done.now(i))
                nc.scalar.activation(sp_abs[:], sp_raw[:], ACT.Abs).then_inc(abs_done.sem, 1)
                act.wait_ge(abs_done.sem, abs_done.now(i))
                act.wait_ge(sum_done.sem, sum_done.before(i))
                nc.scalar.activation(sp_exp[:], sp_abs[:], ACT.Exp, scale=-1.0).then_inc(exp_done.sem, 1)

            def soft_log(i, par):
                act.preload_act_table_set("natural_log")
                act.wait_ge(one_done.sem, one_done.now(i))
                act.wait_ge(exp_done.sem, exp_done.now(i))
                nc.scalar.activation(sp_abs[:], sp_one[:], ACT.Ln).then_inc(log_done.sem, 1)
                act.preload_act_table_set("natural_log_exp_and_others")
                act.wait_ge(bc_r1.sem, bc_r1.now(i))
                nc.scalar.activation(bc_mid[:, :], bc_rest[:, :], ACT.Copy).then_inc(bc_m.sem, 1)
                nc.scalar.activation(bc_stack[32:64, par, :], bc_rest[:, :], ACT.Copy).then_inc(bc_m.sem, 1)

            def front(i, par, n):
                pre = norms["pre"]
                if first:
                    if n == 3:
                        square(i, norms["tok"], cen, sq)
                    if n == 4:
                        inverse_std(i, norms["tok"], logv, rstd, ps_f[:, 1, :])
                    if n == 5:
                        act.wait_ge(tok_scaled.sem, tok_scaled.now(i))
                        act.wait_ge(h_kept.sem, h_kept.before(i - 1))
                        for c in half:
                            nc.scalar.activation(
                                h[:, par, c, :].rearrange("p (m t) -> p m t", m=2)[:, :, 1:SEQ],
                                emb[:, c, :, 1:SEQ], ACT.Identity, bias=tok_beta[:, c:c + 1],
                                scale=tok_g[:, c:c + 1]).then_inc(h_done.sem, 1)
                    if n == 6:
                        square(i, pre, cen, sq)
                    if n == 7:
                        inverse_std(i, pre, logv, rstd, ps_f[:, 1, :])
                    if n == 9:
                        act.wait_ge(x_proj.sem, x_proj.now(i))
                        act.wait_ge(conv_done.sem, conv_done.before(i))
                        nc.scalar.activation(x_pad[:, :, :, 3:], ps_f[0:F, :, 0:COLS].rearrange(
                            "p c (m t) -> p c m t", m=2), ACT.Copy).then_inc(pad_done.sem, 1)
                    if n == 10:
                        act.wait_ge(z_proj.sem, z_proj.now(i))
                        nc.scalar.activation(sz[:, par, :, :], ps_f[0:P, :, 0:COLS], ACT.Copy).then_inc(z_copied.sem, 1)
                    if n == 11:
                        act.wait_ge(z_copied.sem, z_copied.now(i))
                        nc.scalar.activation(sz[:, par, :, :], sz[:, par, :, :], ACT.Silu).then_inc(z_done.sem, 1)
                        for c in range(C):
                            act.wait_ge(conv_done.sem, conv_done.now(i, 4 * c + 4))
                            nc.scalar.activation(u[:, par, c, :], conv[:, c, :, :].rearrange("p m t -> p (m t)"),
                                                 ACT.Silu, bias=conv_b[:, c:c + 1]).then_inc(u_done.sem, 1)
                        act.preload_act_table_set("natural_log_exp_and_others")
                    if n == 12:
                        raw_dt(i, 0)
                        raw_dt(i, 1)
                    if n == 13:
                        split_hi(i, par, 0)
                        soft_exp(i)
                else:
                    if n == 4:
                        square(i, pre, cen, sq)
                    if n == 5:
                        inverse_std(i, pre, logv, rstd, ps_f[:, 1, :])
                    if n in (7, 8, 9):
                        for q in (2 * (n - 7), 2 * (n - 7) + 1):
                            act.wait_ge(xz_proj.sem, xz_proj.now(i, q + 1))
                            dst = u if q < C else sz
                            nc.scalar.activation(dst[:, par, q % C, :], ps_f[0:P, q % 2, 0:COLS],
                                                 ACT.Copy).then_inc(xz_copied.sem, 1)
                    if n == 10:
                        act.wait_ge(xz_copied.sem, xz_copied.now(i))
                        nc.scalar.activation(u[:, par, :, :], u[:, par, :, :], ACT.Silu).then_inc(u_done.sem, 1)
                        nc.scalar.activation(sz[:, par, :, :], sz[:, par, :, :], ACT.Silu).then_inc(z_done.sem, 1)
                        act.preload_act_table_set("natural_log_exp_and_others")
                    if n == 11:
                        act.wait_ge(rank_proj.sem, rank_proj.now(i))
                        nc.scalar.activation(low_rank[:, :], ps_f[0:48, 0, 0:COLS], ACT.Copy).then_inc(rank_copied.sem, 1)
                        split_hi(i, par, 1)
                    if n == 12:
                        raw_dt(i, 0)
                        raw_dt(i, 1)
                    if n == 13:
                        raw_dt(i, 2)
                        soft_exp(i)
                if n == 14:
                    soft_log(i, par)

            def scan(i, par, n):
                if n == 0:
                    act.wait_ge(dt_done.sem, dt_done.now(i))
                act.wait_ge(scanned.sem, ring_free(scanned, i, n))
                for c in range(C):
                    nc.scalar.activation(
                        decay[:, ring(n), c, :].rearrange("p (m t) -> p m t", m=2)[:, :, 1:SEQ],
                        dt[:, par, c, :].rearrange("p (m t) -> p m t", m=2)[:, :, 1:SEQ],
                        ACT.Exp, scale=a_neg[:, c, n:n + 1]).then_inc(decayed.sem, 1)
                act.wait_ge(c_spread.sem, c_spread.now(i, n + 1))
                act.wait_ge(weighed.sem, ring_free(weighed, i, n))
                nc.scalar.activation(c_sb[:, ring(n), :], ps_c[0:P, 0:COLS], ACT.Copy).then_inc(c_copied.sem, 1)

            def back(i, n):
                if n == 5:
                    square(i, norms["post"], cen2, sq2)
                if n == 6:
                    inverse_std(i, norms["post"], logv2, rstd2, ps_k)
                if n == 7:
                    act.wait_ge(r_scaled.sem, r_scaled.now(i))
                    for c in half:
                        nc.scalar.activation(normed[:, c, :], r[:, c, :], ACT.Identity, bias=ln_b[:, c:c + 1],
                                             scale=ln_g[:, c:c + 1]).then_inc(affine.sem, 1)
                if n == 9:
                    square(i, norms["ffn"], cen2, sq2)
                if n == 10:
                    inverse_std(i, norms["ffn"], logv2, rstd2, ps_k)
                t = n - turn_slot
                if 0 <= t < n_turn:
                    act.wait_ge(rows_turned.sem, rows_turned.now(i, t + 1))
                    if t == 0:
                        act.wait_ge(stored.sem, stored.before(i))
                    dst = rows if t >= n_turn - 2 else rows_h
                    nc.scalar.activation(dst[:, 2 * (t % 2):2 * (t % 2) + 2, :].rearrange("p a b -> p (a b)"),
                                         ps_k[0:ROWS, 0:2 * D], ACT.Copy).then_inc(rows_done.sem, 1)
                if n == 15:
                    if first:
                        act.wait_ge(h_out_done.sem, h_out_done.now(i))
                        act.dma_start(dram["h0"][i, :, :], h_out[:].rearrange("p a b -> p (a b)")).then_inc(stored.sem, 16)
                    act.wait_ge(rows_done.sem, rows_done.now(i))
                    if not first:
                        act.dma_start(dram["h1"][i, :, :], rows_h[:].rearrange("p a b -> p (a b)")).then_inc(stored.sem, 16)
                    act.dma_start(dram[f"xf{T}"][i, :, :], rows[:].rearrange("p a b -> p (a b)")).then_inc(stored.sem, 16)

            def front_alone():
                for n in range(N_STATE):
                    front(0, 0, n)

            def turn(i, par, fh, has_front, has_back):
                for n in range(N_STATE):
                    scan(i, par, n)
                    if has_back:
                        back(i - 1, n)
                    if has_front:
                        front(i + 1, 1 - par, n)

            def back_alone():
                for n in range(N_STATE):
                    back(pairs - 1, n)

            all_turns(turn, front_alone, back_alone)(act)
            act.wait_ge(stored.sem, stored.now(pairs - 1))

        @block.gpsimd
        def _(pool):
            prime(pool, weighed)

            def gather(i):
                pool.wait_ge(ix_done.sem, ix_done.now(i))
                pool.wait_ge(turned.sem, turned.before(i))
                pool.sem_inc(waited, 1)
                for j in range(4):
                    pool.indirect_dma_start(
                        out=gathered[:, j, :], out_offset=None, in_=dram["moe_out0"],
                        in_offset=bass.IndirectOffsetOnAxis(ap=slot_ix[:, j:j + 1], axis=0)).then_inc(gather_landed.sem, 16)

            def scan(i, n):
                pool.wait_ge(scanned.sem, scanned.now(i, n + 1))
                pool.wait_ge(c_copied.sem, c_copied.now(i, n + 1))
                pool.wait_ge(summed.sem, ring_free(summed, i, n))
                nc.gpsimd.tensor_tensor(state_c[:, ring(n), :, :], state[:, ring(n), :, :],
                                        c_sb[:, ring(n), :].unsqueeze(1).to_broadcast([P, C, COLS]),
                                        ALU.mult).then_inc(weighed.sem, 1)

            def front_alone():
                if not first:
                    gather(0)

            def turn(i, par, fh, has_front, has_back):
                for n in range(N_STATE):
                    scan(i, n)
                    if n == 0 and has_front and not first:
                        gather(i + 1)

            all_turns(turn, front_alone, lambda: None)(pool)

        @block.vector
        def _(dve):
            nc.vector.memset(eps[:, :], EPS).then_inc(ready, 1)
            chain = [0]

            def link(ins):
                chain[0] += 1
                ins.then_inc(setup, 1)
                dve.wait_ge(setup, chain[0])

            link(nc.vector.memset(decay[:].rearrange("p a b c -> p (a b c)"), 0.0))
            dve.wait_ge(loaded, n_loads)
            if first:
                link(nc.vector.memset(x_pad[:].rearrange("p a b c -> p (a b c)"), 0.0))
                for c in half:
                    link(nc.vector.tensor_scalar(pos[:, c, 1:], pos[:, c, 1:], tok_b[:, c:c + 1], None, ALU.add))
                    for m in half:
                        link(nc.vector.tensor_tensor(emb[:, c, m, 1:2], pos[:, c, 0:1], class_token[:, c:c + 1], ALU.add))
                        link(nc.vector.tensor_copy(emb[:, c, m, 0:1], cls_tok[:, c:c + 1]))
                        for par in half:
                            link(nc.vector.tensor_copy(h[:, par, c, m * SEQ:m * SEQ + 1], cls_tok[:, c:c + 1]))
                link(nc.vector.tensor_copy(cls_emb[:].rearrange("p c m t -> p (c m) t"),
                                           emb[:, :, :, 0:2].rearrange("p c m t -> p (c m) t")))
            prime(dve, gate_done, xn_done, one_done, corr_done, sum_done, dt_done, du_done, bc_r1, bc_lo, driven, scanned,
                  skip_done, y_done, r_done, r_scaled, h_out_done, xf_done, h_kept, *(n.centred for n in norms.values()))
            if first:
                prime(dve, emb_done, emb_cls, tok_scaled, conv_done)
            else:
                prime(dve, h_done, ix_done)
            dve.wait_ge(ready, 2)
            nc.vector.tensor_scalar(a_neg[:].rearrange("p a b -> p (a b)"), a_neg[:].rearrange("p a b -> p (a b)"),
                                    -1.0, None, ALU.mult).then_inc(ready, 1)

            def wide(t):
                return t.unsqueeze(1).to_broadcast([t.shape[0], 2, COLS])

            def centre(n, i, src, cen, bank):
                dve.wait_ge(n.mean.sem, n.mean.now(i))
                nc.vector.tensor_tensor(cen[:], src, wide(bank[0:F, 0:COLS]), ALU.subtract).then_inc(n.centred.sem, 1)

            def scale(n, i, dst, cen, rstd, sig):
                dve.wait_ge(n.rstd.sem, n.rstd.now(i))
                nc.vector.tensor_tensor(dst, cen[:], wide(rstd[:, :]), ALU.mult).then_inc(sig.sem, 1)

            def add_positions(i):
                dve.wait_ge(tok_done.sem, tok_done.now(i))
                dve.wait_ge(h_done.sem, h_done.before(i))
                nc.vector.tensor_copy(emb[:, :, :, 0:2].rearrange("p c m t -> p (c m) t"),
                                      cls_emb[:].rearrange("p c m t -> p (c m) t")).then_inc(emb_cls.sem, 1)
                nc.vector.tensor_tensor(
                    emb[:, :, :, 2:], ps_f[0:F, :, 0:COLS - 4].rearrange("p c (m t) -> p c m t", m=2),
                    pos[:, :, 1:].unsqueeze(2).to_broadcast([F, 2, 2, SEQ - 2]), ALU.add).then_inc(emb_done.sem, 1)

            def convolve(i, c):
                dve.wait_ge(pad_done.sem, pad_done.now(i))
                dve.wait_ge(u_done.sem, u_done.before(i))
                nc.vector.tensor_scalar(conv[:, c, :, :], x_pad[:, c, :, 0:SEQ], conv_w[:, c, 0:1], None,
                                        ALU.mult).then_inc(conv_done.sem, 1)
                for k in range(1, 4):
                    dve.wait_ge(conv_done.sem, conv_done.now(i, 4 * c + k))
                    nc.vector.scalar_tensor_tensor(
                        out=conv[:, c, :, :], in0=x_pad[:, c, :, k:k + SEQ], scalar=conv_w[:, c, k:k + 1],
                        in1=conv[:, c, :, :], op0=ALU.mult, op1=ALU.add).then_inc(conv_done.sem, 1)

            def split_rest(i, par, bank):
                dve.wait_ge(bc_hi.sem, bc_hi.now(i))
                dve.wait_ge(bc_lo.sem, bc_lo.before(i))
                nc.vector.tensor_tensor(bc_rest[:, :], ps_f[0:32, bank, 0:COLS], bc_stack[0:32, par, :],
                                        ALU.subtract).then_inc(bc_r1.sem, 1)

            def one_plus(i):
                dve.wait_ge(exp_done.sem, exp_done.now(i))
                nc.vector.tensor_scalar(sp_one[:], sp_exp[:], 1.0, None, ALU.add).then_inc(one_done.sem, 1)

            def time_steps(i, par):
                dve.wait_ge(one_done.sem, one_done.now(i))
                nc.vector.scalar_tensor_tensor(out=sp_exp[:], in0=sp_one[:], scalar=1.0, in1=sp_exp[:],
                                               op0=ALU.subtract, op1=ALU.subtract).then_inc(corr_done.sem, 1)
                dve.wait_ge(corr_done.sem, corr_done.now(i))
                dve.wait_ge(log_done.sem, log_done.now(i))
                nc.vector.tensor_tensor(sp_abs[:], sp_abs[:], sp_exp[:], ALU.subtract).then_inc(sum_done.sem, 1)
                dve.wait_ge(sum_done.sem, sum_done.now(i))
                nc.vector.scalar_tensor_tensor(out=dt[:, par, :, :], in0=sp_raw[:], scalar=0.0, in1=sp_abs[:],
                                               op0=ALU.max, op1=ALU.add).then_inc(dt_done.sem, 1)
                dve.wait_ge(bc_m.sem, bc_m.now(i))
                nc.vector.tensor_tensor(bc_stack[64:96, par, :], bc_rest[:, :], bc_mid[:, :],
                                        ALU.subtract).then_inc(bc_lo.sem, 1)
                dve.wait_ge(dt_done.sem, dt_done.now(i))
                dve.wait_ge(u_done.sem, u_done.now(i))
                nc.vector.tensor_tensor(du[:, par, :, :], dt[:, par, :, :], u[:, par, :, :], ALU.mult).then_inc(du_done.sem, 1)

            def front(i, par, fh, n):
                pre = norms["pre"]
                hp = h[:, par, :, :]
                if first:
                    tok = norms["tok"]
                    e = emb[:].rearrange("p c m t -> p c (m t)")
                    if n == 2:
                        add_positions(i)
                    if n == 3:
                        dve.wait_ge(emb_cls.sem, emb_cls.now(i))
                        dve.wait_ge(emb_done.sem, emb_done.now(i))
                        centre(tok, i, e, cen, ps_f[:, 0, :])
                    if n == 5:
                        scale(tok, i, e, cen, rstd, tok_scaled)
                    if n == 6:
                        centre(pre, i, hp, cen, ps_f[:, 0, :])
                    if n == 8:
                        scale(pre, i, xn[:, par, :, :], cen, rstd, xn_done)
                    if n == 9:
                        convolve(i, 0)
                    if n == 10:
                        convolve(i, 1)
                    if n == 13:
                        split_rest(i, par, 0)
                        one_plus(i)
                else:
                    if n == 3:
                        dve.wait_ge(turned.sem, turned.now(i))
                        dve.wait_ge(in_landed[par].sem, in_landed[par].now(fh))
                        nc.vector.tensor_tensor(hp, hp, ps_f[0:F, :, 0:COLS], ALU.add).then_inc(h_done.sem, 1)
                    if n == 4:
                        dve.wait_ge(h_done.sem, h_done.now(i))
                        centre(pre, i, hp, cen, ps_f[:, 0, :])
                    if n == 6:
                        scale(pre, i, xn[:, par, :, :], cen, rstd, xn_done)
                    if n == 11:
                        split_rest(i, par, 1)
                    if n == 13:
                        one_plus(i)
                if n == 15:
                    time_steps(i, par)

            def slot_indices(i):
                nc.vector.tensor_copy(slot_ix[:, :], slots[:, bass.ds(i * 4, 4)]).then_inc(ix_done.sem, 1)

            def scan(i, par, n):
                if n == 0:
                    dve.wait_ge(du_done.sem, du_done.now(i))
                dve.wait_ge(b_spread.sem, b_spread.now(i, n + 1))
                dve.wait_ge(scanned.sem, scanned.now(i, n - 1) if n >= 2 else scanned.before(i, N_STATE + n - 1))
                nc.vector.tensor_tensor(drive[:, n % 2, :, :], du[:, par, :, :],
                                        ps_b[0:P, 0:COLS].unsqueeze(1).to_broadcast([P, C, COLS]),
                                        ALU.mult).then_inc(driven.sem, 1)
                dve.wait_ge(driven.sem, driven.now(i, n + 1))
                dve.wait_ge(decayed.sem, decayed.now(i, C * (n + 1)))
                dve.wait_ge(weighed.sem, ring_free(weighed, i, n))
                nc.vector.tensor_tensor_scan(
                    state[:, ring(n), :, :].rearrange("p a b -> p (a b)"),
                    decay[:, ring(n), :, :].rearrange("p a b -> p (a b)"),
                    drive[:, n % 2, :, :].rearrange("p a b -> p (a b)"), 0.0, ALU.mult, ALU.add).then_inc(scanned.sem, 1)

            def back(i, par, n):
                post, ffn = norms["post"], norms["ffn"]
                if n == 0:
                    nc.vector.tensor_copy(h_keep[:], h[:, par, :, :]).then_inc(h_kept.sem, 1)
                if n == 2:
                    dve.wait_ge(summed.sem, summed.now(i))
                    dve.wait_ge(out_proj.sem, out_proj.before(i))
                    for c in range(C):
                        nc.vector.scalar_tensor_tensor(out=y[:, c, :], in0=u[:, par, c, :], scalar=skip_w[:, c:c + 1],
                                                       in1=ps_y[0:P, c, 0:COLS], op0=ALU.mult,
                                                       op1=ALU.add).then_inc(skip_done.sem, 1)
                    dve.wait_ge(skip_done.sem, skip_done.now(i))
                    dve.wait_ge(z_done.sem, z_done.now(i))
                    nc.vector.tensor_tensor(y[:], y[:], sz[:, par, :, :], ALU.mult).then_inc(y_done.sem, 1)
                if n in (3, 4):
                    c = n - 3
                    dve.wait_ge(out_proj.sem, out_proj.now(i, c + 1))
                    dve.wait_ge(affine.sem, affine.before(i))
                    nc.vector.tensor_tensor(r[:, c, :], ps_k[0:F, 0:COLS], xn[:, par, c, :], ALU.add).then_inc(r_done.sem, 1)
                if n == 5:
                    dve.wait_ge(r_done.sem, r_done.now(i))
                    centre(post, i, r[:], cen2, ps_k)
                if n == 7:
                    scale(post, i, r[:], cen2, rstd2, r_scaled)
                if n == 8:
                    dve.wait_ge(affine.sem, affine.now(i))
                    dve.wait_ge(stored.sem, stored.before(i))
                    dve.wait_ge(rows_turned.sem, rows_turned.before(i))
                    dve.wait_ge(h_kept.sem, h_kept.now(i))
                    nc.vector.tensor_tensor(h_out[:], h_keep[:], normed[:], ALU.add).then_inc(h_out_done.sem, 1)
                if n == 9:
                    dve.wait_ge(h_out_done.sem, h_out_done.now(i))
                    centre(ffn, i, h_out[:], cen2, ps_k)
                if n == 11:
                    dve.wait_ge(gate_proj.sem, gate_proj.before(i))
                    scale(ffn, i, xf[:], cen2, rstd2, xf_done)
                if n == turn_slot + n_turn:
                    dve.wait_ge(gate_proj.sem, gate_proj.now(i))
                    dst = logits[:, bass.ds(i * 4, 4), 0:E]
                    src = ps_k[0:ROWS, 0:4 * E].rearrange("p (j e) -> p j e", e=E)
                    if first:
                        nc.vector.tensor_tensor(dst, src, gate_b[:, :].unsqueeze(1).to_broadcast([ROWS, 4, E]),
                                                ALU.add).then_inc(gate_done.sem, 1)
                    else:
                        nc.vector.tensor_copy(dst, src).then_inc(gate_done.sem, 1)

            def front_alone():
                if not first:
                    slot_indices(0)
                for n in range(N_STATE):
                    front(0, 0, 0, n)

            def turn(i, par, fh, has_front, has_back):
                if has_front and not first:
                    slot_indices(i + 1)
                for n in range(N_STATE):
                    if n == 0 and has_back:
                        back(i - 1, 1 - par, 0)
                    if n == 2 and has_back:
                        back(i - 1, 1 - par, 2)
                    scan(i, par, n)
                    if has_back and n not in (0, 2):
                        back(i - 1, 1 - par, n)
                    if has_front:
                        front(i + 1, 1 - par, fh, n)

            def back_alone():
                for n in range(N_STATE):
                    back(pairs - 1, (pairs - 1) % 2, n)

            all_turns(turn, front_alone, back_alone)(dve)


TOP = (1, 2)
EXPERTS = (4, 8)
BLOCKS = tuple(TOKENS * TOP[t] // COLS + EXPERTS[t] - 1 for t in (0, 1))
BISECT = 24


def route(nc, held, layer, dram, logits, slots_in, slots_out, weights, expert_of):
    E, K = EXPERTS[layer], TOP[layer]
    NB = BLOCKS[layer]
    DROP = NB * COLS
    T = str(layer)
    with ExitStack() as ctx:
        def sb(name, shape, dt=F32):
            return ctx.enter_context(nc.sbuf_tensor(f"r{T}_{name}", shape, dt))

        def sem(name):
            return held.take(nc, f"r{T}_{name}")

        earlier = sb("earlier", [ROWS, ROWS])
        ones = sb("ones", [ROWS, ROWS])
        steps = sb("steps", [ROWS, 32])
        numbers = sb("numbers", [ROWS, BLOCKS[1]])
        token_of = sb("token_of", [ROWS, TILES])
        zeros = sb("zeros", [ROWS, 4 * D])
        best = sb("best", [ROWS, K, TILES])
        free = sb("free", [ROWS, TILES])
        work = sb("work", [ROWS, E, TILES])
        equal = sb("equal", [ROWS, E, TILES])
        chosen = sb("chosen", [ROWS, K, E, TILES])
        keep = sb("keep", [ROWS, E, TILES])
        score = sb("score", [ROWS, E, TILES])
        flags = sb("flags", [ROWS, E, TILES])
        flags2 = sb("flags2", [ROWS, E, TILES])
        restart = sb("restart", [ROWS, E, TILES])
        run = sb("run", [ROWS, E, TILES])
        place = sb("place", [ROWS, E, TILES])
        bar = sb("bar", [ROWS, E])
        cand = sb("cand", [ROWS, E])
        step = sb("step", [ROWS, 1])
        part = sb("part", [ROWS, E])
        quota = sb("quota", [ROWS, E])
        over = sb("over", [ROWS, E, 32])
        n_blocks = sb("n_blocks", [ROWS, E])
        ends = sb("ends", [ROWS, E])
        base = sb("base", [ROWS, E])
        owner = sb("owner", [ROWS, NB, E])
        kept = sb("kept", [ROWS, TILES])
        spot = sb("spot", [ROWS, TILES])
        lost = sb("lost", [ROWS, TILES])
        ratio = sb("ratio", [ROWS, TILES])
        rows = sb("rows", [ROWS, 2, 4, D])
        index = sb("index", [ROWS, 2, K, 4], U32)

        ps_sum = ctx.enter_context(nc.psum_tensor(f"r{T}_ps_sum", [128, BANK], F32))
        ps_tile = ctx.enter_context(nc.psum_tensor(f"r{T}_ps_tile", [128, 2, BANK], F32))
        ps_in = ctx.enter_context(nc.psum_tensor(f"r{T}_ps_in", [128, 2, BANK], F32))

        loaded = sem("loaded")
        waited = sem("waited")
        dve_step = sem("dve_step")
        gap_ready = sem("gap_ready")
        exp_ready = sem("exp_ready")
        zeros_ready = sem("zeros_ready")
        zeroed = sem("zeroed")
        slots_ready = sem("slots_ready")
        rounds_counted = Signal(nc, held, f"r{T}_rounds_counted")
        rounds_summed = Signal(nc, held, f"r{T}_rounds_summed")
        flags_ready = sem("flags_ready")
        prefix_ready = sem("prefix_ready")
        rows_landed = [Signal(nc, held, f"r{T}_rows_landed_{p}", 1, 16) for p in (0, 1)]
        index_ready = Signal(nc, held, f"r{T}_index_ready")
        scattered = [Signal(nc, held, f"r{T}_scattered_{p}", 4 * K, 16, primed=False) for p in (0, 1)]
        halves = range((E * TILES + BANK - 1) // BANK)
        wide = E * TILES // len(halves)

        block = ctx.enter_context(nc.Block())

        @block.sync
        def _(sp):
            loads = [(earlier[:, :], dram["earlier"]), (ones[:, :], dram["ones"]), (steps[:, :], dram["steps"]),
                     (numbers[:, :], dram["numbers"]), (token_of[:, :], dram["token_of"])]
            load_all(sp, loads, loaded)
            prime(sp, *rows_landed)
            sp.wait_ge(zeros_ready, 1)
            sp.dma_start(dram["moe_out" + T][DROP:DROP + 1, :], zeros[0:1, 0:D]).then_inc(zeroed, 16)
            with sp.Fori(0, NB) as b:
                sp.dma_start(dram["moe_in" + T][bass.ds(b * COLS, COLS), :].rearrange("(p j) d -> p (j d)", j=4),
                             zeros[:, :]).then_inc(zeroed, 16)

            def fetch(i, par):
                sp.dma_start(rows[:, par, :, :].rearrange("p a b -> p (a b)"),
                             dram["xf" + T][i, :, :]).then_inc(rows_landed[par].sem, 16)

            fetch(0, 0)
            fetch(1, 1)
            with sp.Fori(1, PAIRS // 2) as ii:
                for par in (0, 1):
                    sp.wait_ge(scattered[par].sem, scattered[par].before(ii))
                    sp.dma_start(rows[:, par, :, :].rearrange("p a b -> p (a b)"),
                                 dram["xf" + T][2 * ii + par, :, :]).then_inc(rows_landed[par].sem, 16)

        @block.scalar
        def _(act):
            if K == 2:
                act.wait_ge(gap_ready, 1)
                nc.scalar.activation(ratio[:, :], lost[:, :], ACT.Exp).then_inc(exp_ready, 1)

        @block.tensor
        def _(pe):
            pe.wait_ge(loaded, 16 * 5)
            prime(pe, rounds_summed)
            if K == 2:
                with pe.Fori(0, BISECT + 1) as r:
                    pe.wait_ge(rounds_counted.sem, rounds_counted.now(r))
                    nc.tensor.matmul(ps_sum[0:ROWS, 0:E], ones[:, :], part[:, :], start=True,
                                     stop=True).then_inc(rounds_summed.sem, 1)

            for turn in range(K):
                pe.wait_ge(flags_ready, turn + 1)
                source = flags if turn < K - 1 else keep
                source = source[:].rearrange("p e t -> p (e t)")
                for x in halves:
                    nc.tensor.matmul(ps_in[0:ROWS, x, 0:wide], earlier[:, :], source[:, x * wide:(x + 1) * wide],
                                     start=True, stop=True)
                    mm = nc.tensor.matmul(ps_tile[0:ROWS, x, 0:wide], ones[:, :], source[:, x * wide:(x + 1) * wide],
                                          start=True, stop=True)
                mm.then_inc(prefix_ready, 1)

        @block.vector
        def _(dve):
            count = [0]

            def link(ins):
                count[0] += 1
                ins.then_inc(dve_step, 1)
                dve.wait_ge(dve_step, count[0])

            def over_experts(t):
                return t.unsqueeze(1).to_broadcast([ROWS, E, TILES])

            def over_tiles(t):
                return t.unsqueeze(2).to_broadcast([ROWS, E, TILES])

            nc.vector.memset(zeros[:, :], 0.0).then_inc(zeros_ready, 1)
            link(nc.vector.memset(restart[:].rearrange("p e t -> p (e t)"), 1.0))
            link(nc.vector.memset(restart[:, :, 0:1], 0.0))
            by_expert = logits[:, :, 0:E].rearrange("p t e -> p e t")
            for k in range(K):
                if k == 0:
                    link(nc.vector.tensor_copy(work[:], by_expert))
                else:
                    link(nc.vector.scalar_tensor_tensor(
                        out=work[:].rearrange("p e t -> p (e t)"),
                        in0=chosen[:, 0, :, :].rearrange("p e t -> p (e t)"), scalar=-3.0e38,
                        in1=work[:].rearrange("p e t -> p (e t)"), op0=ALU.mult, op1=ALU.add))
                link(nc.vector.tensor_reduce(best[:, k, :], work[:].rearrange("p e t -> p t e"), AX.X, ALU.max))
                link(nc.vector.tensor_tensor(equal[:], work[:], over_experts(best[:, k, :]), ALU.is_equal))
                link(nc.vector.memset(free[:, :], 1.0))
                for e in range(E):
                    link(nc.vector.tensor_tensor(chosen[:, k, e, :], equal[:, e, :], free[:, :], ALU.mult))
                    link(nc.vector.tensor_tensor(free[:, :], free[:, :], chosen[:, k, e, :], ALU.subtract))

            def prefix(turn):
                dve.wait_ge(prefix_ready, turn + 1)
                for x in halves:
                    part_ = slice(x * wide, (x + 1) * wide)
                    flat = [t[:].rearrange("p e t -> p (e t)")[:, part_] for t in (restart, run, place)]
                    link(nc.vector.tensor_tensor_scan(flat[1], flat[0], ps_tile[0:ROWS, x, 0:wide], 0.0,
                                                      ALU.mult, ALU.add))
                    link(nc.vector.tensor_tensor(flat[2], flat[1], ps_tile[0:ROWS, x, 0:wide], ALU.subtract))
                    link(nc.vector.tensor_tensor(flat[2], flat[2], ps_in[0:ROWS, x, 0:wide], ALU.add))

            if K == 2:
                nc.vector.tensor_tensor(lost[:, :], best[:, 1, :], best[:, 0, :], ALU.subtract).then_inc(gap_ready, 1)
                dve.wait_ge(exp_ready, 1)
                link(nc.vector.tensor_scalar(kept[:, :], ratio[:, :], 1.0, None, ALU.add))
                link(nc.vector.reciprocal(weights[:, 0, :], kept[:, :]))
                link(nc.vector.tensor_tensor(weights[:, 1, :], weights[:, 0, :], ratio[:, :], ALU.mult))
                link(nc.vector.tensor_scalar(spot[:, :], weights[:, 0, :], 0.5, None, ALU.max))
                link(nc.vector.tensor_tensor(score[:], chosen[:, 0, :, :], chosen[:, 1, :, :], ALU.add))
                link(nc.vector.tensor_tensor(score[:], score[:], over_experts(spot[:, :]), ALU.mult))
                link(nc.vector.memset(bar[:, :], 0.5))
                link(nc.vector.memset(step[:, :], 0.5))
                prime(dve, rounds_counted, *())
                start = count[0]
                with dve.Fori(0, BISECT) as r:
                    turn = r * 5 + start
                    nc.vector.tensor_scalar(cand[:, :], bar[:, :], step[:, 0:1], None, ALU.add).then_inc(dve_step, 1)
                    dve.wait_ge(dve_step, turn + 1)
                    nc.vector.tensor_tensor(flags[:], score[:], over_tiles(cand[:, :]), ALU.is_ge).then_inc(dve_step, 1)
                    dve.wait_ge(dve_step, turn + 2)
                    nc.vector.tensor_reduce(part[:, :], flags[:], AX.X, ALU.add).then_inc(rounds_counted.sem, 1)
                    dve.wait_ge(rounds_summed.sem, rounds_summed.now(r))
                    nc.vector.tensor_scalar(quota[:, :], ps_sum[0:ROWS, 0:E], float(CAP), step[:, 0:1],
                                            ALU.is_ge, ALU.mult).then_inc(dve_step, 1)
                    dve.wait_ge(dve_step, turn + 3)
                    nc.vector.tensor_tensor(bar[:, :], bar[:, :], quota[:, :], ALU.add).then_inc(dve_step, 1)
                    dve.wait_ge(dve_step, turn + 4)
                    nc.vector.tensor_scalar(step[:, :], step[:, :], 0.5, None, ALU.mult).then_inc(dve_step, 1)
                    dve.wait_ge(dve_step, turn + 5)
                count[0] = start + 5 * BISECT
                link(nc.vector.tensor_tensor(flags2[:], score[:], over_tiles(bar[:, :]), ALU.is_gt))
                nc.vector.tensor_reduce(part[:, :], flags2[:], AX.X, ALU.add).then_inc(rounds_counted.sem, 1)
                nc.vector.tensor_tensor(flags[:], score[:], over_tiles(bar[:, :]), ALU.is_equal).then_inc(flags_ready, 1)
                dve.wait_ge(rounds_summed.sem, rounds_summed.now(BISECT))
                link(nc.vector.tensor_scalar(quota[:, :], ps_sum[0:ROWS, 0:E], -1.0, float(CAP), ALU.mult, ALU.add))
                prefix(0)
                link(nc.vector.tensor_tensor(place[:], place[:], over_tiles(quota[:, :]), ALU.is_lt))
                link(nc.vector.tensor_tensor(place[:], place[:], flags[:], ALU.mult))
                nc.vector.tensor_tensor(keep[:], place[:], flags2[:], ALU.add).then_inc(flags_ready, 1)
            else:
                nc.vector.tensor_copy(keep[:], chosen[:, 0, :, :]).then_inc(flags_ready, 1)
            prefix(K - 1)
            totals = run[:, :, TILES - 1:TILES].to_broadcast([ROWS, E, 32])
            dve.wait_ge(loaded, 16 * 5)
            link(nc.vector.tensor_tensor(over[:], totals, steps[:, :].unsqueeze(1).to_broadcast([ROWS, E, 32]),
                                         ALU.is_gt))
            link(nc.vector.tensor_reduce(n_blocks[:, :], over[:], AX.X, ALU.add))
            link(nc.vector.tensor_copy(ends[:, 0:1], n_blocks[:, 0:1]))
            for e in range(1, E):
                link(nc.vector.tensor_tensor(ends[:, e:e + 1], ends[:, e - 1:e], n_blocks[:, e:e + 1], ALU.add))
            link(nc.vector.tensor_tensor(base[:, :], ends[:, :], n_blocks[:, :], ALU.subtract))
            link(nc.vector.tensor_scalar(base[:, :], base[:, :], float(COLS), None, ALU.mult))
            link(nc.vector.tensor_tensor(owner[:], numbers[:, 0:NB].unsqueeze(2).to_broadcast([ROWS, NB, E]),
                                         ends[:, :].unsqueeze(1).to_broadcast([ROWS, NB, E]), ALU.is_ge))
            link(nc.vector.tensor_reduce(kept[:, 0:NB], owner[:], AX.X, ALU.add))
            link(nc.vector.tensor_scalar(expert_of[:, 0:NB], kept[0:1, 0:NB], float(E - 1), None, ALU.min))
            link(nc.vector.tensor_tensor(place[:], place[:], over_tiles(base[:, :]), ALU.add))
            for k in range(K):
                link(nc.vector.tensor_tensor(flags[:], chosen[:, k, :, :], keep[:], ALU.mult))
                link(nc.vector.tensor_reduce(kept[:, :], flags[:].rearrange("p e t -> p t e"), AX.X, ALU.add))
                link(nc.vector.tensor_tensor(flags[:], flags[:], place[:], ALU.mult))
                link(nc.vector.tensor_reduce(spot[:, :], flags[:].rearrange("p e t -> p t e"), AX.X, ALU.add))
                if K == 2:
                    link(nc.vector.tensor_tensor(weights[:, k, :], weights[:, k, :], kept[:, :], ALU.mult))
                link(nc.vector.tensor_scalar(kept[:, :], kept[:, :], -1.0, 1.0, ALU.mult, ALU.add))
                link(nc.vector.scalar_tensor_tensor(out=slots_in[:, k, :], in0=kept[:, :], scalar=float(DROP),
                                                    in1=spot[:, :], op0=ALU.mult, op1=ALU.add))
                link(nc.vector.tensor_scalar(lost[:, :], token_of[:, :], float(DROP + k * TOKENS), None, ALU.add))
                link(nc.vector.tensor_tensor(lost[:, :], lost[:, :], kept[:, :], ALU.mult))
                link(nc.vector.tensor_tensor(slots_out[:, k, :], lost[:, :], spot[:, :], ALU.add))
            prime(dve, index_ready)
            for par in (0, 1):
                nc.vector.tensor_copy(index[:, par, :, :], slots_out[:, :, 4 * par:4 * par + 4]).then_inc(index_ready.sem, 1)
            with dve.Fori(1, PAIRS // 2) as ii:
                for par in (0, 1):
                    i = 2 * ii + par
                    dve.wait_ge(scattered[par].sem, scattered[par].before(ii))
                    nc.vector.tensor_copy(index[:, par, :, :], slots_out[:, :, bass.ds(i * 4, 4)]).then_inc(index_ready.sem, 1)

        @block.gpsimd
        def _(pool):
            pool.wait_ge(zeroed, 16 * (NB + 1))
            with pool.Fori(0, PAIRS // 2) as ii:
                for par in (0, 1):
                    i = 2 * ii + par
                    pool.wait_ge(rows_landed[par].sem, rows_landed[par].now(ii))
                    pool.wait_ge(index_ready.sem, index_ready.now(i))
                    pool.sem_inc(waited, 1)
                    for j in range(4):
                        for k in range(K):
                            pool.indirect_dma_start(
                                out=dram["moe_in" + T], in_=rows[:, par, j, :], in_offset=None,
                                out_offset=bass.IndirectOffsetOnAxis(ap=index[:, par, k, j:j + 1], axis=0),
                            ).then_inc(scattered[par].sem, 16)
            for par in (0, 1):
                pool.wait_ge(scattered[par].sem, scattered[par].now(PAIRS // 2 - 1))


def moe(nc, held, layer, dram, expert_of):
    NB = BLOCKS[layer]
    T = str(layer)
    E = EXPERTS[layer]
    KC = HID // 128
    with ExitStack() as ctx:
        def sb(name, shape, dt=F32):
            return ctx.enter_context(nc.sbuf_tensor(f"e{T}_{name}", shape, dt))

        def signal(name, per=1, unit=1):
            return Signal(nc, held, f"e{T}_{name}", per, unit)

        ident = sb("ident", [128, 128])
        w1 = sb("w1", [F, 2, 2, HID])
        w2 = sb("w2", [128, 2, KC, D])
        b1 = sb("b1", [128, 2, KC])
        b2 = sb("b2", [ROWS, 2, D])
        x_rows = sb("x_rows", [ROWS, 2, 4, D])
        x = sb("x", [F, 2, 2, COLS])
        hidden = sb("hidden", [128, KC, COLS])
        y = sb("y", [ROWS, 2, 4, D])
        ps_x = ctx.enter_context(nc.psum_tensor(f"e{T}_ps_x", [128, 2, BANK], F32))
        ps_h = ctx.enter_context(nc.psum_tensor(f"e{T}_ps_h", [128, 2, BANK], F32))
        ps_o = ctx.enter_context(nc.psum_tensor(f"e{T}_ps_o", [128, 4, BANK], F32))

        ident_landed = held.take(nc, f"e{T}_ident_landed")
        x_landed = [signal(f"x_landed_{p}", 1, 16) for p in (0, 1)]
        w_landed = [signal(f"w_landed_{p}", 4, 16) for p in (0, 1)]
        stored = [signal(f"stored_{p}", 1, 16) for p in (0, 1)]
        turned = signal("turned")
        x_done = signal("x_done")
        hid_proj = signal("hid_proj", KC)
        hid_done = signal("hid_done", KC)
        out_proj = signal("out_proj", 4)
        y_done = signal("y_done", 4)

        block = ctx.enter_context(nc.Block())

        def each_block(eng, body):
            with eng.Fori(0, NB // 2) as bb:
                for par in (0, 1):
                    body(bb, 2 * bb + par, par)
            if NB % 2:
                body(NB // 2, NB - 1, 0)

        @block.sync
        def _(sp):
            sp.dma_start(ident[:, :], dram["ident"]).then_inc(ident_landed, 16)
            prime(sp, *x_landed, *w_landed)

            def fetch(bb, b, par):
                sp.wait_ge(turned.sem, turned.before(b - 1) if not isinstance(b, int) or b >= 2 else turned.before(0))
                sp.dma_start(x_rows[:, par, :, :], dram["moe_in" + T][bass.ds(b * COLS, COLS), :].rearrange(
                    "(j p) d -> p j d", p=ROWS)).then_inc(x_landed[par].sem, 16)
                sp.wait_ge(y_done.sem, y_done.before(b - 1) if not isinstance(b, int) or b >= 2 else y_done.before(0))
                e = sp.value_load(expert_of[0:1, bass.ds(b, 1)], min_val=0, max_val=E - 1)
                for dst, src in ((w1[:, par, :, :].rearrange("p a b -> p (a b)"), dram["w1_" + T][bass.ds(e, 1), :, :]),
                                 (w2[:, par, :, :].rearrange("p a b -> p (a b)"), dram["w2_" + T][bass.ds(e, 1), :, :]),
                                 (b1[:, par, :], dram["b1_" + T][bass.ds(e, 1), :, :])):
                    sp.dma_start(dst, src.rearrange("a p n -> (a p) n")).then_inc(w_landed[par].sem, 16)
                sp.dma_start(b2[:, par, :], dram["b2_" + T][bass.ds(e, 1), :, :].rearrange(
                    "a p n -> (a p) n").to_broadcast([ROWS, D])).then_inc(w_landed[par].sem, 16)

            each_block(sp, fetch)

        @block.tensor
        def _(pe):
            prime(pe, turned, hid_proj, out_proj)
            pe.wait_ge(ident_landed, 16)

            def turn(bb, b, par):
                pe.wait_ge(x_landed[par].sem, x_landed[par].now(bb))
                pe.wait_ge(x_done.sem, x_done.before(b))
                for c in (0, 1):
                    for j in range(4):
                        mm = nc.tensor.transpose(ps_x[0:F, c, j * ROWS:(j + 1) * ROWS],
                                                 x_rows[:, par, j, c * F:(c + 1) * F], ident[0:ROWS, 0:ROWS])
                mm.then_inc(turned.sem, 1)

            def hidden_layer(bb, b, par):
                pe.wait_ge(w_landed[par].sem, w_landed[par].now(bb))
                pe.wait_ge(x_done.sem, x_done.now(b))
                for k in range(KC):
                    pe.wait_ge(hid_done.sem, hid_done.now(b, k - 1) if k >= 2 else hid_done.before(b, KC + k - 1))
                    for c in (0, 1):
                        mm = nc.tensor.matmul(ps_h[:, k % 2, 0:COLS], w1[:, par, c, k * 128:(k + 1) * 128],
                                              x[:, par, c, :], start=(c == 0), stop=(c == 1))
                    mm.then_inc(hid_proj.sem, 1)

            def output_layer(bb, b, par):
                pe.wait_ge(hid_done.sem, hid_done.now(b))
                for j in range(4):
                    pe.wait_ge(y_done.sem, y_done.before(b, j + 1))
                    for k in range(KC):
                        mm = nc.tensor.matmul(ps_o[0:ROWS, j, 0:D], hidden[:, k, j * ROWS:(j + 1) * ROWS],
                                              w2[:, par, k, :], start=(k == 0), stop=(k == KC - 1))
                    mm.then_inc(out_proj.sem, 1)

            turn(0, 0, 0)
            with pe.Fori(0, NB // 2) as bb:
                for par in (0, 1):
                    b = 2 * bb + par
                    hidden_layer(bb, b, par)
                    turn(bb + par, b + 1, 1 - par)
                    output_layer(bb, b, par)
            hidden_layer(NB // 2, NB - 1, 0)
            output_layer(NB // 2, NB - 1, 0)

        @block.scalar
        def _(act):
            prime(act, hid_done, *stored)

            def body(bb, b, par):
                act.wait_ge(w_landed[par].sem, w_landed[par].now(bb))
                act.wait_ge(out_proj.sem, out_proj.before(b))
                for k in range(KC):
                    act.wait_ge(hid_proj.sem, hid_proj.now(b, k + 1))
                    nc.scalar.activation(hidden[:, k, :], ps_h[:, k % 2, 0:COLS], ACT.Gelu,
                                         bias=b1[:, par, k:k + 1]).then_inc(hid_done.sem, 1)
                act.wait_ge(y_done.sem, y_done.now(b))
                act.dma_start(dram["moe_out" + T][bass.ds(b * COLS, COLS), :].rearrange("(j p) d -> p j d", p=ROWS),
                              y[:, par, :, :]).then_inc(stored[par].sem, 16)

            each_block(act, body)
            act.wait_ge(stored[0].sem, stored[0].now(NB // 2))
            act.wait_ge(stored[1].sem, stored[1].now(NB // 2 - 1))

        @block.vector
        def _(dve):
            prime(dve, x_done, y_done)

            def body(bb, b, par):
                dve.wait_ge(turned.sem, turned.now(b))
                nc.vector.tensor_copy(x[:, par, :, :], ps_x[0:F, :, 0:COLS]).then_inc(x_done.sem, 1)
                dve.wait_ge(w_landed[par].sem, w_landed[par].now(bb))
                dve.wait_ge(stored[par].sem, stored[par].before(bb))
                for j in range(4):
                    dve.wait_ge(out_proj.sem, out_proj.now(b, j + 1))
                    nc.vector.tensor_tensor(y[:, par, j, :], ps_o[0:ROWS, j, 0:D], b2[:, par, :],
                                            ALU.add).then_inc(y_done.sem, 1)

            each_block(dve, body)


def combine(nc, held, dram, slots_in, weights):
    with ExitStack() as ctx:
        def sb(name, shape, dt=F32):
            return ctx.enter_context(nc.sbuf_tensor(f"c_{name}", shape, dt))

        def by_parity(name, per=1, unit=1):
            return [Signal(nc, held, f"c_{name}_{p}", per, unit) for p in (0, 1)]

        h = sb("h", [ROWS, 2, 4, D])
        picked = sb("picked", [ROWS, 2, 2, 4, D])
        index = sb("index", [ROWS, 2, 2, 4], U32)
        share = sb("share", [ROWS, 2, 2, 4])
        h_landed = by_parity("h_landed", 1, 16)
        gathered = [Signal(nc, held, f"c_gathered_{p}", 8, 16, primed=False) for p in (0, 1)]
        index_done = by_parity("index_done", 2)
        added = by_parity("added", 8)
        stored = by_parity("stored", 1, 16)
        waited = held.take(nc, "c_waited")
        block = ctx.enter_context(nc.Block())

        def each_pair(eng, body):
            with eng.Fori(0, PAIRS // 2) as ii:
                for par in (0, 1):
                    body(ii, 2 * ii + par, par)

        @block.sync
        def _(sp):
            prime(sp, *h_landed)

            def body(ii, i, par):
                sp.wait_ge(stored[par].sem, stored[par].before(ii))
                sp.dma_start(h[:, par, :, :].rearrange("p a b -> p (a b)"), dram["h1"][i, :, :]).then_inc(h_landed[par].sem, 16)

            each_pair(sp, body)

        @block.gpsimd
        def _(pool):
            def body(ii, i, par):
                pool.wait_ge(index_done[par].sem, index_done[par].now(ii))
                pool.wait_ge(added[par].sem, added[par].before(ii))
                pool.sem_inc(waited, 1)
                for k in (0, 1):
                    for j in range(4):
                        pool.indirect_dma_start(
                            out=picked[:, par, k, j, :], out_offset=None, in_=dram["moe_out1"],
                            in_offset=bass.IndirectOffsetOnAxis(ap=index[:, par, k, j:j + 1], axis=0),
                        ).then_inc(gathered[par].sem, 16)

            each_pair(pool, body)

        @block.vector
        def _(dve):
            prime(dve, *index_done, *added)

            def indices(ii, i, par):
                nc.vector.tensor_copy(index[:, par, :, :], slots_in[:, :, bass.ds(i * 4, 4)]).then_inc(index_done[par].sem, 1)
                nc.vector.tensor_copy(share[:, par, :, :], weights[:, :, bass.ds(i * 4, 4)]).then_inc(index_done[par].sem, 1)

            def body(ii, i, par):
                indices(ii, i, par)
                dve.wait_ge(h_landed[par].sem, h_landed[par].now(ii))
                dve.wait_ge(gathered[par].sem, gathered[par].now(ii))
                dve.wait_ge(index_done[par].sem, index_done[par].now(ii))
                for k in (0, 1):
                    for j in range(4):
                        if k == 1:
                            dve.wait_ge(added[par].sem, added[par].now(ii, j + 1))
                        nc.vector.scalar_tensor_tensor(out=h[:, par, j, :], in0=picked[:, par, k, j, :],
                                                       scalar=share[:, par, k, j:j + 1], in1=h[:, par, j, :],
                                                       op0=ALU.mult, op1=ALU.add).then_inc(added[par].sem, 1)

            each_pair(dve, body)

        @block.scalar
        def _(act):
            prime(act, *stored)
            out = dram["out"].rearrange("m t d -> (m t) d").rearrange("(i j p) d -> i p j d", j=4, p=ROWS)

            def body(ii, i, par):
                act.wait_ge(added[par].sem, added[par].now(ii))
                act.dma_start(out[bass.ds(i, 1), :, :, :].rearrange("a p j d -> p (a j) d"), h[:, par, :, :]).then_inc(stored[par].sem, 16)

            each_pair(act, body)
            for par in (0, 1):
                act.wait_ge(stored[par].sem, stored[par].now(PAIRS // 2 - 1))


def bass_vit_tower(nc, dram):
    with ExitStack() as ctx:
        def sb(name, shape, dt=F32):
            return ctx.enter_context(nc.sbuf_tensor(name, shape, dt))

        logits = sb("logits", [ROWS, TILES, 8])
        slots_in = sb("slots_in", [ROWS, 2, TILES], U32)
        slots_out = sb("slots_out", [ROWS, 2, TILES], U32)
        weights = sb("weights", [ROWS, 2, TILES])
        expert_of = sb("expert_of", [1, BLOCKS[1]], I32)
        for layer in (0, 1):
            for stage in ("mamba", "route", "moe"):
                held = Semaphores()
                if stage == "mamba":
                    mamba(nc, held, layer, dram, logits, slots_in[:, 0, :], PAIRS)
                elif stage == "route":
                    route(nc, held, layer, dram, logits, slots_in[:, 0:TOP[layer], :],
                          slots_out[:, 0:TOP[layer], :], weights, expert_of)
                else:
                    moe(nc, held, layer, dram, expert_of)
                held.hand_back(nc)
        combine(nc, Semaphores(), dram, slots_in, weights)


def layouts(inp):
    import numpy as _np
    a = {k: _np.asarray(v) for k, v in inp.items()}
    out = {}

    def put(name, x):
        out[name] = _np.ascontiguousarray(x)

    def chunks(v, p):
        v = v.reshape((-1, p) + v.shape[1:])
        return v.transpose((1, 0) + tuple(range(2, v.ndim)))

    x = a["x"].reshape(PAIRS, 2, 3, GRID, 16, GRID, 16).transpose(0, 2, 4, 6, 1, 3, 5)
    put("x", x.reshape(PAIRS, 6, 128, COLS - 4).transpose(0, 2, 1, 3).reshape(PAIRS, 128, -1))
    put("tok_w", chunks(a["L0_tok_W"].T, 128))
    for n, k in (("tok_b", "L0_tok_b"), ("tok_g", "L0_tok_gamma"), ("tok_beta", "L0_tok_beta"),
                 ("conv_b", "L0_attn_conv_b"), ("dt_b0", "L0_attn_dt_b"), ("skip0", "L0_attn_D_param"),
                 ("ln_g0", "L0_attn_ln_g"), ("ln_b0", "L0_attn_ln_b"), ("ln_g1", "L1_attn_gamma"),
                 ("ln_b1", "L1_attn_beta"), ("a_log0", "L0_attn_A_log")):
        put(n, chunks(a[k], F))
    put("class_token", chunks(a["L0_tok_class_token"].reshape(D), F))
    put("cls_tok", chunks(a["cls_tok"].reshape(D), F))
    put("conv_w", chunks(a["L0_attn_conv_w"].reshape(D, 4), F))
    put("in_w0", chunks(a["L0_attn_in_proj_w"].T, F))
    put("dt_w0", chunks(a["L0_attn_dt_w"].T, F))
    put("bc_w0", chunks(_np.concatenate([a["L0_attn_B_w"], a["L0_attn_C_w"]]).T, F))
    put("out_w0", chunks(a["L0_attn_out_w"].T, F))
    put("gate_w0", chunks(a["L0_ffn_Wg"], F))
    put("gate_b0", _np.broadcast_to(a["L0_ffn_bg"], (ROWS, 4)))
    put("in_w1", chunks(a["L1_attn_W_in"], F))
    put("x_w1", chunks(a["L1_attn_W_x"], 128))
    put("dt_w1", a["L1_attn_W_dt"])
    put("out_w1", chunks(a["L1_attn_W_out"], 128))
    put("gate_w1", chunks(a["L1_ffn_Wg"], F))
    for n, k in (("dt_b1", "L1_attn_b_dt"), ("skip1", "L1_attn_D_skip"), ("a_log1", "L1_attn_A_log")):
        put(n, chunks(a[k], 128))
    for t, e in (("0", 4), ("1", 8)):
        put("w1_" + t, a[f"L{t}_ffn_W1"].reshape(e, 2, F, HID).transpose(0, 2, 1, 3).reshape(e, F, -1))
        put("w2_" + t, a[f"L{t}_ffn_W2"].reshape(e, 6, 128, D).transpose(0, 2, 1, 3).reshape(e, 128, -1))
        put("b1_" + t, a[f"L{t}_ffn_b1"].reshape(e, 6, 128).transpose(0, 2, 1))
        put("b2_" + t, a[f"L{t}_ffn_b2"].reshape(e, 1, D))
    return out


def shape_constants():
    import numpy as _np
    from concourse import mybir as _mybir
    f32 = _np.float32
    out = {"ident": _np.eye(128, dtype=f32), "avg": _np.full((F, F), 1.0 / D, f32)}
    sel = _np.zeros((96, 32, 128), f32)
    sel[_np.arange(96), _np.arange(96) % 32, :] = 1.0
    out["select"] = sel.astype(_mybir.dt.np(BF16))
    i = _np.arange(SEQ - 1, dtype=f32)[:, None]
    j = _np.arange(D, dtype=f32)[None, :]
    angle = i / _np.power(f32(10000.0), (_np.floor(j / f32(2.0)) * f32(2.0) / f32(D)).astype(f32))
    pos = _np.where(_np.arange(D)[None, :] % 2 == 0, _np.sin(angle), _np.cos(angle)).astype(f32)
    out["pos"] = pos.T.reshape(2, F, SEQ - 1).transpose(1, 0, 2)
    out["earlier"] = _np.triu(_np.ones((ROWS, ROWS), f32), 1)
    out["ones"] = _np.ones((ROWS, ROWS), f32)
    out["steps"] = _np.broadcast_to(_np.arange(32, dtype=f32) * COLS, (ROWS, 32))
    out["numbers"] = _np.broadcast_to(_np.arange(BLOCKS[1], dtype=f32), (ROWS, BLOCKS[1]))
    out["token_of"] = _np.arange(TILES, dtype=f32)[None, :] * ROWS + _np.arange(ROWS, dtype=f32)[:, None]
    return {k: _np.ascontiguousarray(v) for k, v in out.items()}


DEBUG = 1


def kernel(**inputs):
    import numpy as _np
    import concourse.bacc as _bacc
    from concourse import mybir as _mybir
    from concourse.bass_utils import run_bass_kernel_spmd as _run

    nc = _bacc.Bacc("TRN2", target_bir_lowering=False, num_devices=1)
    arrays, dram = {}, {}
    for name, v in (layouts(inputs) | shape_constants()).items():
        arrays["in_" + name] = v
        t = nc.dram_tensor("in_" + name, v.shape, _mybir.dt.from_np(v.dtype), kind="ExternalInput").ap()
        if name not in ("x", "w1_0", "w1_1", "w2_0", "w2_1", "b1_0", "b1_1", "b2_0", "b2_1") and len(v.shape) > 2:
            t = t.rearrange("p a b -> p (a b)")
        dram[name] = t
    kind = "ExternalOutput" if DEBUG else "Internal"
    scratch = {"h0": (PAIRS, F, 2 * COLS), "h1": (PAIRS, ROWS, 4 * D)}
    for t in (0, 1):
        scratch[f"xf{t}"] = (PAIRS, ROWS, 4 * D)
        scratch[f"moe_in{t}"] = (BLOCKS[t] * COLS + TOP[t] * TOKENS, D)
        scratch[f"moe_out{t}"] = (BLOCKS[t] * COLS + 1, D)
    for name, shape in scratch.items():
        k = kind if name in ("h0", "h1", "xf0", "xf1") else "Internal"
        dram[name] = nc.dram_tensor(name, shape, F32, kind=k).ap()
    dram["out"] = nc.dram_tensor("out_0", (IMAGES, SEQ, D), F32, kind="ExternalOutput").ap()
    bass_vit_tower(nc, dram)
    r = _run(nc, [arrays], core_ids=[0])
    return r.results[0]["out_0"]
```

```python
from contextlib import ExitStack

import numpy as np

import concourse.bass as bass
from concourse import mybir

F32 = mybir.dt.float32
BF16 = mybir.dt.bfloat16
I32 = mybir.dt.int32
U32 = mybir.dt.uint32
ALU = mybir.AluOpType
ACT = mybir.ActivationFunctionType
AX = mybir.AxisListType

IMAGES = 64
GRID = 14
PATCH_K = 768
SEQ = GRID * GRID + 2
PAIRS = IMAGES // 2
COLS = 2 * SEQ
ROWS = COLS // 4
TILES = PAIRS * 4
TOKENS = IMAGES * SEQ
D = 192
F = D // 2
N_STATE = 16
HID = 768
EPS = 1e-5
BANK = 512
CAP = int(1.25 * TOKENS * 2 / 8)


class Semaphores:

    def __init__(self):
        self.taken = []

    def take(self, nc, name):
        self.taken.append(nc.alloc_semaphore(name=name))
        return self.taken[-1]

    def hand_back(self, nc):
        nc.clear_and_free_semaphores(self.taken)
        nc.all_engine_barrier()


class Signal:

    def __init__(self, nc, held, name, per=1, unit=1, primed=True):
        self.sem = held.take(nc, name)
        self.per, self.unit, self.ahead = per, unit, int(primed)

    def now(self, i, k=None):
        return (i + self.ahead) * (self.per * self.unit) + (self.per if k is None else k) * self.unit

    def before(self, i, k=None):
        return (i - 1 + self.ahead) * (self.per * self.unit) + (self.per if k is None else k) * self.unit


def prime(eng, *signals):
    for s in signals:
        eng.sem_inc(s.sem, s.per * s.unit)


class Norm:

    def __init__(self, nc, held, name):
        self.mean = Signal(nc, held, name + "_mean")
        self.centred = Signal(nc, held, name + "_centred")
        self.square = Signal(nc, held, name + "_square")
        self.var = Signal(nc, held, name + "_var")
        self.log = Signal(nc, held, name + "_log")
        self.rstd = Signal(nc, held, name + "_rstd")


def load_all(sp, loads, sem):
    for dst, src in loads:
        sp.dma_start(dst, src).then_inc(sem, 16)
    return 16 * len(loads)


def mamba(nc, held, layer, dram, logits, slots, pairs):
    first = layer == 0
    P, C = (96, 2) if first else (128, 3)
    E = 4 if first else 8
    RING = 3
    JOINED = (1, 3, 5, 7, 9, 11, 13, 15) if first else (1, 5, 9, 13)
    SUMMED = [n for n in range(N_STATE) if n + 1 not in JOINED]
    T = str(layer)
    with ExitStack() as ctx:
        def sb(name, shape, dt=F32):
            return ctx.enter_context(nc.sbuf_tensor(f"m{T}_{name}", shape, dt))

        def ps(name, shape):
            return ctx.enter_context(nc.psum_tensor(f"m{T}_ps_{name}", shape, F32))

        def signal(name, per=1, unit=1):
            return Signal(nc, held, f"m{T}_{name}", per, unit)

        loads = []

        def const(name, key, shape, dt=F32):
            t = sb(name, shape, dt)
            flat = t[:] if len(shape) == 2 else t[:].rearrange(
                "p a b -> p (a b)" if len(shape) == 3 else "p a b c -> p (a b c)")
            loads.append((flat, dram[key]))
            return t

        ident = const("ident", "ident", [128, 128])
        select = const("select", "select", [96, 32, 128], BF16)
        avg = const("avg", "avg", [F, F])
        gate_w = const("gate_w", f"gate_w{T}", [F, 2, E])
        a_log = const("a_log", f"a_log{T}", [P, C, N_STATE])
        skip_w = const("skip_w", f"skip{T}", [P, C])
        dt_bias = const("dt_bias", f"dt_b{T}", [P, C])
        ln_g = const("ln_g", f"ln_g{T}", [F, 2])
        ln_b = const("ln_b", f"ln_b{T}", [F, 2])
        out_w = const("out_w", f"out_w{T}", [P, C, D])
        in_w = const("in_w", f"in_w{T}", [F, 2, 2 * P * C])
        if first:
            tok_w = const("tok_w", "tok_w", [128, 6, D])
            tok_b = const("tok_b", "tok_b", [F, 2])
            tok_g = const("tok_g", "tok_g", [F, 2])
            tok_beta = const("tok_beta", "tok_beta", [F, 2])
            class_token = const("class_token", "class_token", [F, 2])
            cls_tok = const("cls_tok", "cls_tok", [F, 2])
            pos = const("pos", "pos", [F, 2, SEQ - 1])
            conv_w = const("conv_w", "conv_w", [F, 2, 4])
            conv_b = const("conv_b", "conv_b", [F, 2])
            dt_w = const("dt_w", "dt_w0", [F, 2, D])
            bc_w = const("bc_w", "bc_w0", [F, 2, 32])
            gate_b = const("gate_b", "gate_b0", [ROWS, E])
        else:
            x_w = const("x_w", "x_w1", [P, C, 80])
            dt_w = const("dt_w", "dt_w1", [48, P * C])
        n_loads = 16 * len(loads)
        eps = sb("eps", [128, 1])
        a_neg = sb("a_neg", [P, C, N_STATE])

        if first:
            patches = sb("patches", [128, 2, 6, COLS - 4])
            emb = sb("emb", [F, 2, 2, SEQ])
            cls_emb = sb("cls_emb", [F, 2, 2, 2])
            x_pad = sb("x_pad", [F, 2, 2, SEQ + 3])
            conv = sb("conv", [F, 2, 2, SEQ])
        else:
            gathered = sb("gathered", [ROWS, 4, D])
            slot_ix = sb("slot_ix", [ROWS, 4], U32)
            low_rank = sb("low_rank", [48, COLS])
        h = sb("h", [F, 2, 2, COLS])
        xn = sb("xn", [F, 2, 2, COLS])
        cen = sb("cen", [F, 2, COLS])
        sq = sb("sq", [F, 2, COLS])
        logv = sb("logv", [F, COLS])
        rstd = sb("rstd", [F, COLS])
        u = sb("u", [P, 2, C, COLS])
        sz = sb("sz", [P, 2, C, COLS])
        sp_abs = sb("sp_abs", [P, C, COLS])
        sp_exp = sb("sp_exp", [P, C, COLS])
        sp_one = sb("sp_one", [P, C, COLS])
        sp_raw = sb("sp_raw", [P, C, COLS])
        dt = sb("dt", [P, 2, C, COLS])
        du = sb("du", [P, 2, C, COLS])
        bc_stack = sb("bc_stack", [96, 2, COLS], BF16)
        bc_rest = sb("bc_rest", [32, COLS])
        bc_mid = sb("bc_mid", [32, COLS], BF16)
        c_sb = sb("c_sb", [P, RING, COLS])
        decay = sb("decay", [P, RING, C, COLS])
        drive = sb("drive", [P, 2, C, COLS])
        state = sb("state", [P, RING, C, COLS])
        state_c = sb("state_c", [P, RING, C, COLS])
        y = sb("y", [P, C, COLS])
        r = sb("r", [F, 2, COLS])
        cen2 = sb("cen2", [F, 2, COLS])
        sq2 = sb("sq2", [F, 2, COLS])
        logv2 = sb("logv2", [F, COLS])
        rstd2 = sb("rstd2", [F, COLS])
        normed = sb("normed", [F, 2, COLS])
        h_out = sb("h_out", [F, 2, COLS])
        h_keep = sb("h_keep", [F, 2, COLS])
        xf = sb("xf", [F, 2, COLS])
        rows = sb("rows", [ROWS, 4, D])
        rows_h = None if first else sb("rows_h", [ROWS, 4, D])

        ps_y = ps("y", [128, C, BANK])
        ps_b = ps("b", [128, 2, BANK])
        ps_c = ps("c", [128, BANK])
        ps_f = ps("f", [128, 2 if first else 1, BANK])
        var_bank = ps_f[:, 1 if first else 0, :]
        ps_k = ps("k", [128, BANK])

        loaded = held.take(nc, f"m{T}_loaded")
        ready = held.take(nc, f"m{T}_ready")
        waited = held.take(nc, f"m{T}_waited")
        in_landed = [signal(f"in_landed_{p}", 1, 16) for p in (0, 1)]
        norms = {k: Norm(nc, held, f"m{T}_{k}") for k in (["tok"] if first else []) + ["pre", "post", "ffn"]}
        setup = held.take(nc, f"m{T}_setup")
        if first:
            tok_done = signal("tok_done")
            emb_cls = signal("emb_cls")
            emb_done = signal("emb_done")
            tok_scaled = signal("tok_scaled")
            h_done = signal("h_done", 2)
            x_proj = signal("x_proj")
            pad_done = signal("pad_done")
            z_proj = signal("z_proj")
            z_copied = signal("z_copied")
            conv_done = signal("conv_done", 8)
        else:
            ix_done = signal("ix_done")
            gather_landed = Signal(nc, held, f"m{T}_gather_landed", 4, 16, primed=False)
            turned = signal("turned", 2)
            h_done = signal("h_done", 2)
            rank_proj = signal("rank_proj")
            rank_copied = signal("rank_copied")
            xz_proj = signal("xz_proj", 2 * C)
            xz_copied = signal("xz_copied", 2 * C)
        xn_done = signal("xn_done")
        h_kept = signal("h_kept")
        u_done = signal("u_done", 2 if first else 1)
        z_done = signal("z_done")
        dt_proj = signal("dt_proj", C)
        bc_proj = signal("bc_proj")
        raw_done = signal("raw_done", C)
        abs_done = signal("abs_done")
        exp_done = signal("exp_done")
        one_done = signal("one_done")
        log_done = signal("log_done")
        corr_done = signal("corr_done")
        sum_done = signal("sum_done")
        dt_done = signal("dt_done")
        du_done = signal("du_done")
        bc_hi = signal("bc_hi")
        bc_r1 = signal("bc_r1")
        bc_m = signal("bc_m", 2)
        bc_lo = signal("bc_lo")
        b_spread = signal("b_spread", N_STATE)
        c_spread = signal("c_spread", N_STATE)
        c_copied = signal("c_copied", N_STATE)
        decayed = signal("decayed", N_STATE * C)
        driven = signal("driven", N_STATE)
        scanned = signal("scanned", N_STATE)
        weighed = signal("weighed", N_STATE)
        joined = signal("joined", len(JOINED))
        summed = signal("summed", len(SUMMED))
        skip_done = signal("skip_done", C)
        y_done = signal("y_done")
        out_proj = signal("out_proj", 2)
        r_done = signal("r_done", 2)
        r_scaled = signal("r_scaled")
        affine = signal("affine", 2)
        h_out_done = signal("h_out_done")
        xf_done = signal("xf_done")
        n_turn = 2 if first else 4
        turn_slot = 13 if first else 11
        ffn_slot = 10 if first else 9
        late = (6,) if first else (6, 10)
        rows_turned = signal("rows_turned", n_turn)
        rows_done = signal("rows_done", n_turn)
        gate_proj = signal("gate_proj")
        gate_done = signal("gate_done")
        stored = signal("stored", 2, 16)

        block = ctx.enter_context(nc.Block())
        half = range(2)

        def ring(n):
            return n % RING if n < N_STATE - 1 else 1

        def ring_free(sig, i, n):
            if n < RING:
                return sig.before(i, max(m for m in range(N_STATE) if ring(m) == n) + 1)
            return sig.now(i, max(m for m in range(n) if ring(m) == ring(n)) + 1)

        def is_first(i):
            return isinstance(i, int) and i == 0

        def nothing(*where):
            pass

        def count_to(kinds, n):
            return sum(m <= n for m in kinds)

        def all_turns(turn, front, early, back):

            def run(eng):
                for n in range(N_STATE):
                    early(0, 0, 0, n)
                for n in range(N_STATE):
                    front(0, 0, 0, n)
                    early(1, 1, 0, n)
                turn(0, 0, 0, 1, True, True, False)
                with eng.Fori(0, (pairs - 4) // 2) as jj:
                    for q in (0, 1):
                        turn(2 * jj + 1 + q, (1 + q) % 2, jj + 1, jj + 1 + q, True, True, True)
                turn(pairs - 3, 1, (pairs - 2) // 2, (pairs - 1) // 2, True, True, True)
                turn(pairs - 2, 0, (pairs - 1) // 2, None, True, False, True)
                turn(pairs - 1, 1, None, None, False, False, True)
                for n in range(N_STATE):
                    back(pairs - 1, 1, n)

            return run

        @block.sync
        def _(sp):
            load_all(sp, loads, loaded)
            prime(sp, *in_landed)

            def fetch(i, par):
                if first:
                    sp.dma_start(patches[:, par, :, :].rearrange("p a b -> p (a b)"),
                                 dram["x"][i, :, :]).then_inc(in_landed[par].sem, 16)
                else:
                    sp.dma_start(h[:, par, :, :].rearrange("p a b -> p (a b)"),
                                 dram["h0"][i, :, :]).then_inc(in_landed[par].sem, 16)

            fetch(0, 0)
            fetch(1, 1)
            with sp.Fori(0, pairs // 2 - 1) as ii:
                for par in half:
                    if first:
                        sp.wait_ge(tok_done.sem, tok_done.now(2 * ii + par))
                    else:
                        sp.wait_ge(h_kept.sem, h_kept.now(2 * ii + par))
                    fetch(2 * ii + par + 2, par)

        @block.tensor
        def _(pe):
            pe.wait_ge(loaded, n_loads)
            pe.wait_ge(ready, 3)
            prime(pe, dt_proj, bc_proj, b_spread, c_spread, summed, out_proj, rows_turned, gate_proj,
                  *(n.mean for n in norms.values()), *(n.var for n in norms.values()))
            if first:
                prime(pe, tok_done, x_proj, z_proj)
            else:
                prime(pe, turned, rank_proj, xz_proj)

            def average(src, bank, sig):
                for c in half:
                    mm = nc.tensor.matmul(bank[0:F, 0:COLS], avg[:, :], src[:, c, :], start=(c == 0), stop=(c == 1))
                mm.then_inc(sig.sem, 1)

            def project(bank, m0, m1, weights, src, k):
                for c in range(k):
                    mm = nc.tensor.matmul(bank[0:m1 - m0, 0:COLS], weights[:, c, m0:m1], src[:, c, :],
                                          start=(c == 0), stop=(c == k - 1))
                return mm

            def embed(i, par, ih, part):
                if part == 0:
                    pe.wait_ge(in_landed[par].sem, in_landed[par].now(ih))
                    pe.wait_ge(bc_hi.sem, bc_hi.before(i))
                    pe.wait_ge(bc_r1.sem, bc_r1.before(i))
                    pe.wait_ge(raw_done.sem, raw_done.before(i))
                for step in range(4 * part, 4 * part + 4):
                    c, k = step // 6, step % 6
                    mm = nc.tensor.matmul(ps_f[0:F, c, 0:COLS - 4], tok_w[:, k, c * F:(c + 1) * F],
                                          patches[:, par, k, :], start=(k == 0), stop=(k == 5))
                if part == 2:
                    mm.then_inc(tok_done.sem, 1)

            def turn_moe_rows(i, c):
                if c == 0:
                    pe.wait_ge(gather_landed.sem, gather_landed.now(i))
                    pe.wait_ge(raw_done.sem, raw_done.before(i))
                else:
                    pe.wait_ge(h_done.sem, h_done.now(i, 1))
                for j in range(4):
                    mm = nc.tensor.transpose(ps_f[0:F, 0, j * ROWS:(j + 1) * ROWS],
                                             gathered[:, j, c * F:(c + 1) * F], ident[0:ROWS, 0:ROWS])
                mm.then_inc(turned.sem, 1)

            def pre_mean(i, par):
                pe.wait_ge(h_done.sem, h_done.now(i))
                average(h[:, par, :, :], ps_f[:, 0, :], norms["pre"].mean)

            def front_var(i, name):
                n = norms[name]
                pe.wait_ge(n.square.sem, n.square.now(i))
                average(sq, var_bank, n.var)

            def project_both(i, par, sig):
                for c in half:
                    m = (c if sig is x_proj else C + c) * P
                    mm = project(ps_f[:, c, :], m, m + P, in_w, xn[:, par, :, :], 2)
                mm.then_inc(sig.sem, 1)

            def project_xz(i, par, q):
                if q == 0:
                    pe.wait_ge(xn_done.sem, xn_done.now(i))
                else:
                    pe.wait_ge(xz_copied.sem, xz_copied.now(i, q))
                project(ps_f[:, 0, :], q * P, (q + 1) * P, in_w, xn[:, par, :, :], 2).then_inc(xz_proj.sem, 1)

            def front(i, par, fh, n):
                if first:
                    if n == 1:
                        pe.wait_ge(emb_done.sem, emb_done.now(i))
                        average(emb[:].rearrange("p c m t -> p c (m t)"), ps_f[:, 0, :], norms["tok"].mean)
                    if n == 2:
                        front_var(i, "tok")
                    if n == 4:
                        pre_mean(i, par)
                    if n == 5:
                        front_var(i, "pre")
                    if n == 8:
                        pe.wait_ge(pad_done.sem, pad_done.now(i))
                        project_both(i, par, z_proj)
                else:
                    if n == 1:
                        pre_mean(i, par)
                    if n in (5, 6, 7):
                        project_xz(i, par, 2 * (n - 5) + 1)
                    if n == 9:
                        pe.wait_ge(xz_copied.sem, xz_copied.now(i))
                        pe.wait_ge(u_done.sem, u_done.now(i))
                        project(ps_f[:, 0, :], 0, 48, x_w, u[:, par, :, :], C).then_inc(rank_proj.sem, 1)
                    if n == 11:
                        project_dt(i, 1)

            def project_dt(i, c):
                if c == 0:
                    pe.wait_ge(bc_hi.sem, bc_hi.now(i))
                    pe.wait_ge(bc_r1.sem, bc_r1.now(i))
                else:
                    pe.wait_ge(raw_done.sem, raw_done.now(i, c))
                nc.tensor.matmul(ps_f[0:P, 0, 0:COLS], dt_w[:, c * P:(c + 1) * P], low_rank[:, :],
                                 start=True, stop=True).then_inc(dt_proj.sem, 1)

            def front_first(i, par, n):
                if first and n == 7:
                    pe.wait_ge(xn_done.sem, xn_done.now(i))
                    project_both(i, par, x_proj)
                if first and n == 12:
                    pe.wait_ge(raw_done.sem, raw_done.now(i, 1))
                    project(ps_f[:, 0, :], 0, 32, bc_w, u[:, par, :, :], C).then_inc(bc_proj.sem, 1)
                if first and n == 11:
                    pe.wait_ge(z_copied.sem, z_copied.now(i))
                    pe.wait_ge(u_done.sem, u_done.now(i))
                    for c in half:
                        project(ps_f[:, c, :], c * P, (c + 1) * P, dt_w, u[:, par, :, :], C).then_inc(dt_proj.sem, 1)
                if not first:
                    if n == 3:
                        front_var(i, "pre")
                    if n in (5, 6, 7):
                        project_xz(i, par, 2 * (n - 5))
                    if n == 10:
                        pe.wait_ge(rank_copied.sem, rank_copied.now(i))
                        project(ps_f[:, 0, :], 48, 80, x_w, u[:, par, :, :], C).then_inc(bc_proj.sem, 1)
                    if n in (11, 12):
                        project_dt(i, 2 * (n - 11))

            def early(i, par, ih, n):
                if first and n >= 13:
                    embed(i, par, ih, n - 13)
                if not first and n in (13, 15):
                    turn_moe_rows(i, (n - 13) // 2)

            def sum_states(i, n):
                if n not in SUMMED:
                    return
                if n in JOINED:
                    pe.wait_ge(joined.sem, joined.now(i, count_to(JOINED, n)))
                else:
                    pe.wait_ge(weighed.sem, weighed.now(i, n + 1))
                if n == SUMMED[0]:
                    pe.wait_ge(skip_done.sem, skip_done.before(i))
                for c in range(C):
                    mm = nc.tensor.matmul(ps_y[0:P, c, 0:COLS], ident[0:P, 0:P], state_c[:, ring(n), c, :],
                                          start=(n == SUMMED[0]), stop=(n == SUMMED[-1]))
                mm.then_inc(summed.sem, 1)

            def spread_b(i, par, n):
                if n == 0:
                    pe.wait_ge(bc_lo.sem, bc_lo.now(i))
                    pe.wait_ge(bc_m.sem, bc_m.now(i))
                pe.wait_ge(driven.sem, driven.now(i, n - 1) if n >= 2 else driven.before(i, N_STATE - 1 + n))
                nc.tensor.matmul(ps_b[0:P, n % 2, 0:COLS], select[:, n, 0:P], bc_stack[:, par, :],
                                 start=True, stop=True).then_inc(b_spread.sem, 1)

            def scan(i, par, n, has_front, has_back):
                pe.wait_ge(c_copied.sem, c_copied.now(i, n) if n else c_copied.before(i))
                nc.tensor.matmul(ps_c[0:P, 0:COLS], select[:, N_STATE + n, 0:P], bc_stack[:, par, :],
                                 start=True, stop=True).then_inc(c_spread.sem, 1)
                if n + 1 < N_STATE:
                    spread_b(i, par, n + 1)
                if has_front:
                    front_first(i + 1, 1 - par, n)
                if n >= 2:
                    sum_states(i, n - 2)
                elif has_back:
                    sum_states(i - 1, N_STATE - 2 + n)

            def back(i, par, n):
                if n in (3, 4):
                    c = n - 3
                    if c == 0:
                        pe.wait_ge(y_done.sem, y_done.now(i))
                        pe.wait_ge(gate_done.sem, gate_done.before(i))
                    else:
                        pe.wait_ge(r_done.sem, r_done.now(i, 1))
                    project(ps_k, c * F, (c + 1) * F, out_w, y, C).then_inc(out_proj.sem, 1)
                if n == 5:
                    pe.wait_ge(r_done.sem, r_done.now(i))
                    average(r, ps_k, norms["post"].mean)
                if n == ffn_slot:
                    pe.wait_ge(h_out_done.sem, h_out_done.now(i))
                    average(h_out, ps_k, norms["ffn"].mean)
                if n in (6, ffn_slot + 1):
                    nm = norms["post" if n == 6 else "ffn"]
                    pe.wait_ge(nm.square.sem, nm.square.now(i))
                    average(sq2, ps_k, nm.var)
                t = n - turn_slot
                if 0 <= t < n_turn:
                    src = xf if t >= n_turn - 2 else h_out
                    if t == 0:
                        pe.wait_ge(norms["ffn"].log.sem, norms["ffn"].log.now(i))
                    else:
                        pe.wait_ge(rows_done.sem, rows_done.now(i, t))
                    if t == n_turn - 2:
                        pe.wait_ge(xf_done.sem, xf_done.now(i))
                    for j in half:
                        for c in half:
                            a = (2 * (t % 2) + j) * ROWS
                            mm = nc.tensor.transpose(ps_k[0:ROWS, j * D + c * F:j * D + (c + 1) * F],
                                                     src[:, c, a:a + ROWS], ident[0:F, 0:F])
                    mm.then_inc(rows_turned.sem, 1)
                if t == n_turn:
                    pe.wait_ge(rows_done.sem, rows_done.now(i))
                    for j in range(4):
                        for c in half:
                            mm = nc.tensor.matmul(ps_k[0:ROWS, j * E:(j + 1) * E], xf[:, c, j * ROWS:(j + 1) * ROWS],
                                                  gate_w[:, c, :], start=(c == 0), stop=(c == 1))
                    mm.then_inc(gate_proj.sem, 1)

            def turn(i, par, fh, eh, has_front, has_early, has_back):
                for n in range(N_STATE):
                    scan(i, par, n, has_front, has_back)
                    if has_back and n not in late:
                        back(i - 1, 1 - par, n)
                    if has_front:
                        front(i + 1, 1 - par, fh, n)
                    if has_back and n in late:
                        back(i - 1, 1 - par, n)
                    if has_early:
                        early(i + 2, par, eh, n)
                if has_front:
                    spread_b(i + 1, 1 - par, 0)

            def last_back(i, par, n):
                if n < 2:
                    sum_states(i, N_STATE - 2 + n)
                back(i, par, n)

            def first_front(i, par, fh, n):
                front_first(i, par, n)
                front(i, par, fh, n)
                if n == N_STATE - 1:
                    spread_b(i, par, 0)

            all_turns(turn, first_front, early, last_back)(pe)

        @block.scalar
        def _(act):
            act.wait_ge(loaded, n_loads)
            act.wait_ge(ready, 1)
            prime(act, u_done, z_done, raw_done, abs_done, exp_done, log_done, bc_hi, bc_m, c_copied, decayed, affine,
                  rows_done, stored, *(n.square for n in norms.values()), *(n.log for n in norms.values()),
                  *(n.rstd for n in norms.values()))
            if first:
                prime(act, h_done, pad_done, z_copied)
            else:
                prime(act, rank_copied, xz_copied)
            act.preload_act_table_set("natural_log_exp_and_others")
            nc.scalar.activation(a_neg[:].rearrange("p a b -> p (a b)"), a_log[:].rearrange("p a b -> p (a b)"),
                                 ACT.Exp).then_inc(ready, 1)
            act.wait_ge(ready, 3)

            def square(i, n, cen, sq):
                act.wait_ge(n.centred.sem, n.centred.now(i))
                nc.scalar.activation(sq[:], cen[:], ACT.Square).then_inc(n.square.sem, 1)

            def inverse_std(i, n, logv, rstd, bank):
                act.wait_ge(n.var.sem, n.var.now(i))
                nc.scalar.activation(logv[:, :], bank[0:F, 0:COLS], ACT.Ln, bias=eps[0:F, :]).then_inc(n.log.sem, 1)
                act.wait_ge(n.log.sem, n.log.now(i))
                nc.scalar.activation(rstd[:, :], logv[:, :], ACT.Exp, scale=-0.5).then_inc(n.rstd.sem, 1)

            def raw_dt(i, c):
                act.wait_ge(dt_proj.sem, dt_proj.now(i, c + 1))
                if c == 0:
                    act.wait_ge(dt_done.sem, dt_done.before(i))
                nc.scalar.activation(sp_raw[:, c, :], ps_f[0:P, c if first else 0, 0:COLS], ACT.Identity,
                                     bias=dt_bias[:, c:c + 1]).then_inc(raw_done.sem, 1)

            def split_hi(i, par, bank):
                act.wait_ge(bc_proj.sem, bc_proj.now(i))
                nc.scalar.activation(bc_stack[0:32, par, :], ps_f[0:32, bank, 0:COLS], ACT.Copy).then_inc(bc_hi.sem, 1)

            def soft_exp(i):
                act.wait_ge(raw_done.sem, raw_done.now(i))
                nc.scalar.activation(sp_abs[:], sp_raw[:], ACT.Abs).then_inc(abs_done.sem, 1)
                act.wait_ge(abs_done.sem, abs_done.now(i))
                act.wait_ge(dt_done.sem, dt_done.before(i))
                nc.scalar.activation(sp_exp[:], sp_abs[:], ACT.Exp, scale=-1.0).then_inc(exp_done.sem, 1)

            def soft_log(i, par):
                act.preload_act_table_set("natural_log")
                act.wait_ge(one_done.sem, one_done.now(i))
                act.wait_ge(exp_done.sem, exp_done.now(i))
                nc.scalar.activation(sp_abs[:], sp_one[:], ACT.Ln).then_inc(log_done.sem, 1)
                act.preload_act_table_set("natural_log_exp_and_others")

            def split_mid(i, par):
                act.wait_ge(bc_r1.sem, bc_r1.now(i))
                nc.scalar.activation(bc_mid[:, :], bc_rest[:, :], ACT.Copy).then_inc(bc_m.sem, 1)
                nc.scalar.activation(bc_stack[32:64, par, :], bc_rest[:, :], ACT.Copy).then_inc(bc_m.sem, 1)

            def front(i, par, fh, n):
                pre = norms["pre"]
                if first:
                    if n == 1:
                        square(i, norms["tok"], cen, sq)
                    if n == 2:
                        inverse_std(i, norms["tok"], logv, rstd, var_bank)
                    if n == 3:
                        act.wait_ge(tok_scaled.sem, tok_scaled.now(i))
                        if not is_first(i):
                            act.wait_ge(h_kept.sem, h_kept.before(i - 1))
                        for c in half:
                            nc.scalar.activation(
                                h[:, par, c, :].rearrange("p (m t) -> p m t", m=2)[:, :, 1:SEQ],
                                emb[:, c, :, 1:SEQ], ACT.Identity, bias=tok_beta[:, c:c + 1],
                                scale=tok_g[:, c:c + 1]).then_inc(h_done.sem, 1)
                    if n == 4:
                        square(i, pre, cen, sq)
                    if n == 5:
                        inverse_std(i, pre, logv, rstd, var_bank)
                    if n == 8:
                        act.wait_ge(z_proj.sem, z_proj.now(i))
                        nc.scalar.activation(sz[:, par, :, :], ps_f[0:P, :, 0:COLS], ACT.Copy).then_inc(z_copied.sem, 1)
                    if n == 9:
                        for c in range(C):
                            act.wait_ge(conv_done.sem, conv_done.now(i, 4 * c + 4))
                            nc.scalar.activation(u[:, par, c, :], conv[:, c, :, :].rearrange("p m t -> p (m t)"),
                                                 ACT.Silu, bias=conv_b[:, c:c + 1]).then_inc(u_done.sem, 1)
                        act.wait_ge(z_copied.sem, z_copied.now(i))
                        nc.scalar.activation(sz[:, par, :, :], sz[:, par, :, :], ACT.Silu).then_inc(z_done.sem, 1)
                        act.preload_act_table_set("natural_log_exp_and_others")
                    if n == 11:
                        raw_dt(i, 0)
                        raw_dt(i, 1)
                else:
                    if n == 1:
                        square(i, pre, cen, sq)
                    if n in (5, 6, 7):
                        copy_xz(i, par, 2 * (n - 5) + 1)
                    if n == 8:
                        act.wait_ge(xz_copied.sem, xz_copied.now(i))
                        nc.scalar.activation(u[:, par, :, :], u[:, par, :, :], ACT.Silu).then_inc(u_done.sem, 1)
                        nc.scalar.activation(sz[:, par, :, :], sz[:, par, :, :], ACT.Silu).then_inc(z_done.sem, 1)
                        act.preload_act_table_set("natural_log_exp_and_others")
                    if n == 9:
                        act.wait_ge(rank_proj.sem, rank_proj.now(i))
                        nc.scalar.activation(low_rank[:, :], ps_f[0:48, 0, 0:COLS], ACT.Copy).then_inc(rank_copied.sem, 1)
                    if n == 11:
                        raw_dt(i, 1)
                        split_mid(i, par)
                if n == 12:
                    soft_exp(i)
                if first and n == 13:
                    split_mid(i, par)
                if n == 14:
                    soft_log(i, par)

            def copy_xz(i, par, q):
                act.wait_ge(xz_proj.sem, xz_proj.now(i, q + 1))
                dst = u if q < C else sz
                nc.scalar.activation(dst[:, par, q % C, :], ps_f[0:P, 0, 0:COLS], ACT.Copy).then_inc(xz_copied.sem, 1)

            def front_first(i, par, n):
                if first and n == 7:
                    act.wait_ge(x_proj.sem, x_proj.now(i))
                    act.wait_ge(conv_done.sem, conv_done.before(i))
                    nc.scalar.activation(x_pad[:, :, :, 3:], ps_f[0:F, :, 0:COLS].rearrange(
                        "p c (m t) -> p c m t", m=2), ACT.Copy).then_inc(pad_done.sem, 1)
                if first and n == 12:
                    split_hi(i, par, 0)
                if not first:
                    if n == 3:
                        inverse_std(i, norms["pre"], logv, rstd, var_bank)
                    if n in (5, 6, 7):
                        copy_xz(i, par, 2 * (n - 5))
                    if n == 10:
                        split_hi(i, par, 0)
                    if n in (11, 12):
                        raw_dt(i, 2 * (n - 11))

            def decay_state(i, par, n):
                if n == 0:
                    act.wait_ge(dt_done.sem, dt_done.now(i))
                act.wait_ge(scanned.sem, ring_free(scanned, i, n))
                for c in range(C):
                    nc.scalar.activation(
                        decay[:, ring(n), c, :].rearrange("p (m t) -> p m t", m=2)[:, :, 1:SEQ],
                        dt[:, par, c, :].rearrange("p (m t) -> p m t", m=2)[:, :, 1:SEQ],
                        ACT.Exp, scale=a_neg[:, c, n:n + 1]).then_inc(decayed.sem, 1)

            def scan(i, par, n):
                act.wait_ge(c_spread.sem, c_spread.now(i, n + 1))
                act.wait_ge(weighed.sem, ring_free(weighed, i, n))
                nc.scalar.activation(c_sb[:, ring(n), :], ps_c[0:P, 0:COLS], ACT.Copy).then_inc(c_copied.sem, 1)
                if n + 1 < N_STATE:
                    decay_state(i, par, n + 1)

            def back(i, par, n):
                if n == 5:
                    square(i, norms["post"], cen2, sq2)
                if n == 6:
                    inverse_std(i, norms["post"], logv2, rstd2, ps_k)
                if n == 7:
                    act.wait_ge(r_scaled.sem, r_scaled.now(i))
                    for c in half:
                        nc.scalar.activation(normed[:, c, :], r[:, c, :], ACT.Identity, bias=ln_b[:, c:c + 1],
                                             scale=ln_g[:, c:c + 1]).then_inc(affine.sem, 1)
                if n == ffn_slot:
                    square(i, norms["ffn"], cen2, sq2)
                if n == ffn_slot + 1:
                    inverse_std(i, norms["ffn"], logv2, rstd2, ps_k)
                t = n - turn_slot
                if 0 <= t < n_turn:
                    act.wait_ge(rows_turned.sem, rows_turned.now(i, t + 1))
                    if t == 0:
                        act.wait_ge(stored.sem, stored.before(i))
                    dst = rows if t >= n_turn - 2 else rows_h
                    nc.scalar.activation(dst[:, 2 * (t % 2):2 * (t % 2) + 2, :].rearrange("p a b -> p (a b)"),
                                         ps_k[0:ROWS, 0:2 * D], ACT.Copy).then_inc(rows_done.sem, 1)
                if n == 15:
                    if first:
                        act.wait_ge(h_out_done.sem, h_out_done.now(i))
                        act.dma_start(dram["h0"][i, :, :], h_out[:].rearrange("p a b -> p (a b)")).then_inc(stored.sem, 16)
                    act.wait_ge(rows_done.sem, rows_done.now(i))
                    if not first:
                        act.dma_start(dram["h1"][i, :, :], rows_h[:].rearrange("p a b -> p (a b)")).then_inc(stored.sem, 16)
                    act.dma_start(dram[f"xf{T}"][i, :, :], rows[:].rearrange("p a b -> p (a b)")).then_inc(stored.sem, 16)

            def turn(i, par, fh, eh, has_front, has_early, has_back):
                for n in range(N_STATE):
                    scan(i, par, n)
                    if has_front:
                        front_first(i + 1, 1 - par, n)
                    if has_back and n not in late:
                        back(i - 1, 1 - par, n)
                    if has_front:
                        front(i + 1, 1 - par, fh, n)
                    if has_back and n in late:
                        back(i - 1, 1 - par, n)
                if has_front:
                    decay_state(i + 1, 1 - par, 0)

            def first_front(i, par, fh, n):
                front_first(i, par, n)
                front(i, par, fh, n)
                if n == N_STATE - 1:
                    decay_state(i, par, 0)

            all_turns(turn, first_front, nothing, back)(act)
            act.wait_ge(stored.sem, stored.now(pairs - 1))

        @block.gpsimd
        def _(pool):
            prime(pool, weighed, joined)

            def gather(i):
                pool.wait_ge(ix_done.sem, ix_done.now(i))
                pool.wait_ge(turned.sem, turned.before(i))
                pool.sem_inc(waited, 1)
                for j in range(4):
                    pool.indirect_dma_start(
                        out=gathered[:, j, :], out_offset=None, in_=dram["moe_out0"],
                        in_offset=bass.IndirectOffsetOnAxis(ap=slot_ix[:, j:j + 1], axis=0)).then_inc(gather_landed.sem, 16)

            def scan(i, n):
                pool.wait_ge(scanned.sem, scanned.now(i, n + 1))
                pool.wait_ge(c_copied.sem, c_copied.now(i, n + 1))
                last = max(m for m in (range(N_STATE) if n < RING else range(n)) if ring(m) == ring(n))
                used, k = (joined, count_to(JOINED, last + 1)) if last + 1 in JOINED else (summed, count_to(SUMMED, last))
                pool.wait_ge(used.sem, used.before(i, k) if n < RING else used.now(i, k))
                nc.gpsimd.tensor_tensor(state_c[:, ring(n), :, :], state[:, ring(n), :, :],
                                        c_sb[:, ring(n), :].unsqueeze(1).to_broadcast([P, C, COLS]),
                                        ALU.mult).then_inc(weighed.sem, 1)
                if n in JOINED:
                    pool.wait_ge(weighed.sem, weighed.now(i, n + 1))
                    nc.gpsimd.tensor_tensor(state_c[:, ring(n), :, :], state_c[:, ring(n), :, :],
                                            state_c[:, ring(n - 1), :, :], ALU.add).then_inc(joined.sem, 1)

            def early(i, par, ih, n):
                if not first and n == 8:
                    gather(i)

            def turn(i, par, fh, eh, has_front, has_early, has_back):
                for n in range(N_STATE):
                    scan(i, n)
                    if has_early:
                        early(i + 2, par, eh, n)

            all_turns(turn, nothing, early, nothing)(pool)

        @block.vector
        def _(dve):
            nc.vector.memset(eps[:, :], EPS).then_inc(ready, 1)
            chain = [0]

            def link(ins):
                chain[0] += 1
                ins.then_inc(setup, 1)
                dve.wait_ge(setup, chain[0])

            link(nc.vector.memset(decay[:].rearrange("p a b c -> p (a b c)"), 0.0))
            dve.wait_ge(loaded, n_loads)
            if first:
                link(nc.vector.memset(x_pad[:].rearrange("p a b c -> p (a b c)"), 0.0))
                for c in half:
                    link(nc.vector.tensor_scalar(pos[:, c, 1:], pos[:, c, 1:], tok_b[:, c:c + 1], None, ALU.add))
                    for m in half:
                        link(nc.vector.tensor_tensor(emb[:, c, m, 1:2], pos[:, c, 0:1], class_token[:, c:c + 1], ALU.add))
                        link(nc.vector.tensor_copy(emb[:, c, m, 0:1], cls_tok[:, c:c + 1]))
                        for par in half:
                            link(nc.vector.tensor_copy(h[:, par, c, m * SEQ:m * SEQ + 1], cls_tok[:, c:c + 1]))
                link(nc.vector.tensor_copy(cls_emb[:].rearrange("p c m t -> p (c m) t"),
                                           emb[:, :, :, 0:2].rearrange("p c m t -> p (c m) t")))
            prime(dve, gate_done, xn_done, one_done, corr_done, sum_done, dt_done, du_done, bc_r1, bc_lo, driven, scanned,
                  skip_done, y_done, r_done, r_scaled, h_out_done, xf_done, h_kept, *(n.centred for n in norms.values()))
            if first:
                prime(dve, emb_done, emb_cls, tok_scaled, conv_done)
            else:
                prime(dve, h_done, ix_done)
            dve.wait_ge(ready, 2)
            nc.vector.tensor_scalar(a_neg[:].rearrange("p a b -> p (a b)"), a_neg[:].rearrange("p a b -> p (a b)"),
                                    -1.0, None, ALU.mult).then_inc(ready, 1)

            def wide(t):
                return t.unsqueeze(1).to_broadcast([t.shape[0], 2, COLS])

            def centre(n, i, src, cen, bank):
                dve.wait_ge(n.mean.sem, n.mean.now(i))
                nc.vector.tensor_tensor(cen[:], src, wide(bank[0:F, 0:COLS]), ALU.subtract).then_inc(n.centred.sem, 1)

            def scale(n, i, dst, cen, rstd, sig):
                dve.wait_ge(n.rstd.sem, n.rstd.now(i))
                nc.vector.tensor_tensor(dst, cen[:], wide(rstd[:, :]), ALU.mult).then_inc(sig.sem, 1)

            def add_positions(i):
                dve.wait_ge(tok_done.sem, tok_done.now(i))
                dve.wait_ge(h_done.sem, h_done.before(i))
                nc.vector.tensor_copy(emb[:, :, :, 0:2].rearrange("p c m t -> p (c m) t"),
                                      cls_emb[:].rearrange("p c m t -> p (c m) t")).then_inc(emb_cls.sem, 1)
                nc.vector.tensor_tensor(
                    emb[:, :, :, 2:], ps_f[0:F, :, 0:COLS - 4].rearrange("p c (m t) -> p c m t", m=2),
                    pos[:, :, 1:].unsqueeze(2).to_broadcast([F, 2, 2, SEQ - 2]), ALU.add).then_inc(emb_done.sem, 1)

            def convolve(i, c, taps):
                for k in taps:
                    if k == 0:
                        dve.wait_ge(pad_done.sem, pad_done.now(i))
                        dve.wait_ge(u_done.sem, u_done.before(i))
                        nc.vector.tensor_scalar(conv[:, c, :, :], x_pad[:, c, :, 0:SEQ], conv_w[:, c, 0:1], None,
                                                ALU.mult).then_inc(conv_done.sem, 1)
                    else:
                        dve.wait_ge(conv_done.sem, conv_done.now(i, 4 * c + k))
                        nc.vector.scalar_tensor_tensor(
                            out=conv[:, c, :, :], in0=x_pad[:, c, :, k:k + SEQ], scalar=conv_w[:, c, k:k + 1],
                            in1=conv[:, c, :, :], op0=ALU.mult, op1=ALU.add).then_inc(conv_done.sem, 1)

            def split_rest(i, par, bank):
                dve.wait_ge(bc_hi.sem, bc_hi.now(i))
                dve.wait_ge(bc_lo.sem, bc_lo.before(i))
                nc.vector.tensor_tensor(bc_rest[:, :], ps_f[0:32, bank, 0:COLS], bc_stack[0:32, par, :],
                                        ALU.subtract).then_inc(bc_r1.sem, 1)

            def one_plus(i):
                dve.wait_ge(exp_done.sem, exp_done.now(i))
                nc.vector.tensor_scalar(sp_one[:], sp_exp[:], 1.0, None, ALU.add).then_inc(one_done.sem, 1)

            def norm_stream(i, par):
                if not is_first(i):
                    dve.wait_ge(r_done.sem, r_done.before(i - 1))
                scale(norms["pre"], i, xn[:, par, :, :], cen, rstd, xn_done)

            def time_steps(i, par, n):
                if n == 13:
                    dve.wait_ge(one_done.sem, one_done.now(i))
                    nc.vector.scalar_tensor_tensor(out=sp_exp[:], in0=sp_one[:], scalar=1.0, in1=sp_exp[:],
                                                   op0=ALU.subtract, op1=ALU.subtract).then_inc(corr_done.sem, 1)
                if n == 14:
                    dve.wait_ge(corr_done.sem, corr_done.now(i))
                    dve.wait_ge(raw_done.sem, raw_done.now(i))
                    nc.vector.scalar_tensor_tensor(out=sp_exp[:], in0=sp_raw[:], scalar=0.0, in1=sp_exp[:],
                                                   op0=ALU.max, op1=ALU.subtract).then_inc(sum_done.sem, 1)
                    dve.wait_ge(bc_m.sem, bc_m.now(i))
                    nc.vector.tensor_tensor(bc_stack[64:96, par, :], bc_rest[:, :], bc_mid[:, :],
                                            ALU.subtract).then_inc(bc_lo.sem, 1)
                if n == 15:
                    dve.wait_ge(sum_done.sem, sum_done.now(i))
                    dve.wait_ge(log_done.sem, log_done.now(i))
                    nc.vector.tensor_tensor(dt[:, par, :, :], sp_abs[:], sp_exp[:], ALU.add).then_inc(dt_done.sem, 1)
                    dve.wait_ge(dt_done.sem, dt_done.now(i))
                    dve.wait_ge(u_done.sem, u_done.now(i))
                    nc.vector.tensor_tensor(du[:, par, :, :], dt[:, par, :, :], u[:, par, :, :],
                                            ALU.mult).then_inc(du_done.sem, 1)

            def front(i, par, fh, n):
                pre = norms["pre"]
                hp = h[:, par, :, :]
                if first:
                    tok = norms["tok"]
                    e = emb[:].rearrange("p c m t -> p c (m t)")
                    if n == 0:
                        add_positions(i)
                    if n == 1:
                        dve.wait_ge(emb_cls.sem, emb_cls.now(i))
                        dve.wait_ge(emb_done.sem, emb_done.now(i))
                        centre(tok, i, e, cen, ps_f[:, 0, :])
                    if n == 3:
                        scale(tok, i, e, cen, rstd, tok_scaled)
                    if n == 4:
                        centre(pre, i, hp, cen, ps_f[:, 0, :])
                    if n == 6:
                        norm_stream(i, par)
                    if n == 7:
                        convolve(i, 0, range(4))
                    if n in (8, 9):
                        convolve(i, 1, range(2 * (n - 8), 2 * (n - 8) + 2))
                    if n == 12:
                        split_rest(i, par, 0)
                else:
                    if n == 0:
                        add_moe_rows(i, par, fh, 1)
                    if n == 1:
                        dve.wait_ge(h_done.sem, h_done.now(i))
                        centre(pre, i, hp, cen, ps_f[:, 0, :])
                    if n == 4:
                        norm_stream(i, par)
                    if n == 10:
                        split_rest(i, par, 0)
                if n in (13, 14, 15):
                    time_steps(i, par, n)

            def add_moe_rows(i, par, ih, c):
                dve.wait_ge(turned.sem, turned.now(i, c + 1))
                if c == 0:
                    dve.wait_ge(in_landed[par].sem, in_landed[par].now(ih))
                nc.vector.tensor_tensor(h[:, par, c, :], h[:, par, c, :], ps_f[0:F, 0, 0:COLS],
                                        ALU.add).then_inc(h_done.sem, 1)

            def slot_indices(i):
                nc.vector.tensor_copy(slot_ix[:, :], slots[:, bass.ds(i * 4, 4)]).then_inc(ix_done.sem, 1)

            def scan(i, par, n):
                if n == 0:
                    dve.wait_ge(du_done.sem, du_done.now(i))
                dve.wait_ge(b_spread.sem, b_spread.now(i, n + 1))
                dve.wait_ge(scanned.sem, scanned.now(i, n - 1) if n >= 2 else scanned.before(i, N_STATE + n - 1))
                nc.vector.tensor_tensor(drive[:, n % 2, :, :], du[:, par, :, :],
                                        ps_b[0:P, n % 2, 0:COLS].unsqueeze(1).to_broadcast([P, C, COLS]),
                                        ALU.mult).then_inc(driven.sem, 1)
                dve.wait_ge(driven.sem, driven.now(i, n + 1))
                dve.wait_ge(decayed.sem, decayed.now(i, C * (n + 1)))
                dve.wait_ge(weighed.sem, ring_free(weighed, i, n))
                nc.vector.tensor_tensor_scan(
                    state[:, ring(n), :, :].rearrange("p a b -> p (a b)"),
                    decay[:, ring(n), :, :].rearrange("p a b -> p (a b)"),
                    drive[:, n % 2, :, :].rearrange("p a b -> p (a b)"), 0.0, ALU.mult, ALU.add).then_inc(scanned.sem, 1)

            def back(i, par, n):
                post, ffn = norms["post"], norms["ffn"]
                if n == 2:
                    dve.wait_ge(summed.sem, summed.now(i))
                    dve.wait_ge(out_proj.sem, out_proj.before(i))
                    for c in range(C):
                        nc.vector.scalar_tensor_tensor(out=y[:, c, :], in0=u[:, par, c, :], scalar=skip_w[:, c:c + 1],
                                                       in1=ps_y[0:P, c, 0:COLS], op0=ALU.mult,
                                                       op1=ALU.add).then_inc(skip_done.sem, 1)
                    dve.wait_ge(skip_done.sem, skip_done.now(i))
                    dve.wait_ge(z_done.sem, z_done.now(i))
                    nc.vector.tensor_tensor(y[:], y[:], sz[:, par, :, :], ALU.mult).then_inc(y_done.sem, 1)
                if n in (3, 4):
                    c = n - 3
                    dve.wait_ge(out_proj.sem, out_proj.now(i, c + 1))
                    dve.wait_ge(affine.sem, affine.before(i))
                    nc.vector.tensor_tensor(r[:, c, :], ps_k[0:F, 0:COLS], xn[:, par, c, :], ALU.add).then_inc(r_done.sem, 1)
                if n == 5:
                    dve.wait_ge(r_done.sem, r_done.now(i))
                    centre(post, i, r[:], cen2, ps_k)
                if n == 7:
                    scale(post, i, r[:], cen2, rstd2, r_scaled)
                if n == ffn_slot - 1:
                    dve.wait_ge(affine.sem, affine.now(i))
                    dve.wait_ge(stored.sem, stored.before(i))
                    dve.wait_ge(rows_turned.sem, rows_turned.before(i))
                    dve.wait_ge(h_kept.sem, h_kept.now(i))
                    nc.vector.tensor_tensor(h_out[:], h_keep[:], normed[:], ALU.add).then_inc(h_out_done.sem, 1)
                if n == ffn_slot:
                    dve.wait_ge(h_out_done.sem, h_out_done.now(i))
                    centre(ffn, i, h_out[:], cen2, ps_k)
                if n == ffn_slot + 2:
                    dve.wait_ge(gate_proj.sem, gate_proj.before(i))
                    scale(ffn, i, xf[:], cen2, rstd2, xf_done)
                if n == turn_slot + n_turn:
                    dve.wait_ge(gate_proj.sem, gate_proj.now(i))
                    dst = logits[:, bass.ds(i * 4, 4), 0:E]
                    src = ps_k[0:ROWS, 0:4 * E].rearrange("p (j e) -> p j e", e=E)
                    if first:
                        nc.vector.tensor_tensor(dst, src, gate_b[:, :].unsqueeze(1).to_broadcast([ROWS, 4, E]),
                                                ALU.add).then_inc(gate_done.sem, 1)
                    else:
                        nc.vector.tensor_copy(dst, src).then_inc(gate_done.sem, 1)

            def early(i, par, ih, n):
                if not first and n == 7:
                    slot_indices(i)
                if not first and n == 14:
                    add_moe_rows(i, par, ih, 0)

            def turn(i, par, fh, eh, has_front, has_early, has_back):
                for n in range(N_STATE):
                    scan(i, par, n)
                    if n == 13 and has_front:
                        one_plus(i + 1)
                    after_front = (15,)
                    if has_back and n not in after_front:
                        back(i - 1, 1 - par, n)
                    if n == 10:
                        dve.wait_ge(h_out_done.sem, h_out_done.before(i))
                        nc.vector.tensor_copy(h_keep[:], h[:, par, :, :]).then_inc(h_kept.sem, 1)
                    if has_front:
                        front(i + 1, 1 - par, fh, n)
                    if has_back and n in after_front:
                        back(i - 1, 1 - par, n)
                    if has_early:
                        early(i + 2, par, eh, n)

            def first_front(i, par, fh, n):
                if n == 13:
                    one_plus(i)
                front(i, par, fh, n)

            all_turns(turn, first_front, early, back)(dve)


TOP = (1, 2)
EXPERTS = (4, 8)
BLOCKS = tuple(TOKENS * TOP[t] // COLS + EXPERTS[t] - 1 for t in (0, 1))
BISECT = 24


def route(nc, held, layer, dram, logits, slots_in, slots_out, weights, expert_of):
    E, K = EXPERTS[layer], TOP[layer]
    NB = BLOCKS[layer]
    DROP = NB * COLS
    T = str(layer)
    with ExitStack() as ctx:
        def sb(name, shape, dt=F32):
            return ctx.enter_context(nc.sbuf_tensor(f"r{T}_{name}", shape, dt))

        def sem(name):
            return held.take(nc, f"r{T}_{name}")

        earlier = sb("earlier", [ROWS, ROWS])
        ones = sb("ones", [ROWS, ROWS])
        steps = sb("steps", [ROWS, 32])
        numbers = sb("numbers", [ROWS, BLOCKS[1]])
        token_of = sb("token_of", [ROWS, TILES])
        zeros = sb("zeros", [ROWS, 4 * D])
        best = sb("best", [ROWS, K, TILES])
        free = sb("free", [ROWS, TILES])
        work = sb("work", [ROWS, E, TILES])
        equal = sb("equal", [ROWS, E, TILES])
        chosen = sb("chosen", [ROWS, K, E, TILES])
        keep = sb("keep", [ROWS, E, TILES])
        score = sb("score", [ROWS, E, TILES])
        flags = sb("flags", [ROWS, E, TILES])
        flags2 = sb("flags2", [ROWS, E, TILES])
        restart = sb("restart", [ROWS, E, TILES])
        run = sb("run", [ROWS, E, TILES])
        place = sb("place", [ROWS, E, TILES])
        bar = sb("bar", [ROWS, E])
        cand = sb("cand", [ROWS, E])
        step = sb("step", [ROWS, 1])
        part = sb("part", [ROWS, E])
        quota = sb("quota", [ROWS, E])
        over = sb("over", [ROWS, E, 32])
        n_blocks = sb("n_blocks", [ROWS, E])
        ends = sb("ends", [ROWS, E])
        base = sb("base", [ROWS, E])
        owner = sb("owner", [ROWS, NB, E])
        kept = sb("kept", [ROWS, TILES])
        spot = sb("spot", [ROWS, TILES])
        lost = sb("lost", [ROWS, TILES])
        ratio = sb("ratio", [ROWS, TILES])
        rows = sb("rows", [ROWS, 2, 4, D])
        index = sb("index", [ROWS, 2, K, 4], U32)

        ps_sum = ctx.enter_context(nc.psum_tensor(f"r{T}_ps_sum", [128, BANK], F32))
        ps_tile = ctx.enter_context(nc.psum_tensor(f"r{T}_ps_tile", [128, 2, BANK], F32))
        ps_in = ctx.enter_context(nc.psum_tensor(f"r{T}_ps_in", [128, 2, BANK], F32))

        loaded = sem("loaded")
        waited = sem("waited")
        dve_step = sem("dve_step")
        gap_ready = sem("gap_ready")
        exp_ready = sem("exp_ready")
        zeros_ready = sem("zeros_ready")
        zeroed = sem("zeroed")
        slots_ready = sem("slots_ready")
        rounds_counted = Signal(nc, held, f"r{T}_rounds_counted")
        rounds_summed = Signal(nc, held, f"r{T}_rounds_summed")
        flags_ready = sem("flags_ready")
        prefix_ready = sem("prefix_ready")
        rows_landed = [Signal(nc, held, f"r{T}_rows_landed_{p}", 1, 16) for p in (0, 1)]
        index_ready = Signal(nc, held, f"r{T}_index_ready")
        scattered = [Signal(nc, held, f"r{T}_scattered_{p}", 4 * K, 16, primed=False) for p in (0, 1)]
        halves = range((E * TILES + BANK - 1) // BANK)
        wide = E * TILES // len(halves)

        block = ctx.enter_context(nc.Block())

        @block.sync
        def _(sp):
            loads = [(earlier[:, :], dram["earlier"]), (ones[:, :], dram["ones"]), (steps[:, :], dram["steps"]),
                     (numbers[:, :], dram["numbers"]), (token_of[:, :], dram["token_of"])]
            load_all(sp, loads, loaded)
            prime(sp, *rows_landed)
            sp.wait_ge(zeros_ready, 1)
            sp.dma_start(dram["moe_out" + T][DROP:DROP + 1, :], zeros[0:1, 0:D]).then_inc(zeroed, 16)
            with sp.Fori(0, NB) as b:
                sp.dma_start(dram["moe_in" + T][bass.ds(b * COLS, COLS), :].rearrange("(p j) d -> p (j d)", j=4),
                             zeros[:, :]).then_inc(zeroed, 16)

            def fetch(i, par):
                sp.dma_start(rows[:, par, :, :].rearrange("p a b -> p (a b)"),
                             dram["xf" + T][i, :, :]).then_inc(rows_landed[par].sem, 16)

            fetch(0, 0)
            fetch(1, 1)
            with sp.Fori(1, PAIRS // 2) as ii:
                for par in (0, 1):
                    sp.wait_ge(scattered[par].sem, scattered[par].before(ii))
                    sp.dma_start(rows[:, par, :, :].rearrange("p a b -> p (a b)"),
                                 dram["xf" + T][2 * ii + par, :, :]).then_inc(rows_landed[par].sem, 16)

        @block.scalar
        def _(act):
            if K == 2:
                act.wait_ge(gap_ready, 1)
                nc.scalar.activation(ratio[:, :], lost[:, :], ACT.Exp).then_inc(exp_ready, 1)

        @block.tensor
        def _(pe):
            pe.wait_ge(loaded, 16 * 5)
            prime(pe, rounds_summed)
            if K == 2:
                with pe.Fori(0, BISECT + 1) as r:
                    pe.wait_ge(rounds_counted.sem, rounds_counted.now(r))
                    nc.tensor.matmul(ps_sum[0:ROWS, 0:E], ones[:, :], part[:, :], start=True,
                                     stop=True).then_inc(rounds_summed.sem, 1)

            for turn in range(K):
                pe.wait_ge(flags_ready, turn + 1)
                source = flags if turn < K - 1 else keep
                source = source[:].rearrange("p e t -> p (e t)")
                for x in halves:
                    nc.tensor.matmul(ps_in[0:ROWS, x, 0:wide], earlier[:, :], source[:, x * wide:(x + 1) * wide],
                                     start=True, stop=True)
                    mm = nc.tensor.matmul(ps_tile[0:ROWS, x, 0:wide], ones[:, :], source[:, x * wide:(x + 1) * wide],
                                          start=True, stop=True)
                mm.then_inc(prefix_ready, 1)

        @block.vector
        def _(dve):
            count = [0]

            def link(ins):
                count[0] += 1
                ins.then_inc(dve_step, 1)
                dve.wait_ge(dve_step, count[0])

            def over_experts(t):
                return t.unsqueeze(1).to_broadcast([ROWS, E, TILES])

            def over_tiles(t):
                return t.unsqueeze(2).to_broadcast([ROWS, E, TILES])

            nc.vector.memset(zeros[:, :], 0.0).then_inc(zeros_ready, 1)
            link(nc.vector.memset(restart[:].rearrange("p e t -> p (e t)"), 1.0))
            link(nc.vector.memset(restart[:, :, 0:1], 0.0))
            by_expert = logits[:, :, 0:E].rearrange("p t e -> p e t")
            for k in range(K):
                if k == 0:
                    link(nc.vector.tensor_copy(work[:], by_expert))
                else:
                    link(nc.vector.scalar_tensor_tensor(
                        out=work[:].rearrange("p e t -> p (e t)"),
                        in0=chosen[:, 0, :, :].rearrange("p e t -> p (e t)"), scalar=-3.0e38,
                        in1=work[:].rearrange("p e t -> p (e t)"), op0=ALU.mult, op1=ALU.add))
                link(nc.vector.tensor_reduce(best[:, k, :], work[:].rearrange("p e t -> p t e"), AX.X, ALU.max))
                link(nc.vector.tensor_tensor(equal[:], work[:], over_experts(best[:, k, :]), ALU.is_equal))
                link(nc.vector.memset(free[:, :], 1.0))
                for e in range(E):
                    link(nc.vector.tensor_tensor(chosen[:, k, e, :], equal[:, e, :], free[:, :], ALU.mult))
                    link(nc.vector.tensor_tensor(free[:, :], free[:, :], chosen[:, k, e, :], ALU.subtract))

            def prefix(turn):
                dve.wait_ge(prefix_ready, turn + 1)
                for x in halves:
                    part_ = slice(x * wide, (x + 1) * wide)
                    flat = [t[:].rearrange("p e t -> p (e t)")[:, part_] for t in (restart, run, place)]
                    link(nc.vector.tensor_tensor_scan(flat[1], flat[0], ps_tile[0:ROWS, x, 0:wide], 0.0,
                                                      ALU.mult, ALU.add))
                    link(nc.vector.tensor_tensor(flat[2], flat[1], ps_tile[0:ROWS, x, 0:wide], ALU.subtract))
                    link(nc.vector.tensor_tensor(flat[2], flat[2], ps_in[0:ROWS, x, 0:wide], ALU.add))

            if K == 2:
                nc.vector.tensor_tensor(lost[:, :], best[:, 1, :], best[:, 0, :], ALU.subtract).then_inc(gap_ready, 1)
                dve.wait_ge(exp_ready, 1)
                link(nc.vector.tensor_scalar(kept[:, :], ratio[:, :], 1.0, None, ALU.add))
                link(nc.vector.reciprocal(weights[:, 0, :], kept[:, :]))
                link(nc.vector.tensor_tensor(weights[:, 1, :], weights[:, 0, :], ratio[:, :], ALU.mult))
                link(nc.vector.tensor_scalar(spot[:, :], weights[:, 0, :], 0.5, None, ALU.max))
                link(nc.vector.tensor_tensor(score[:], chosen[:, 0, :, :], chosen[:, 1, :, :], ALU.add))
                link(nc.vector.tensor_tensor(score[:], score[:], over_experts(spot[:, :]), ALU.mult))
                link(nc.vector.memset(bar[:, :], 0.5))
                link(nc.vector.memset(step[:, :], 0.5))
                prime(dve, rounds_counted)
                start = count[0]
                with dve.Fori(0, BISECT) as r:
                    turn = r * 5 + start
                    nc.vector.tensor_scalar(cand[:, :], bar[:, :], step[:, 0:1], None, ALU.add).then_inc(dve_step, 1)
                    dve.wait_ge(dve_step, turn + 1)
                    nc.vector.tensor_tensor(flags[:], score[:], over_tiles(cand[:, :]), ALU.is_ge).then_inc(dve_step, 1)
                    dve.wait_ge(dve_step, turn + 2)
                    nc.vector.tensor_reduce(part[:, :], flags[:], AX.X, ALU.add).then_inc(rounds_counted.sem, 1)
                    dve.wait_ge(rounds_summed.sem, rounds_summed.now(r))
                    nc.vector.tensor_scalar(quota[:, :], ps_sum[0:ROWS, 0:E], float(CAP), step[:, 0:1],
                                            ALU.is_ge, ALU.mult).then_inc(dve_step, 1)
                    dve.wait_ge(dve_step, turn + 3)
                    nc.vector.tensor_tensor(bar[:, :], bar[:, :], quota[:, :], ALU.add).then_inc(dve_step, 1)
                    dve.wait_ge(dve_step, turn + 4)
                    nc.vector.tensor_scalar(step[:, :], step[:, :], 0.5, None, ALU.mult).then_inc(dve_step, 1)
                    dve.wait_ge(dve_step, turn + 5)
                count[0] = start + 5 * BISECT
                link(nc.vector.tensor_tensor(flags2[:], score[:], over_tiles(bar[:, :]), ALU.is_gt))
                nc.vector.tensor_reduce(part[:, :], flags2[:], AX.X, ALU.add).then_inc(rounds_counted.sem, 1)
                nc.vector.tensor_tensor(flags[:], score[:], over_tiles(bar[:, :]), ALU.is_equal).then_inc(flags_ready, 1)
                dve.wait_ge(rounds_summed.sem, rounds_summed.now(BISECT))
                link(nc.vector.tensor_scalar(quota[:, :], ps_sum[0:ROWS, 0:E], -1.0, float(CAP), ALU.mult, ALU.add))
                prefix(0)
                link(nc.vector.tensor_tensor(place[:], place[:], over_tiles(quota[:, :]), ALU.is_lt))
                link(nc.vector.tensor_tensor(place[:], place[:], flags[:], ALU.mult))
                nc.vector.tensor_tensor(keep[:], place[:], flags2[:], ALU.add).then_inc(flags_ready, 1)
            else:
                nc.vector.tensor_copy(keep[:], chosen[:, 0, :, :]).then_inc(flags_ready, 1)
            prefix(K - 1)
            totals = run[:, :, TILES - 1:TILES].to_broadcast([ROWS, E, 32])
            dve.wait_ge(loaded, 16 * 5)
            link(nc.vector.tensor_tensor(over[:], totals, steps[:, :].unsqueeze(1).to_broadcast([ROWS, E, 32]),
                                         ALU.is_gt))
            link(nc.vector.tensor_reduce(n_blocks[:, :], over[:], AX.X, ALU.add))
            link(nc.vector.tensor_copy(ends[:, 0:1], n_blocks[:, 0:1]))
            for e in range(1, E):
                link(nc.vector.tensor_tensor(ends[:, e:e + 1], ends[:, e - 1:e], n_blocks[:, e:e + 1], ALU.add))
            link(nc.vector.tensor_tensor(base[:, :], ends[:, :], n_blocks[:, :], ALU.subtract))
            link(nc.vector.tensor_scalar(base[:, :], base[:, :], float(COLS), None, ALU.mult))
            link(nc.vector.tensor_tensor(owner[:], numbers[:, 0:NB].unsqueeze(2).to_broadcast([ROWS, NB, E]),
                                         ends[:, :].unsqueeze(1).to_broadcast([ROWS, NB, E]), ALU.is_ge))
            link(nc.vector.tensor_reduce(kept[:, 0:NB], owner[:], AX.X, ALU.add))
            link(nc.vector.tensor_scalar(expert_of[:, 0:NB], kept[0:1, 0:NB], float(E - 1), None, ALU.min))
            link(nc.vector.tensor_tensor(place[:], place[:], over_tiles(base[:, :]), ALU.add))
            for k in range(K):
                link(nc.vector.tensor_tensor(flags[:], chosen[:, k, :, :], keep[:], ALU.mult))
                link(nc.vector.tensor_reduce(kept[:, :], flags[:].rearrange("p e t -> p t e"), AX.X, ALU.add))
                link(nc.vector.tensor_tensor(flags[:], flags[:], place[:], ALU.mult))
                link(nc.vector.tensor_reduce(spot[:, :], flags[:].rearrange("p e t -> p t e"), AX.X, ALU.add))
                if K == 2:
                    link(nc.vector.tensor_tensor(weights[:, k, :], weights[:, k, :], kept[:, :], ALU.mult))
                link(nc.vector.tensor_scalar(kept[:, :], kept[:, :], -1.0, 1.0, ALU.mult, ALU.add))
                link(nc.vector.scalar_tensor_tensor(out=slots_in[:, k, :], in0=kept[:, :], scalar=float(DROP),
                                                    in1=spot[:, :], op0=ALU.mult, op1=ALU.add))
                link(nc.vector.tensor_scalar(lost[:, :], token_of[:, :], float(DROP + k * TOKENS), None, ALU.add))
                link(nc.vector.tensor_tensor(lost[:, :], lost[:, :], kept[:, :], ALU.mult))
                link(nc.vector.tensor_tensor(slots_out[:, k, :], lost[:, :], spot[:, :], ALU.add))
            prime(dve, index_ready)
            for par in (0, 1):
                nc.vector.tensor_copy(index[:, par, :, :], slots_out[:, :, 4 * par:4 * par + 4]).then_inc(index_ready.sem, 1)
            with dve.Fori(1, PAIRS // 2) as ii:
                for par in (0, 1):
                    i = 2 * ii + par
                    dve.wait_ge(scattered[par].sem, scattered[par].before(ii))
                    nc.vector.tensor_copy(index[:, par, :, :], slots_out[:, :, bass.ds(i * 4, 4)]).then_inc(index_ready.sem, 1)

        @block.gpsimd
        def _(pool):
            pool.wait_ge(zeroed, 16 * (NB + 1))
            with pool.Fori(0, PAIRS // 2) as ii:
                for par in (0, 1):
                    i = 2 * ii + par
                    pool.wait_ge(rows_landed[par].sem, rows_landed[par].now(ii))
                    pool.wait_ge(index_ready.sem, index_ready.now(i))
                    pool.sem_inc(waited, 1)
                    for j in range(4):
                        for k in range(K):
                            pool.indirect_dma_start(
                                out=dram["moe_in" + T], in_=rows[:, par, j, :], in_offset=None,
                                out_offset=bass.IndirectOffsetOnAxis(ap=index[:, par, k, j:j + 1], axis=0),
                            ).then_inc(scattered[par].sem, 16)
            for par in (0, 1):
                pool.wait_ge(scattered[par].sem, scattered[par].now(PAIRS // 2 - 1))


def moe(nc, held, layer, dram, expert_of):
    NB = BLOCKS[layer]
    T = str(layer)
    E = EXPERTS[layer]
    KC = HID // 128
    with ExitStack() as ctx:
        def sb(name, shape, dt=F32):
            return ctx.enter_context(nc.sbuf_tensor(f"e{T}_{name}", shape, dt))

        def signal(name, per=1, unit=1):
            return Signal(nc, held, f"e{T}_{name}", per, unit)

        ident = sb("ident", [128, 128])
        w1 = sb("w1", [F, 2, 2, HID])
        w2 = sb("w2", [128, 2, KC, D])
        b1 = sb("b1", [128, 2, KC])
        b2 = sb("b2", [ROWS, 2, D])
        x_rows = sb("x_rows", [ROWS, 2, 4, D])
        x = sb("x", [F, 2, 2, COLS])
        hidden = sb("hidden", [128, KC, COLS])
        y = sb("y", [ROWS, 2, 4, D])
        ps_x = ctx.enter_context(nc.psum_tensor(f"e{T}_ps_x", [128, 2, BANK], F32))
        ps_h = ctx.enter_context(nc.psum_tensor(f"e{T}_ps_h", [128, 2, BANK], F32))
        ps_o = ctx.enter_context(nc.psum_tensor(f"e{T}_ps_o", [128, 4, BANK], F32))

        ident_landed = held.take(nc, f"e{T}_ident_landed")
        x_landed = [signal(f"x_landed_{p}", 1, 16) for p in (0, 1)]
        w_landed = [signal(f"w_landed_{p}", 4, 16) for p in (0, 1)]
        stored = [signal(f"stored_{p}", 1, 16) for p in (0, 1)]
        turned = signal("turned")
        x_done = signal("x_done")
        hid_proj = signal("hid_proj", KC)
        hid_done = signal("hid_done", KC)
        out_proj = signal("out_proj", 4)
        y_done = signal("y_done", 4)

        block = ctx.enter_context(nc.Block())

        def each_block(eng, body):
            with eng.Fori(0, NB // 2) as bb:
                for par in (0, 1):
                    body(bb, 2 * bb + par, par)
            if NB % 2:
                body(NB // 2, NB - 1, 0)

        @block.sync
        def _(sp):
            sp.dma_start(ident[:, :], dram["ident"]).then_inc(ident_landed, 16)
            prime(sp, *x_landed, *w_landed)

            def fetch(bb, b, par):
                sp.wait_ge(turned.sem, turned.before(b - 1) if not isinstance(b, int) or b >= 2 else turned.before(0))
                sp.dma_start(x_rows[:, par, :, :], dram["moe_in" + T][bass.ds(b * COLS, COLS), :].rearrange(
                    "(j p) d -> p j d", p=ROWS)).then_inc(x_landed[par].sem, 16)
                sp.wait_ge(y_done.sem, y_done.before(b - 1) if not isinstance(b, int) or b >= 2 else y_done.before(0))
                e = sp.value_load(expert_of[0:1, bass.ds(b, 1)], min_val=0, max_val=E - 1)
                for dst, src in ((w1[:, par, :, :].rearrange("p a b -> p (a b)"), dram["w1_" + T][bass.ds(e, 1), :, :]),
                                 (w2[:, par, :, :].rearrange("p a b -> p (a b)"), dram["w2_" + T][bass.ds(e, 1), :, :]),
                                 (b1[:, par, :], dram["b1_" + T][bass.ds(e, 1), :, :])):
                    sp.dma_start(dst, src.rearrange("a p n -> (a p) n")).then_inc(w_landed[par].sem, 16)
                sp.dma_start(b2[:, par, :], dram["b2_" + T][bass.ds(e, 1), :, :].rearrange(
                    "a p n -> (a p) n").to_broadcast([ROWS, D])).then_inc(w_landed[par].sem, 16)

            each_block(sp, fetch)

        @block.tensor
        def _(pe):
            prime(pe, turned, hid_proj, out_proj)
            pe.wait_ge(ident_landed, 16)

            def turn(bb, b, par):
                pe.wait_ge(x_landed[par].sem, x_landed[par].now(bb))
                pe.wait_ge(x_done.sem, x_done.before(b))
                for c in (0, 1):
                    for j in range(4):
                        mm = nc.tensor.transpose(ps_x[0:F, c, j * ROWS:(j + 1) * ROWS],
                                                 x_rows[:, par, j, c * F:(c + 1) * F], ident[0:ROWS, 0:ROWS])
                mm.then_inc(turned.sem, 1)

            def hidden_layer(bb, b, par):
                pe.wait_ge(w_landed[par].sem, w_landed[par].now(bb))
                pe.wait_ge(x_done.sem, x_done.now(b))
                for k in range(KC):
                    pe.wait_ge(hid_done.sem, hid_done.now(b, k - 1) if k >= 2 else hid_done.before(b, KC + k - 1))
                    for c in (0, 1):
                        mm = nc.tensor.matmul(ps_h[:, k % 2, 0:COLS], w1[:, par, c, k * 128:(k + 1) * 128],
                                              x[:, par, c, :], start=(c == 0), stop=(c == 1))
                    mm.then_inc(hid_proj.sem, 1)

            def output_layer(bb, b, par):
                pe.wait_ge(hid_done.sem, hid_done.now(b))
                for j in range(4):
                    pe.wait_ge(y_done.sem, y_done.before(b, j + 1))
                    for k in range(KC):
                        mm = nc.tensor.matmul(ps_o[0:ROWS, j, 0:D], hidden[:, k, j * ROWS:(j + 1) * ROWS],
                                              w2[:, par, k, :], start=(k == 0), stop=(k == KC - 1))
                    mm.then_inc(out_proj.sem, 1)

            turn(0, 0, 0)
            with pe.Fori(0, NB // 2) as bb:
                for par in (0, 1):
                    b = 2 * bb + par
                    hidden_layer(bb, b, par)
                    turn(bb + par, b + 1, 1 - par)
                    output_layer(bb, b, par)
            hidden_layer(NB // 2, NB - 1, 0)
            output_layer(NB // 2, NB - 1, 0)

        @block.scalar
        def _(act):
            prime(act, hid_done, *stored)

            def body(bb, b, par):
                act.wait_ge(w_landed[par].sem, w_landed[par].now(bb))
                act.wait_ge(out_proj.sem, out_proj.before(b))
                for k in range(KC):
                    act.wait_ge(hid_proj.sem, hid_proj.now(b, k + 1))
                    nc.scalar.activation(hidden[:, k, :], ps_h[:, k % 2, 0:COLS], ACT.Gelu,
                                         bias=b1[:, par, k:k + 1]).then_inc(hid_done.sem, 1)
                act.wait_ge(y_done.sem, y_done.now(b))
                act.dma_start(dram["moe_out" + T][bass.ds(b * COLS, COLS), :].rearrange("(j p) d -> p j d", p=ROWS),
                              y[:, par, :, :]).then_inc(stored[par].sem, 16)

            each_block(act, body)
            act.wait_ge(stored[0].sem, stored[0].now(NB // 2))
            act.wait_ge(stored[1].sem, stored[1].now(NB // 2 - 1))

        @block.vector
        def _(dve):
            prime(dve, x_done, y_done)

            def body(bb, b, par):
                dve.wait_ge(turned.sem, turned.now(b))
                nc.vector.tensor_copy(x[:, par, :, :], ps_x[0:F, :, 0:COLS]).then_inc(x_done.sem, 1)
                dve.wait_ge(w_landed[par].sem, w_landed[par].now(bb))
                dve.wait_ge(stored[par].sem, stored[par].before(bb))
                for j in range(4):
                    dve.wait_ge(out_proj.sem, out_proj.now(b, j + 1))
                    nc.vector.tensor_tensor(y[:, par, j, :], ps_o[0:ROWS, j, 0:D], b2[:, par, :],
                                            ALU.add).then_inc(y_done.sem, 1)

            each_block(dve, body)


def combine(nc, held, dram, slots_in, weights):
    with ExitStack() as ctx:
        def sb(name, shape, dt=F32):
            return ctx.enter_context(nc.sbuf_tensor(f"c_{name}", shape, dt))

        def by_parity(name, per=1, unit=1):
            return [Signal(nc, held, f"c_{name}_{p}", per, unit) for p in (0, 1)]

        h = sb("h", [ROWS, 2, 4, D])
        picked = sb("picked", [ROWS, 2, 2, 4, D])
        index = sb("index", [ROWS, 2, 2, 4], U32)
        share = sb("share", [ROWS, 2, 2, 4])
        h_landed = by_parity("h_landed", 1, 16)
        gathered = [Signal(nc, held, f"c_gathered_{p}", 8, 16, primed=False) for p in (0, 1)]
        index_done = by_parity("index_done", 2)
        added = by_parity("added", 8)
        stored = by_parity("stored", 1, 16)
        waited = held.take(nc, "c_waited")
        block = ctx.enter_context(nc.Block())

        def each_pair(eng, body):
            with eng.Fori(0, PAIRS // 2) as ii:
                for par in (0, 1):
                    body(ii, 2 * ii + par, par)

        @block.sync
        def _(sp):
            prime(sp, *h_landed)

            def body(ii, i, par):
                sp.wait_ge(stored[par].sem, stored[par].before(ii))
                sp.dma_start(h[:, par, :, :].rearrange("p a b -> p (a b)"), dram["h1"][i, :, :]).then_inc(h_landed[par].sem, 16)

            each_pair(sp, body)

        @block.gpsimd
        def _(pool):
            def body(ii, i, par):
                pool.wait_ge(index_done[par].sem, index_done[par].now(ii))
                pool.wait_ge(added[par].sem, added[par].before(ii))
                pool.sem_inc(waited, 1)
                for k in (0, 1):
                    for j in range(4):
                        pool.indirect_dma_start(
                            out=picked[:, par, k, j, :], out_offset=None, in_=dram["moe_out1"],
                            in_offset=bass.IndirectOffsetOnAxis(ap=index[:, par, k, j:j + 1], axis=0),
                        ).then_inc(gathered[par].sem, 16)

            each_pair(pool, body)

        @block.vector
        def _(dve):
            prime(dve, *index_done, *added)

            def indices(ii, i, par):
                dve.wait_ge(added[par].sem, added[par].before(ii))
                nc.vector.tensor_copy(index[:, par, :, :], slots_in[:, :, bass.ds(i * 4, 4)]).then_inc(index_done[par].sem, 1)
                nc.vector.tensor_copy(share[:, par, :, :], weights[:, :, bass.ds(i * 4, 4)]).then_inc(index_done[par].sem, 1)

            def add(ii, i, par):
                dve.wait_ge(h_landed[par].sem, h_landed[par].now(ii))
                dve.wait_ge(gathered[par].sem, gathered[par].now(ii))
                dve.wait_ge(index_done[par].sem, index_done[par].now(ii))
                for k in (0, 1):
                    for j in range(4):
                        if k == 1:
                            dve.wait_ge(added[par].sem, added[par].now(ii, j + 1))
                        nc.vector.scalar_tensor_tensor(out=h[:, par, j, :], in0=picked[:, par, k, j, :],
                                                       scalar=share[:, par, k, j:j + 1], in1=h[:, par, j, :],
                                                       op0=ALU.mult, op1=ALU.add).then_inc(added[par].sem, 1)

            indices(0, 0, 0)
            with dve.Fori(0, PAIRS // 2 - 1) as ii:
                indices(ii, 2 * ii + 1, 1)
                add(ii, 2 * ii, 0)
                indices(ii + 1, 2 * ii + 2, 0)
                add(ii, 2 * ii + 1, 1)
            indices(PAIRS // 2 - 1, PAIRS - 1, 1)
            add(PAIRS // 2 - 1, PAIRS - 2, 0)
            add(PAIRS // 2 - 1, PAIRS - 1, 1)

        @block.scalar
        def _(act):
            prime(act, *stored)
            out = dram["out"].rearrange("m t d -> (m t) d").rearrange("(i j p) d -> i p j d", j=4, p=ROWS)

            def body(ii, i, par):
                act.wait_ge(added[par].sem, added[par].now(ii))
                act.dma_start(out[bass.ds(i, 1), :, :, :].rearrange("a p j d -> p (a j) d"), h[:, par, :, :]).then_inc(stored[par].sem, 16)

            each_pair(act, body)
            for par in (0, 1):
                act.wait_ge(stored[par].sem, stored[par].now(PAIRS // 2 - 1))


def bass_vit_tower(nc, dram):
    with ExitStack() as ctx:
        def sb(name, shape, dt=F32):
            return ctx.enter_context(nc.sbuf_tensor(name, shape, dt))

        logits = sb("logits", [ROWS, TILES, 8])
        slots_in = sb("slots_in", [ROWS, 2, TILES], U32)
        slots_out = sb("slots_out", [ROWS, 2, TILES], U32)
        weights = sb("weights", [ROWS, 2, TILES])
        expert_of = sb("expert_of", [1, BLOCKS[1]], I32)
        for layer in (0, 1):
            for stage in ("mamba", "route", "moe"):
                held = Semaphores()
                if stage == "mamba":
                    mamba(nc, held, layer, dram, logits, slots_in[:, 0, :], PAIRS)
                elif stage == "route":
                    route(nc, held, layer, dram, logits, slots_in[:, 0:TOP[layer], :],
                          slots_out[:, 0:TOP[layer], :], weights, expert_of)
                else:
                    moe(nc, held, layer, dram, expert_of)
                held.hand_back(nc)
        combine(nc, Semaphores(), dram, slots_in, weights)


def layouts(inp):
    import numpy as _np
    a = {k: _np.asarray(v) for k, v in inp.items()}
    out = {}

    def put(name, x):
        out[name] = _np.ascontiguousarray(x)

    def chunks(v, p):
        v = v.reshape((-1, p) + v.shape[1:])
        return v.transpose((1, 0) + tuple(range(2, v.ndim)))

    x = a["x"].reshape(PAIRS, 2, 3, GRID, 16, GRID, 16).transpose(0, 2, 4, 6, 1, 3, 5)
    put("x", x.reshape(PAIRS, 6, 128, COLS - 4).transpose(0, 2, 1, 3).reshape(PAIRS, 128, -1))
    put("tok_w", chunks(a["L0_tok_W"].T, 128))
    for n, k in (("tok_b", "L0_tok_b"), ("tok_g", "L0_tok_gamma"), ("tok_beta", "L0_tok_beta"),
                 ("conv_b", "L0_attn_conv_b"), ("dt_b0", "L0_attn_dt_b"), ("skip0", "L0_attn_D_param"),
                 ("ln_g0", "L0_attn_ln_g"), ("ln_b0", "L0_attn_ln_b"), ("ln_g1", "L1_attn_gamma"),
                 ("ln_b1", "L1_attn_beta"), ("a_log0", "L0_attn_A_log")):
        put(n, chunks(a[k], F))
    put("class_token", chunks(a["L0_tok_class_token"].reshape(D), F))
    put("cls_tok", chunks(a["cls_tok"].reshape(D), F))
    put("conv_w", chunks(a["L0_attn_conv_w"].reshape(D, 4), F))
    put("in_w0", chunks(a["L0_attn_in_proj_w"].T, F))
    put("dt_w0", chunks(a["L0_attn_dt_w"].T, F))
    put("bc_w0", chunks(_np.concatenate([a["L0_attn_B_w"], a["L0_attn_C_w"]]).T, F))
    put("out_w0", chunks(a["L0_attn_out_w"].T, F))
    put("gate_w0", chunks(a["L0_ffn_Wg"], F))
    put("gate_b0", _np.broadcast_to(a["L0_ffn_bg"], (ROWS, 4)))
    put("in_w1", chunks(a["L1_attn_W_in"], F))
    put("x_w1", chunks(a["L1_attn_W_x"], 128))
    put("dt_w1", a["L1_attn_W_dt"])
    put("out_w1", chunks(a["L1_attn_W_out"], 128))
    put("gate_w1", chunks(a["L1_ffn_Wg"], F))
    for n, k in (("dt_b1", "L1_attn_b_dt"), ("skip1", "L1_attn_D_skip"), ("a_log1", "L1_attn_A_log")):
        put(n, chunks(a[k], 128))
    for t, e in (("0", 4), ("1", 8)):
        put("w1_" + t, a[f"L{t}_ffn_W1"].reshape(e, 2, F, HID).transpose(0, 2, 1, 3).reshape(e, F, -1))
        put("w2_" + t, a[f"L{t}_ffn_W2"].reshape(e, 6, 128, D).transpose(0, 2, 1, 3).reshape(e, 128, -1))
        put("b1_" + t, a[f"L{t}_ffn_b1"].reshape(e, 6, 128).transpose(0, 2, 1))
        put("b2_" + t, a[f"L{t}_ffn_b2"].reshape(e, 1, D))
    return out


def shape_constants():
    import numpy as _np
    from concourse import mybir as _mybir
    f32 = _np.float32
    out = {"ident": _np.eye(128, dtype=f32), "avg": _np.full((F, F), 1.0 / D, f32)}
    sel = _np.zeros((96, 32, 128), f32)
    sel[_np.arange(96), _np.arange(96) % 32, :] = 1.0
    out["select"] = sel.astype(_mybir.dt.np(BF16))
    i = _np.arange(SEQ - 1, dtype=f32)[:, None]
    j = _np.arange(D, dtype=f32)[None, :]
    angle = i / _np.power(f32(10000.0), (_np.floor(j / f32(2.0)) * f32(2.0) / f32(D)).astype(f32))
    pos = _np.where(_np.arange(D)[None, :] % 2 == 0, _np.sin(angle), _np.cos(angle)).astype(f32)
    out["pos"] = pos.T.reshape(2, F, SEQ - 1).transpose(1, 0, 2)
    out["earlier"] = _np.triu(_np.ones((ROWS, ROWS), f32), 1)
    out["ones"] = _np.ones((ROWS, ROWS), f32)
    out["steps"] = _np.broadcast_to(_np.arange(32, dtype=f32) * COLS, (ROWS, 32))
    out["numbers"] = _np.broadcast_to(_np.arange(BLOCKS[1], dtype=f32), (ROWS, BLOCKS[1]))
    out["token_of"] = _np.arange(TILES, dtype=f32)[None, :] * ROWS + _np.arange(ROWS, dtype=f32)[:, None]
    return {k: _np.ascontiguousarray(v) for k, v in out.items()}


def kernel(**inputs):
    import numpy as _np
    import concourse.bacc as _bacc
    from concourse import mybir as _mybir
    from concourse.bass_utils import run_bass_kernel_spmd as _run

    nc = _bacc.Bacc("TRN2", target_bir_lowering=False, num_devices=1)
    arrays, dram = {}, {}
    for name, v in (layouts(inputs) | shape_constants()).items():
        arrays["in_" + name] = v
        t = nc.dram_tensor("in_" + name, v.shape, _mybir.dt.from_np(v.dtype), kind="ExternalInput").ap()
        if name not in ("x", "w1_0", "w1_1", "w2_0", "w2_1", "b1_0", "b1_1", "b2_0", "b2_1") and len(v.shape) > 2:
            t = t.rearrange("p a b -> p (a b)")
        dram[name] = t
    scratch = {"h0": (PAIRS, F, 2 * COLS), "h1": (PAIRS, ROWS, 4 * D)}
    for t in (0, 1):
        scratch[f"xf{t}"] = (PAIRS, ROWS, 4 * D)
        scratch[f"moe_in{t}"] = (BLOCKS[t] * COLS + TOP[t] * TOKENS, D)
        scratch[f"moe_out{t}"] = (BLOCKS[t] * COLS + 1, D)
    for name, shape in scratch.items():
        dram[name] = nc.dram_tensor(name, shape, F32, kind="Internal").ap()
    dram["out"] = nc.dram_tensor("out_0", (IMAGES, SEQ, D), F32, kind="ExternalOutput").ap()
    bass_vit_tower(nc, dram)
    r = _run(nc, [arrays], core_ids=[0])
    return r.results[0]["out_0"]
```
